# Optimizing a Trainium2 kernel written in Bass

```python
import numpy as np
import jax
import jax.numpy as jnp

def _softmax(x, axis=-1):
    return jax.nn.softmax(x, axis=axis)

def _gelu(x):
    return jax.nn.gelu(x, approximate=True)

def _silu(x):
    return jax.nn.silu(x)

def _sigmoid(x):
    return jax.nn.sigmoid(x)

def _layernorm(x, axis=-1, eps=1e-05):
    m = jnp.mean(x, axis=axis, keepdims=True)
    v = jnp.var(x, axis=axis, keepdims=True)
    return (x - m) / jnp.sqrt(v + eps)

def _scatter_add(tgt, idx, src, axis=0):
    return tgt.at[idx].add(src)

def _segment_sum(src, seg, n):
    return jax.ops.segment_sum(src, seg, n)
kernel_name = 'mk_lm_tower_d1_tok_ids768_r4_e81b64'

def setup_inputs(seed: int=0):
    np.random.seed(seed)
    _w = jnp.asarray

    def _rec_inputs():
        import jax
        import jax.numpy as jnp
        _rk = jax.random.key(seed)
        x = jax.random.randint(jax.random.fold_in(_rk, 1), (1, 2048), 0, 31921, jnp.int32)
        return x
    x = _rec_inputs()

    def _L0_tok_setup():
        import jax, jax.numpy as jnp
        import numpy as np
        B, L, V, D_MODEL = (1, 512, 8000, 192)
        N_LAYER, D_STATE, EXPAND, D_CONV = (2, 16, 2, 4)
        D_INNER = EXPAND * D_MODEL
        DT_RANK = -(-D_MODEL // D_STATE)
        EPS = 1e-05

        def _rmsnorm(x, w):
            return x * jax.lax.rsqrt(jnp.mean(x * x, axis=-1, keepdims=True) + EPS) * w

        def _selective_scan(u, delta, A, Bm, Cm, D):
            deltaA = jnp.exp(delta[..., None] * A)
            dBu = delta[..., None] * Bm[:, :, None, :] * u[..., None]

            def comb(c1, c2):
                a1, b1 = c1
                a2, b2 = c2
                return (a2 * a1, a2 * b1 + b2)
            _, h = jax.lax.associative_scan(comb, (deltaA, dBu), axis=1)
            y = jnp.einsum('bldn,bln->bld', h, Cm)
            return y + u * D

        def _mamba_block(x, in_proj_w, conv_w, conv_b, x_proj_w, dt_proj_w, dt_proj_b, A_log, D, out_proj_w):
            xz = x @ in_proj_w
            xr, res = jnp.split(xz, 2, axis=-1)
            xc = jax.lax.conv_general_dilated(jnp.swapaxes(xr, 1, 2), conv_w, (1,), [(D_CONV - 1, 0)], feature_group_count=D_INNER, dimension_numbers=('NCH', 'OIH', 'NCH'))
            xr = jax.nn.silu(jnp.swapaxes(xc + conv_b[:, None], 1, 2))
            A = -jnp.exp(A_log)
            x_dbl = xr @ x_proj_w
            dt, Bm, Cm = jnp.split(x_dbl, [DT_RANK, DT_RANK + D_STATE], axis=-1)
            delta = jax.nn.softplus(dt @ dt_proj_w + dt_proj_b)
            y = _selective_scan(xr, delta, A, Bm, Cm, D)
            return y * jax.nn.silu(res) @ out_proj_w
        key = jax.random.key(seed)
        ks = jax.random.split(key, 12)
        s = 0.02
        inp = {'input_ids': jax.random.randint(ks[0], (B, L), 0, V), 'emb': jax.random.normal(ks[1], (V, D_MODEL), jnp.float32) * s, 'norm_w': jnp.ones((N_LAYER, D_MODEL), jnp.float32), 'in_proj_w': jax.random.normal(ks[2], (N_LAYER, D_MODEL, 2 * D_INNER), jnp.float32) * s, 'conv_w': jax.random.normal(ks[3], (N_LAYER, D_INNER, 1, D_CONV), jnp.float32) * s, 'conv_b': jnp.zeros((N_LAYER, D_INNER), jnp.float32), 'x_proj_w': jax.random.normal(ks[4], (N_LAYER, D_INNER, DT_RANK + 2 * D_STATE), jnp.float32) * s, 'dt_proj_w': jax.random.normal(ks[5], (N_LAYER, DT_RANK, D_INNER), jnp.float32) * s, 'dt_proj_b': jax.random.normal(ks[6], (N_LAYER, D_INNER), jnp.float32) * s, 'A_log': jnp.tile(jnp.log(jnp.arange(1, D_STATE + 1, dtype=jnp.float32)), (N_LAYER, D_INNER, 1)), 'D': jnp.ones((N_LAYER, D_INNER), jnp.float32), 'out_proj_w': jax.random.normal(ks[7], (N_LAYER, D_INNER, D_MODEL), jnp.float32) * s}
        return inp
    _L0_tok_all = _L0_tok_setup()
    _L0_tok_in = {k: v for k, v in _L0_tok_all.items() if k in ('emb', 'norm_w', 'in_proj_w', 'conv_w', 'conv_b', 'x_proj_w', 'dt_proj_w', 'dt_proj_b', 'A_log', 'D', 'out_proj_w')}
    del _L0_tok_all

    def _L0_attn_setup():
        import jax, jax.numpy as jnp
        import numpy as np
        B_, L_, DM, DS, DC, EXP = (2, 1024, 192, 64, 4, 2)
        DI = DM * EXP
        key = jax.random.key(seed)
        ks = jax.random.split(key, 8)
        s = lambda k, shape, scale: jax.random.normal(k, shape, jnp.float32) * scale
        return {'x': jax.random.normal(ks[0], (B_, L_, DM), jnp.float32), 'in_w': s(ks[1], (DM, 2 * DI), DM ** (-0.5)), 'conv_w': s(ks[2], (DI, 1, DC), DC ** (-0.5)), 'conv_b': jnp.zeros((DI,), jnp.float32), 'xproj_w': s(ks[3], (DI, 2 * DS + 1), DI ** (-0.5)), 'A_log': jnp.tile(jnp.log(jnp.arange(1, DS + 1, dtype=jnp.float32))[None, :], (DI, 1)), 'dt_bias': jax.random.uniform(ks[4], (DI,), jnp.float32, float(np.log(0.001)), float(np.log(0.1))), 'D': jnp.ones((DI,), jnp.float32), 'out_w': s(ks[5], (DI, DM), DI ** (-0.5))}
    _L0_attn_all = _L0_attn_setup()
    _L0_attn_in = {k: v for k, v in _L0_attn_all.items() if k in ('in_w', 'conv_w', 'conv_b', 'xproj_w', 'A_log', 'dt_bias', 'D', 'out_w')}
    del _L0_attn_all

    def _L0_ffn_setup():
        import jax, jax.numpy as jnp
        import numpy as np
        DIM = 192
        NUM_EXPERTS = 4
        NUM_HEADS = 12
        HEAD_DIM = DIM // NUM_HEADS
        MLP_HID = 4 * DIM
        FC1_OUT = MLP_HID + 3 * DIM
        FC2_IN = MLP_HID + DIM
        FC2_OUT = 2 * DIM
        CAP_FACTOR = 0.5
        LN_EPS = 1e-06
        key = jax.random.key(seed)
        ks = jax.random.split(key, 4)
        B, N = (8, 256)
        return {'x': jax.random.normal(ks[0], (B, N, DIM), jnp.float32), 'w_router': jax.random.normal(ks[1], (NUM_EXPERTS, DIM), jnp.float32) * 0.02, 'gamma1': jnp.ones((DIM,), jnp.float32), 'beta1': jnp.zeros((DIM,), jnp.float32), 'w1': jax.random.normal(ks[2], (FC1_OUT, DIM), jnp.float32) * 0.02, 'b1': jnp.zeros((FC1_OUT,), jnp.float32), 'w2': jax.random.normal(ks[3], (FC2_OUT, FC2_IN), jnp.float32) * 0.02, 'b2': jnp.zeros((FC2_OUT,), jnp.float32)}
    _L0_ffn_all = _L0_ffn_setup()
    _L0_ffn_in = {k: v for k, v in _L0_ffn_all.items() if k in ('w_router', 'gamma1', 'beta1', 'w1', 'b1', 'w2', 'b2')}
    del _L0_ffn_all
    return {'x': x, 'L0_tok_emb': _L0_tok_in['emb'], 'L0_tok_norm_w': _L0_tok_in['norm_w'], 'L0_tok_in_proj_w': _L0_tok_in['in_proj_w'], 'L0_tok_conv_w': _L0_tok_in['conv_w'], 'L0_tok_conv_b': _L0_tok_in['conv_b'], 'L0_tok_x_proj_w': _L0_tok_in['x_proj_w'], 'L0_tok_dt_proj_w': _L0_tok_in['dt_proj_w'], 'L0_tok_dt_proj_b': _L0_tok_in['dt_proj_b'], 'L0_tok_A_log': _L0_tok_in['A_log'], 'L0_tok_D': _L0_tok_in['D'], 'L0_tok_out_proj_w': _L0_tok_in['out_proj_w'], 'L0_attn_in_w': _L0_attn_in['in_w'], 'L0_attn_conv_w': _L0_attn_in['conv_w'], 'L0_attn_conv_b': _L0_attn_in['conv_b'], 'L0_attn_xproj_w': _L0_attn_in['xproj_w'], 'L0_attn_A_log': _L0_attn_in['A_log'], 'L0_attn_dt_bias': _L0_attn_in['dt_bias'], 'L0_attn_D': _L0_attn_in['D'], 'L0_attn_out_w': _L0_attn_in['out_w'], 'L0_ffn_w_router': _L0_ffn_in['w_router'], 'L0_ffn_gamma1': _L0_ffn_in['gamma1'], 'L0_ffn_beta1': _L0_ffn_in['beta1'], 'L0_ffn_w1': _L0_ffn_in['w1'], 'L0_ffn_b1': _L0_ffn_in['b1'], 'L0_ffn_w2': _L0_ffn_in['w2'], 'L0_ffn_b2': _L0_ffn_in['b2']}

def reference(x, L0_tok_emb, L0_tok_norm_w, L0_tok_in_proj_w, L0_tok_conv_w, L0_tok_conv_b, L0_tok_x_proj_w, L0_tok_dt_proj_w, L0_tok_dt_proj_b, L0_tok_A_log, L0_tok_D, L0_tok_out_proj_w, L0_attn_in_w, L0_attn_conv_w, L0_attn_conv_b, L0_attn_xproj_w, L0_attn_A_log, L0_attn_dt_bias, L0_attn_D, L0_attn_out_w, L0_ffn_w_router, L0_ffn_gamma1, L0_ffn_beta1, L0_ffn_w1, L0_ffn_b1, L0_ffn_w2, L0_ffn_b2):
    import jax
    import jax.numpy as jnp

    def _L0_tok_ref(input_ids, emb, norm_w, in_proj_w, conv_w, conv_b, x_proj_w, dt_proj_w, dt_proj_b, A_log, D, out_proj_w):
        import jax, jax.numpy as jnp
        import numpy as np
        B, L, V, D_MODEL = (1, 512, 8000, 192)
        N_LAYER, D_STATE, EXPAND, D_CONV = (2, 16, 2, 4)
        D_INNER = EXPAND * D_MODEL
        DT_RANK = -(-D_MODEL // D_STATE)
        EPS = 1e-05

        def _rmsnorm(x, w):
            return x * jax.lax.rsqrt(jnp.mean(x * x, axis=-1, keepdims=True) + EPS) * w

        def _selective_scan(u, delta, A, Bm, Cm, D):
            deltaA = jnp.exp(delta[..., None] * A)
            dBu = delta[..., None] * Bm[:, :, None, :] * u[..., None]

            def comb(c1, c2):
                a1, b1 = c1
                a2, b2 = c2
                return (a2 * a1, a2 * b1 + b2)
            _, h = jax.lax.associative_scan(comb, (deltaA, dBu), axis=1)
            y = jnp.einsum('bldn,bln->bld', h, Cm)
            return y + u * D

        def _mamba_block(x, in_proj_w, conv_w, conv_b, x_proj_w, dt_proj_w, dt_proj_b, A_log, D, out_proj_w):
            xz = x @ in_proj_w
            xr, res = jnp.split(xz, 2, axis=-1)
            xc = jax.lax.conv_general_dilated(jnp.swapaxes(xr, 1, 2), conv_w, (1,), [(D_CONV - 1, 0)], feature_group_count=D_INNER, dimension_numbers=('NCH', 'OIH', 'NCH'))
            xr = jax.nn.silu(jnp.swapaxes(xc + conv_b[:, None], 1, 2))
            A = -jnp.exp(A_log)
            x_dbl = xr @ x_proj_w
            dt, Bm, Cm = jnp.split(x_dbl, [DT_RANK, DT_RANK + D_STATE], axis=-1)
            delta = jax.nn.softplus(dt @ dt_proj_w + dt_proj_b)
            y = _selective_scan(xr, delta, A, Bm, Cm, D)
            return y * jax.nn.silu(res) @ out_proj_w
        x = emb[input_ids]
        for i in range(N_LAYER):
            x = x + _mamba_block(_rmsnorm(x, norm_w[i]), in_proj_w[i], conv_w[i], conv_b[i], x_proj_w[i], dt_proj_w[i], dt_proj_b[i], A_log[i], D[i], out_proj_w[i])
        return x

    def _L0_attn_ref(x, in_w, conv_w, conv_b, xproj_w, A_log, dt_bias, D, out_w):
        import jax, jax.numpy as jnp
        import numpy as np
        B_, L_, DM, DS, DC, EXP = (2, 1024, 192, 64, 4, 2)
        DI = DM * EXP
        batch, seq_len, _ = x.shape
        d_inner = conv_b.shape[0]
        d_state = A_log.shape[1]
        xz = x @ in_w
        x_ssm, z = (xz[..., :d_inner], xz[..., d_inner:])
        xc = jax.lax.conv_general_dilated(x_ssm.transpose(0, 2, 1), conv_w, (1,), [(conv_w.shape[-1] - 1, 0)], feature_group_count=d_inner, dimension_numbers=('NCH', 'OIH', 'NCH'))
        xc = (xc + conv_b[None, :, None]).transpose(0, 2, 1)
        xc = jax.nn.silu(xc)
        p = xc @ xproj_w
        Bm = p[..., :d_state]
        Cm = p[..., d_state:2 * d_state]
        dt = jax.nn.softplus(p[..., -1:] + dt_bias)
        A = -jnp.exp(A_log)

        def step(h, ins):
            xt, Bt, Ct, dtt = ins
            A_bar = jnp.exp(A * dtt[..., None])
            h = A_bar * h + dtt[..., None] * Bt[:, None, :] * xt[..., None]
            y = jnp.einsum('bn,bdn->bd', Ct, h)
            return (h, y)
        h0 = jnp.zeros((batch, d_inner, d_state), x.dtype)
        ins = (xc.transpose(1, 0, 2), Bm.transpose(1, 0, 2), Cm.transpose(1, 0, 2), dt.transpose(1, 0, 2))
        _, ys = jax.lax.scan(step, h0, ins)
        y = ys.transpose(1, 0, 2)
        y = y + D * xc
        y = y * jax.nn.silu(z)
        return y @ out_w

    def _L0_ffn_ref(x, w_router, gamma1, beta1, w1, b1, w2, b2):
        import jax, jax.numpy as jnp
        import numpy as np
        DIM = 192
        NUM_EXPERTS = 4
        NUM_HEADS = 12
        HEAD_DIM = DIM // NUM_HEADS
        MLP_HID = 4 * DIM
        FC1_OUT = MLP_HID + 3 * DIM
        FC2_IN = MLP_HID + DIM
        FC2_OUT = 2 * DIM
        CAP_FACTOR = 0.5
        LN_EPS = 1e-06
        B, N, C = x.shape
        E = NUM_EXPERTS
        cap = int(CAP_FACTOR * N)
        m = np.array([C // 2 ** (E - 1 - e) for e in range(E)])
        in_mask = (np.arange(C)[None, :] < m[:, None]).astype(np.float32)
        in_mask = jnp.asarray(in_mask)
        out_mask = jnp.concatenate([in_mask, in_mask], axis=-1)
        logits = jnp.einsum('bnc,ec->bne', x, w_router)
        probs = jax.nn.softmax(logits, axis=-1)
        gate, idx = jax.lax.top_k(jnp.swapaxes(probs, 1, 2), cap)
        dispatch = jax.nn.one_hot(idx, N, dtype=x.dtype)
        combine = dispatch * gate[..., None]
        mu = jnp.mean(x, -1, keepdims=True)
        var = jnp.var(x, -1, keepdims=True)
        y = (x - mu) * jax.lax.rsqrt(var + LN_EPS) * gamma1 + beta1
        xg = jnp.einsum('becn,bnd->becd', dispatch, y)
        xg = xg * in_mask[None, :, None, :]
        h = jnp.einsum('becd,fd->becf', xg, w1) + b1
        h = jnp.einsum('becn,becf->bnf', dispatch, h)
        x_mlp, x_qkv = (h[..., :MLP_HID], h[..., MLP_HID:])
        qkv = x_qkv.reshape(B, N, 3, NUM_HEADS, HEAD_DIM).transpose(2, 0, 3, 1, 4)
        q, k, v = (qkv[0], qkv[1], qkv[2])
        scale = HEAD_DIM ** (-0.5)
        attn = jax.nn.softmax(jnp.einsum('bhqd,bhkd->bhqk', q, k) * scale, axis=-1)
        x_attn = jnp.einsum('bhqk,bhkd->bhqd', attn, v)
        x_attn = x_attn.transpose(0, 2, 1, 3).reshape(B, N, C)
        x_mlp = jax.nn.gelu(x_mlp, approximate=False)
        y2 = jnp.concatenate([x_mlp, x_attn], axis=-1)
        yg = jnp.einsum('becn,bnf->becf', dispatch, y2)
        o = jnp.einsum('becf,of->beco', yg, w2) + b2
        o = o * out_mask[None, :, None, :]
        z = jnp.einsum('becn,beco->bno', combine, o)
        x_mlp2, x_attn2 = (z[..., :C], z[..., C:])
        return x + x_mlp2 + x_attn2
    h = _L0_tok_ref(x, L0_tok_emb, L0_tok_norm_w, L0_tok_in_proj_w, L0_tok_conv_w, L0_tok_conv_b, L0_tok_x_proj_w, L0_tok_dt_proj_w, L0_tok_dt_proj_b, L0_tok_A_log, L0_tok_D, L0_tok_out_proj_w)
    h = h + _L0_attn_ref(_layernorm(h, axis=-1), L0_attn_in_w, L0_attn_conv_w, L0_attn_conv_b, L0_attn_xproj_w, L0_attn_A_log, L0_attn_dt_bias, L0_attn_D, L0_attn_out_w)
    h = h + _L0_ffn_ref(_layernorm(h, axis=-1), L0_ffn_w_router, L0_ffn_gamma1, L0_ffn_beta1, L0_ffn_w1, L0_ffn_b1, L0_ffn_w2, L0_ffn_b2)
    return h

_drawn_inputs = setup_inputs


def setup_inputs(seed=0):
    import zlib

    import numpy as np

    out = dict(_drawn_inputs(seed))
    spreads = {'L0_tok_norm_w': (1.0, 0.2),
     'L0_tok_conv_b': (0.0, 0.1),
     'L0_tok_D': (1.0, 0.2),
     'L0_attn_conv_b': (0.0, 0.1),
     'L0_attn_D': (1.0, 0.2),
     'L0_ffn_gamma1': (1.0, 0.6),
     'L0_ffn_beta1': (0.0, 0.8),
     'L0_ffn_b1': (0.0, 0.1),
     'L0_ffn_b2': (0.0, 0.1)}
    factors = {'L0_tok_x_proj_w': 8.0,
     'L0_tok_dt_proj_w': 200.0,
     'L0_tok_dt_proj_b': 200.0,
     'L0_tok_A_log': 200.0}
    for name, (base, spread) in spreads.items():
        noise = np.random.default_rng([zlib.crc32(name.encode()), seed]).standard_normal(out[name].shape)
        drawn = base * np.exp(spread * noise) if base else spread * noise
        out[name] = jnp.asarray(drawn.astype(out[name].dtype))
    for name, factor in factors.items():
        out[name] = (out[name] * factor).astype(out[name].dtype)
    return out
```

```python
from contextlib import ExitStack

import numpy as np
import concourse.bass as bass
from concourse import mybir

F32 = mybir.dt.float32
BF16 = mybir.dt.bfloat16
I32 = mybir.dt.int32
ALU = mybir.AluOpType
ACT = mybir.ActivationFunctionType
AX_X = mybir.AxisListType.X

P = 128
L = 2048
C = 192
V = 8000
CH = C // 2
DI = 2 * C
NJ = DI // P
CK = 512
NC = L // CK
TAPS = 4
TOK_N, TOK_R = 16, 12
ATT_N = 64
BLOCK_N = (TOK_N, TOK_N, ATT_N)
BLOCK_R = (TOK_R, TOK_R, 1)
STEP0 = (0, NC * TOK_N, 2 * NC * TOK_N, 2 * NC * TOK_N + NC * ATT_N)
NB = 3
A_LOG_MAX = 85.0
A_SLOTS, H_SLOTS = 2, 4
LAG = 2

E = 4
WIDTH = [C // 2 ** (E - 1 - e) for e in range(E)]
CAP = L // 2
HEADS, HD = 12, 16
HID = 4 * C
F1 = HID + 3 * C
F2 = HID + C
HG = 4
NG = HEADS // HG
KT = L // P
PARTS = 3
PAIRS = ((0, 0), (0, 1), (1, 0), (1, 1), (0, 2), (2, 0))
KR = len(PAIRS) * HD
SEARCH_BITS, SEARCH_ROUNDS = 5, 6
MAX_RING = 3


def part_stack(t, part, group, lo, hi):
    return t[32 * part:32 * part + 32, group, lo:hi]


def build(nc, x, emb, norm_w, w_in, conv_w, conv_b, x_proj, dt_w, dt_b, a_log, d_skip, w_out, ffn, consts, out):
    with ExitStack() as ctx:
        def sb(name, shape, dt=F32):
            return ctx.enter_context(nc.sbuf_tensor(name, shape, dt))

        def sem(name):
            return ctx.enter_context(nc.semaphore(name))

        bank = ctx.enter_context(nc.psum_tensor("bank", [P, 8, CK], F32))
        resid = sb("resid", [CH, 2, L])
        region = sb("region", [P, 3 * (NJ * L) + NJ * (L + TAPS - 1)])
        scratch = sb("scratch", [P, (A_SLOTS + H_SLOTS) * NJ * CK])
        stack_all = sb("stack", [P, 4, L], BF16)
        stack = stack_all[0:3 * 32]
        c_row = sb("c_row", [P, 2, CK])
        weights = sb("weights", [P, 32 * P // 2 + 2 * 2 * DI])
        sel = weights[0:3 * 32, 0:32 * P // 2].bitcast(BF16).rearrange("p (m k) -> p m k", k=P)
        w_in_sb = weights[0:CH, 32 * P // 2:].rearrange("p (i n) -> p i n", i=2)
        w_out_sb = sb("w_out_sb", [P, NB, NJ, C])
        w_x_sb = [sb(f"w_x{k}", [P, NJ, BLOCK_R[k] + 2 * BLOCK_N[k]]) for k in range(NB)]
        w_dt_sb = sb("w_dt_sb", [TOK_R, 2, DI])
        norm_sb = sb("norm_sb", [CH, 2, 2])
        conv_w_sb = sb("conv_w_sb", [P, NB, NJ, TAPS])
        vec_sb = sb("vec_sb", [P, 3, NB, NJ])
        a_sb = [sb(f"a{k}", [P, NJ, BLOCK_N[k]]) for k in range(NB)]
        diag = sb("diag", [P, NJ, P])
        state = sb("state", [P, ATT_N, NJ])
        ident = sb("ident", [P, P])
        w1t = weights[0:CH + 1, 0:2 * F1].rearrange("p (i f) -> p i f", i=2)
        w2t = w_out_sb[:].rearrange("p k j c -> p (k j) c")
        w_router_sb = sb("w_router_sb", [CH, 2, E])
        ffn_rows = sb("ffn_rows", [8, CH])
        ffn_vec = sb("ffn_vec", [CH, 4, 2])
        width_mask = sb("width_mask", [P, C + 1])
        group_ones = sb("group_ones", [P, P])
        sum_pick = sb("sum_pick", [P, P])
        search_off = sb("search_off", [P, SEARCH_ROUNDS], I32)
        probs = sb("probs", [P, KT, E])
        psum_e = sb("psum_e", [P, KT])
        search = sb("search", [P, 8])
        search_i = sb("search_i", [P, 4], I32)
        max_part = sb("max_part", [P, HG * 4, 4])
        max_q = sb("max_q", [P, HG * 4])
        max_left = sb("max_left", [HG * 4, P])
        max_row = sb("max_row", [HG * 4, 3, P], BF16)
        fold = sb("fold", [P, 32])
        ones = sb("ones", [P, P])
        idx_rows = sb("idx_rows", [L // P, P], I32)
        idx_f = sb("idx_f", [L // P, 2, P])
        idx = sb("idx", [P, L // P], I32)
        vec_rows = sb("vec_rows", [3 * NB * NJ, P])
        norm_rows = sb("norm_rows", [4, CH])

        RW = NJ * L
        xr = region[:, 0:NJ * (L + TAPS - 1)].rearrange("p (j t) -> p j t", j=NJ)
        dtu = xr[:, :, TAPS - 1:]
        r0 = NJ * (L + TAPS - 1)
        u = region[:, r0:r0 + RW].rearrange("p (j t) -> p j t", j=NJ)
        gate = region[:, r0 + RW:r0 + 2 * RW].rearrange("p (j t) -> p j t", j=NJ)
        delta = region[:, r0 + 2 * RW:r0 + 3 * RW].rearrange("p (j t) -> p j t", j=NJ)
        xn = region[0:CH, r0 + 2 * RW:r0 + 2 * RW + 2 * L].rearrange("p (i t) -> p i t", i=2)
        a_slot = scratch[:, 0:A_SLOTS * NJ * CK].rearrange("p (s j t) -> p s j t", s=A_SLOTS, j=NJ)
        h_slot = scratch[:, A_SLOTS * NJ * CK:].rearrange("p (s j t) -> p s j t", s=H_SLOTS, j=NJ)
        square = scratch[0:CH, 0:2 * L].rearrange("p (i t) -> p i t", i=2)
        rstd = scratch[0:CH, 2 * L:3 * L]
        soft = scratch[:, 0:NJ * L].rearrange("p (j t) -> p j t", j=NJ)
        parts = scratch[:, NJ * L:NJ * L + 3 * L // 2].bitcast(BF16).rearrange("p (s t) -> p s t", s=3)
        dt_low = dtu[0:TOK_R, 0, :]
        left = scratch[:, 0:L]
        tok_rows = scratch[:, 0:L // P * C].rearrange("p (b c) -> p b c", b=L // P)

        xf = xn
        yw = region[0:CH + 1, 0:2 * L].rearrange("p (i t) -> p i t", i=2)
        selgate = region[:, 2 * L:3 * L]
        v_sb = region[:, 3 * L:6 * L].rearrange("p (b h d) -> p b h d", b=KT, h=HEADS)
        mlp = region[:, 3 * L:9 * L].rearrange("p (f t) -> p f t", f=HID // P)
        w1_raw = region[0:CH, 3 * L:3 * L + 14 * C].rearrange("p (b c) -> p b c", c=C)
        o = 3 * L + 14 * C
        w2_raw = region[0:CH, o:o + 4 * F2].rearrange("p (b f) -> p b f", b=4)
        o += 4 * F2
        w2_pad = region[0:CH, o:o + 2 * NG * P].rearrange("p (i g j d) -> p i g j d", i=2, g=NG, j=HG)
        xa = region[:, r0 + 2 * RW:r0 + 3 * RW].rearrange("p (g t) -> p g t", g=NG)
        k_stack = [region[:, 6 * L:8 * L].bitcast(BF16).rearrange("p (h t) -> p h t", h=HG),
                   scratch[:, 2 * L:4 * L].bitcast(BF16).rearrange("p (h t) -> p h t", h=HG)]
        q_stack = stack_all[:].rearrange("p a t -> p (a t)")

        def q_cols(c, head, n, at=0):
            return bass.ds(c * (HG * CK) + (head * CK + at), n)
        p_slot = scratch[:, 0:2 * L].rearrange("p (s h t) -> p s h t", s=4, h=2)
        prob_bc = scratch[:, 0:L]
        prob_wide = scratch[:, 3 * L:4 * L].rearrange("p (b e m) -> p b e m", b=KT, e=E)
        chosen = scratch[:, L:2 * L]
        flag = scratch[:, 2 * L:3 * L]
        prefix = scratch[:, 3 * L:4 * L]
        qk_part = scratch[0:CH, 0:3 * L].bitcast(BF16).rearrange("p (s a t) -> p s a t", s=2, a=PARTS)
        qk_left = scratch[0:CH, 3 * L:4 * L]
        inv_sb = scratch[:, 0:L]
        P0 = 2
        O0 = 1
        b2_sum = ffn_vec[:, 2, :]
        PV0 = 2
        o_sb = scratch[0:CH, 0:4 * L].rearrange("p (i t) -> p i t", i=4)[:, 0:2]
        qk_dram = nc.dram_tensor("qk_parts", (2, HEADS, KR, L), BF16, kind="Internal").ap()

        s_const = sem("s_const")
        s_small = sem("s_small")
        s_vec = sem("s_vec")
        s_turned = sem("s_turned")
        s_vec_ok = sem("s_vec_ok")
        s_win = sem("s_win")
        s_idx = sem("s_idx")
        s_idx_ok = sem("s_idx_ok")
        s_rows = [sem(f"s_rows{c}") for c in range(NC)]
        s_rows_t = sem("s_rows_t")
        s_resid = sem("s_resid")
        s_sel = sem("s_sel")
        s_sum = sem("s_sum")
        s_centered = sem("s_centered")
        s_square = sem("s_square")
        s_var = sem("s_var")
        s_inv = sem("s_inv")
        s_rstd = sem("s_rstd")
        s_norm = sem("s_norm")
        s_inproj = sem("s_inproj")
        s_inproj_out = sem("s_inproj_out")
        s_conv = sem("s_conv")
        s_u = sem("s_u")
        s_bc_rows = sem("s_bc_rows")
        s_split = sem("s_split")
        s_stack = sem("s_stack")
        s_dt_in = sem("s_dt_in")
        s_dt_sb = sem("s_dt_sb")
        s_dt_proj = sem("s_dt_proj")
        s_dt_x = sem("s_dt_x")
        s_u_ln = sem("s_u_ln")
        s_dtu = sem("s_dtu")
        s_a_log = sem("s_a_log")
        s_a_mat = sem("s_a_mat")
        s_a_ready = sem("s_a_ready")
        s_diag = sem("s_diag")
        s_b_bc = sem("s_b_bc")
        s_c_bc = sem("s_c_bc")
        s_b_used = sem("s_b_used")
        s_c_row = sem("s_c_row")
        s_a = sem("s_a")
        s_scan = sem("s_scan")
        s_carry = sem("s_carry")
        s_hc = sem("s_hc")
        s_ysum = sem("s_ysum")
        s_y = sem("s_y")
        s_outproj = sem("s_outproj")
        s_v = sem("s_v")
        s_act = sem("s_act")
        s_fin_t = sem("s_fin_t")
        s_fin = sem("s_fin")
        s_out = sem("s_out")
        s_pool = sem("s_pool")
        f_w_raw = sem("f_w_raw")
        f_ffn_c = sem("f_ffn_c")
        f_ffn_v = sem("f_ffn_v")
        f_w2_sum = sem("f_w2_sum")
        f_w_turn = sem("f_w_turn")
        f_w_turned = sem("f_w_turned")
        f_logit = sem("f_logit")
        f_probs = sem("f_probs")
        f_prob_t = sem("f_prob_t")
        f_prob_bc = sem("f_prob_bc")
        f_cand = sem("f_cand")
        f_flag = sem("f_flag")
        f_votes = sem("f_votes")
        f_chosen = sem("f_chosen")
        f_share = sem("f_share")
        f_yw = sem("f_yw")
        f_qk = sem("f_qk")
        f_qk_hi = sem("f_qk_hi")
        f_qk_left = sem("f_qk_left")
        f_qk_mid = sem("f_qk_mid")
        f_qk_lo = sem("f_qk_lo")
        f_qk_store = [sem(f"f_qk_store{tile}") for tile in range(4)]
        f_v = sem("f_v")
        f_v_sb = sem("f_v_sb")
        f_v_pad = sem("f_v_pad")
        f_k_pad = sem("f_k_pad")
        f_gate2 = sem("f_gate2")
        f_ffv = sem("f_ffv")
        f_ffp = sem("f_ffp")
        f_st = sem("f_st")
        f_p = sem("f_p")
        f_pv = sem("f_pv")
        f_attn = sem("f_attn")
        f_mscore = sem("f_mscore")
        f_mred = sem("f_mred")
        f_mx = sem("f_mx")
        f_mxt = sem("f_mxt")
        f_mxrow = sem("f_mxrow")
        f_qrow = sem("f_qrow")
        f_sums = sem("f_sums")
        f_inv = sem("f_inv")
        f_xa = sem("f_xa")
        f_fc1 = sem("f_fc1")
        f_mlp = sem("f_mlp")
        f_fc2 = sem("f_fc2")
        f_o = sem("f_o")
        f_g = sem("f_g")
        f_zz = sem("f_zz")
        f_kload = [sem(f"f_kload{i}") for i in range(2)]
        f_qload = [sem(f"f_qload{c}") for c in range(NC)]

        def ck(c):
            return slice(c * CK, (c + 1) * CK)

        def bn(b, rows=P):
            return bank[0:rows, b, :]

        block = ctx.enter_context(nc.Block())

        @block.sync
        def _(sp):
            sp.dma_start(idx_rows[:], x.rearrange("a (b p) -> (a b) p", p=P)).then_inc(s_idx, 16)
            sp.dma_start(ident[:], consts["ident"]).then_inc(s_const, 16)
            sp.dma_start(fold[:], consts["fold"]).then_inc(s_const, 16)
            for t, name in ((width_mask, "width_mask"), (group_ones, "group_ones"), (sum_pick, "sum_pick"),
                            (search_off, "search_off")):
                sp.dma_start(t[:], consts[name]).then_inc(f_ffn_c, 16)
            for i, name in enumerate(("gamma", "beta")):
                sp.dma_start(ffn_rows[2 * i:2 * i + 2, :], ffn[name].rearrange("(i p) -> i p", i=2)).then_inc(s_vec, 16)
            sp.dma_start(ffn_rows[4:8, :], ffn["b2"].rearrange("(i p) -> i p", i=4)).then_inc(s_vec, 16)
            for i in range(2):
                with nc.allow_non_contiguous_dma(reason="768 numbers"):
                    sp.dma_start(w_router_sb[:, i, :], ffn["w_router"][:, i * CH:(i + 1) * CH].rearrange("e p -> p e")).then_inc(f_ffn_c, 16)
            for k in range(2):
                sp.dma_start(norm_rows[2 * k:2 * k + 2, :], norm_w[k].rearrange("(i p) -> i p", i=2)).then_inc(s_vec, 16)
                sp.dma_start(w_dt_sb[:, k, :], dt_w[k]).then_inc(s_small, 16)
            for k in range(NB):
                sp.dma_start(conv_w_sb[:, k], conv_w[k].rearrange("(j p) a b -> p j (a b)", p=P)).then_inc(s_small, 16)
                for i, v in enumerate((conv_b, d_skip, dt_b)):
                    row = (i * NB + k) * NJ
                    sp.dma_start(vec_rows[row:row + NJ, :], v[k].rearrange("(j p) -> j p", p=P)).then_inc(s_vec, 16)
                sp.dma_start(a_sb[k][:], a_log[k].rearrange("(j p) n -> p j n", p=P)).then_inc(s_small, 16)
                sp.dma_start(w_x_sb[k][:], x_proj[k].rearrange("(j p) n -> p j n", p=P)).then_inc(s_small, 16)
                sp.dma_start(w_out_sb[:, k], w_out[k].rearrange("(j p) n -> p j n", p=P)).then_inc(s_small, 16)
            stacked = 0
            for k in range(NB):
                if k:
                    sp.wait_ge(s_inproj, 6 * NC * k)
                sp.dma_start(w_in_sb[:], w_in[k].rearrange("(i p) n -> p i n", i=2)).then_inc(s_win, 16)
                sp.wait_ge(s_split, NC * (k + 1))
                for g in range(max(1, 2 * BLOCK_N[k] // 32)):
                    for part in range(3):
                        sp.dma_start(part_stack(stack, part, g, 0, L),
                                     parts[32 * g:32 * g + 32, part, :]).then_inc(s_stack, 16)
            sp.wait_ge(s_resid, NC * (NB + 1))
            sp.dma_start(w1t[CH:CH + 1, 1, :], ffn["b1"].rearrange("(a f) -> a f", a=1)).then_inc(f_ffn_c, 16)
            sp.dma_start(w1_raw, ffn["w1"].rearrange("(b p) c -> p b c", p=CH)).then_inc(f_w_raw, 16)
            sp.dma_start(w2_raw, ffn["w2"].rearrange("(b p) f -> p b f", p=CH)).then_inc(f_w_raw, 16)
            for tile in range(4):
                side, half = tile // 2, tile % 2
                sp.wait_ge(f_qk_lo, NC * (tile + 1))
                for j, pair in enumerate(PAIRS):
                    sp.dma_start(qk_dram[side, 6 * half:6 * half + 6, HD * j:HD * j + HD, :],
                                 qk_part[:, tile % 2, pair[side], :]).then_inc(f_qk_store[tile], 16)
            def put_maxima(step, c):
                sp.wait_ge(f_mxrow, step + 1)
                for a in range(3):
                    sp.dma_start(q_stack[KR + a:KR + a + 1, q_cols(c, 0, HG * CK)], max_row[:, a, :]).then_inc(f_qrow, 16)
            for g in range(NG):
                with sp.Fori(0, NC) as c:
                    put_maxima(c + g * NC, c)
            for b in range(L // P):
                sp.wait_ge(s_fin, b + 1)
                sp.dma_start(out[0, b * P:(b + 1) * P, :], tok_rows[:, b, :]).then_inc(s_out, 16)
            sp.wait_ge(s_out, 16 * (L // P))

        SMALL_DMAS = 16 * (2 + NB * 4)
        STACKED = [0]
        for k in range(NB):
            STACKED.append(STACKED[-1] + 16 * 3 * max(1, 2 * BLOCK_N[k] // 32))

        def steps(eng, k, emit, c):
            n = BLOCK_N[k]
            emit(0, range(4), True)
            if n > 4:
                halves = [(4, min(n, 32))] + ([(32, n)] if n > 32 else [])
                for lo, hi in halves:
                    with eng.Fori(lo // 4, hi // 4) as turn:
                        emit(turn * 4, range(4), False, lo)

        @block.gpsimd
        def _(pool):
            pool.wait_ge(s_idx_ok, 2)
            for b in range(L // P):
                pool.indirect_dma_start(tok_rows[:, b, :], None, emb,
                                        bass.IndirectOffsetOnAxis(idx[:, b:b + 1], 0)).then_inc(s_rows[b * P // CK], 16)
            for k in range(NB):
                n = BLOCK_N[k]
                for c in range(NC):
                    base = STEP0[k] + c * n
                    with pool.Fori(0, n // 4) as turn:
                        s = turn * 4
                        for i in range(4):
                            pool.wait_ge(s_carry, s + (base + i + 1))
                            pool.wait_ge(s_c_row, s + (base + i + 1))
                            cr = c_row[:, i % 2, :].unsqueeze(1).broadcast_to([P, NJ, CK])
                            pool.tensor_tensor(h_slot[:, i], h_slot[:, i], cr, ALU.mult).then_inc(s_hc, 1)
            pool.wait_ge(f_w_turned, 32)
            pool.memset(v_sb, 0.0).then_inc(f_v_pad, 1)
            pool.wait_ge(f_v_pad, 1)
            pool.memset(v_sb[:, :, :, HD:HD + 1], 1.0).then_inc(f_v_pad, 1)
            for tile in range(4):
                for c in range(NC):
                    pool.wait_ge(f_qk_mid, NC * tile + c + 1)
                    pool.tensor_tensor(qk_part[:, tile % 2, 2, ck(c)], qk_left[:, ck(c)], qk_part[:, tile % 2, 1, ck(c)],
                                       ALU.subtract).then_inc(f_qk_lo, 1)
            for tile in range(4):
                pool.wait_ge(f_qk_store[tile], 16 * len(PAIRS))

            def load_k(g):
                pool.dma_start(k_stack[g % 2][0:KR], qk_dram[1, HG * g:HG * g + HG].rearrange("h r t -> r h t")).then_inc(f_kload[g % 2], 16)

            def load_q(g, c):
                pool.dma_start(q_stack[0:KR, q_cols(c, 0, HG * CK)].rearrange("r (h t) -> r h t", h=HG),
                               qk_dram[0, HG * g:HG * g + HG, :, ck(c)].rearrange("h r t -> r h t")).then_inc(f_qload[c], 16)
            load_k(0)
            for c in range(NC):
                load_q(0, c)
            load_k(1)
            for i in range(2):
                pool.memset(k_stack[i][KR:KR + 3], 1.0).then_inc(f_k_pad, 1)
            for g in range(NG - 1):
                for c in range(NC):
                    pool.wait_ge(f_p, 2 * KT * (NC * g + c + 1) + P0)
                    load_q(g + 1, c)
                if g + 2 < NG:
                    load_k(g + 2)

        @block.scalar
        def _(act):
            def norm_act(r):
                src = xn if r < 4 else yw[0:CH]
                for c in range(NC):
                    if r < 2:
                        act.wait_ge(s_resid, NC * r + (c + 1 if r else NC))
                        src = resid
                    else:
                        act.wait_ge(s_centered, NC * (r - 2) + c + 1)
                    act.activation(square[:, :, ck(c)], src[:, :, ck(c)], ACT.Square).then_inc(s_square, 1)
                for c in range(NC):
                    act.wait_ge(s_inv, NC * r + c + 1)
                    act.activation(rstd[:, ck(c)], rstd[:, ck(c)], ACT.Sqrt).then_inc(s_rstd, 1)

            for k in range(NB):
                n = BLOCK_N[k]
                norm_act(k)
                for m in range(2 * NJ):
                    for c in range(NC):
                        item = m * NC + c
                        act.wait_ge(s_inproj, 6 * NC * k + item + 1)
                        if m < NJ:
                            act.activation(dtu[:, m, ck(c)], bn(item % 8), ACT.Copy).then_inc(s_inproj_out, 1)
                        else:
                            act.activation(gate[:, m - NJ, ck(c)], bn(item % 8), ACT.Silu).then_inc(s_inproj_out, 1)
                for j in range(NJ):
                    act.wait_ge(s_conv, NJ * k + j + 1)
                    act.activation(u[:, j, :], u[:, j, :], ACT.Silu, bias=vec_sb[:, 0, k, j:j + 1]).then_inc(s_u, 1)
                R = BLOCK_R[k]
                for c in range(NC):
                    act.wait_ge(s_dt_in, NC * k + c + 1)
                    act.activation(dt_low[0:R, ck(c)], bn(4 + c, R), ACT.Copy).then_inc(s_dt_sb, 1)
                act.wait_ge(s_a_log, k + 1)
                act.activation(a_sb[k][:], a_sb[k][:], ACT.Exp).then_inc(s_a_mat, 1)
                for j in range(NJ):
                    act.wait_ge(s_dt_x, NC * (NJ * k + j + 1))
                    act.activation(soft[:, j, :], delta[:, j, :], ACT.Abs).then_inc(s_act, 1)
                    act.wait_ge(s_act, 2 * NJ * k + 2 * j + 1)
                    act.activation(soft[:, j, :], soft[:, j, :], ACT.Exp, scale=-1.0).then_inc(s_act, 1)
                act.wait_ge(s_act, 2 * NJ * (k + 1))
                for j in range(NJ):
                    act.activation(dtu[:, j, :], soft[:, j, :], ACT.Ln, bias=1.0).then_inc(s_u_ln, 1)
                act.wait_ge(s_a_ready, k + 1)
                act.wait_ge(s_dtu, NJ * (k + 1))
                for c in range(NC):
                    base = STEP0[k] + c * n

                    def scan_act(s, us, first, lo=0):
                        for i in us:
                            if not first or i >= A_SLOTS or k + c:
                                act.wait_ge(s_scan, s + (base + i + 1 - A_SLOTS))
                            for j in range(NJ):
                                ins = act.activation(a_slot[:, i % 2, j, :], delta[:, j, ck(c)], ACT.Exp,
                                                     scale=a_sb[k][:, j, bass.ds(s + i, 1)])
                            ins.then_inc(s_a, 1)
                            act.wait_ge(s_c_bc, s + (base + i + 1))
                            if not first or i >= 2 or k + c:
                                act.wait_ge(s_hc, s + (base + i - 1))
                            act.activation(c_row[:, i % 2, :], bn(4), ACT.Copy).then_inc(s_c_row, 1)
                    steps(act, k, scan_act, c)
            norm_act(3)
            norm_act(4)
            act.wait_ge(f_logit, 2)
            act.activation(probs[:], probs[:], ACT.Exp).then_inc(f_probs, 1)
            for c in range(NC):
                act.wait_ge(f_prob_t, c + 1)
                act.activation(prob_bc[:, ck(c)], bn(4 + c), ACT.Copy).then_inc(f_prob_bc, 1)
            for tile in range(4):
                scale = HD ** -0.5 if tile < 2 else 1.0
                for c in range(NC):
                    item = tile * NC + c
                    act.wait_ge(f_qk, item + 1)
                    if tile >= 2 and c == 0:
                        act.wait_ge(f_qk_store[tile - 2], 16 * len(PAIRS))
                    act.activation(qk_part[:, tile % 2, 0, ck(c)], bn(item % 8, CH), ACT.Copy, scale=scale).then_inc(f_qk_hi, 1)
                    act.wait_ge(f_qk_left, item + 1)
                    act.activation(qk_part[:, tile % 2, 1, ck(c)], qk_left[:, ck(c)], ACT.Copy).then_inc(f_qk_mid, 1)
            act.wait_ge(f_v_pad, 2)
            for b in range(KT):
                act.wait_ge(f_v, b + 1)
                act.activation(v_sb[:, b, :, 0:HD], bank[:, b % 8, 0:C].rearrange("p (h d) -> p h d", h=HEADS),
                               ACT.Copy).then_inc(f_v_sb, 1)
            def attn_act(step):
                for kt in range(KT):
                    for half in range(2):
                        act.wait_ge(f_st, (step * (2 * KT)) + (2 * kt + half + 1))
                        act.wait_ge(f_pv, step * KT + (kt - 1 + PV0))
                        act.activation(p_slot[:, 2 * (kt % 2) + half], bank[:, 2 * half:2 * half + 2, :],
                                       ACT.Exp).then_inc(f_p, 1)
            for g in range(NG):
                with act.Fori(0, NC) as c:
                    attn_act(c + g * NC)
            for f in range(HID // P):
                for c in range(NC):
                    item = f * NC + c
                    act.wait_ge(f_fc1, item + 1)
                    act.activation(mlp[:, f, ck(c)], bn(item % 8), ACT.Gelu).then_inc(f_mlp, 1)
            for c in range(NC):
                for i in range(2):
                    item = 2 * c + i
                    act.wait_ge(f_fc2, item + 1)
                    act.activation(o_sb[:, i, ck(c)], bn(item % 4, CH), ACT.Identity, bias=b2_sum[:, i:i + 1]).then_inc(f_o, 1)

        @block.vector
        def _(dve):
            chain = [0]

            def link(ins):
                chain[0] += 1
                ins.then_inc(s_v, 1)
                dve.wait_ge(s_v, chain[0])

            dve.wait_ge(s_idx, 16)
            link(dve.tensor_scalar(idx_f[:, 0, :], idx_rows[:], 0.0, float(V), ALU.is_lt, ALU.mult))
            link(dve.tensor_tensor(idx_f[:, 1, :], idx_rows[:], idx_f[:, 0, :], ALU.add))
            dve.tensor_scalar(idx_f[:, 0, :], idx_f[:, 1, :], 0.0, float(V - 1), ALU.max, ALU.min).then_inc(s_idx_ok, 1)
            dve.wait_ge(s_turned, 1)
            dve.tensor_copy(idx[:], bank[:, 5, 0:L // P]).then_inc(s_idx_ok, 1)
            dve.wait_ge(s_turned, 2)
            dve.tensor_copy(vec_sb[:].rearrange("p a b c -> p (a b c)"), bank[:, 7, 0:3 * NB * NJ]).then_inc(s_vec_ok, 1)
            dve.tensor_copy(norm_sb[:].rearrange("p a b -> p (a b)"), bank[0:CH, 6, 0:4]).then_inc(s_vec_ok, 1)
            dve.tensor_copy(ffn_vec[:].rearrange("p a b -> p (a b)"), bank[0:CH, 6, 8:16]).then_inc(s_vec_ok, 1)
            dve.memset(ones[:], 1.0).then_inc(s_sel, 1)
            dve.memset(xr[:, :, 0:TAPS - 1], 0.0)
            dve.wait_ge(s_const, 32)
            dve.tensor_copy(sel[:], fold[0:96, :].unsqueeze(2).broadcast_to([96, 32, P])).then_inc(s_sel, 1)
            for c in range(NC):
                dve.wait_ge(s_rows_t, c + 1)
                dve.tensor_copy(resid[:, :, ck(c)], bank[0:CH, 2 * c:2 * c + 2, :]).then_inc(s_resid, 1)
            dve.wait_ge(s_small, SMALL_DMAS)
            for k in range(NB):
                dve.tensor_scalar(a_sb[k][:], a_sb[k][:], A_LOG_MAX, None, ALU.min).then_inc(s_a_log, 1)

            def norm_dve(r, eps, w, src=resid, xn=xn):
                if r >= 2:
                    for c in range(NC):
                        dve.wait_ge(s_sum, NC * (r - 2) + c + 1)
                        mean = bank[0:CH, c:c + 1, :].broadcast_to([CH, 2, CK])
                        dve.scalar_tensor_tensor(xn[:, :, ck(c)], mean, -1.0 / C, src[:, :, ck(c)],
                                                 ALU.mult, ALU.add).then_inc(s_centered, 1)
                for c in range(NC):
                    dve.wait_ge(s_var, NC * r + c + 1)
                    link(dve.tensor_scalar(rstd[:, ck(c)], bn(4 + c, CH), 1.0 / C, eps, ALU.mult, ALU.add))
                    dve.reciprocal(rstd[:, ck(c)], rstd[:, ck(c)]).then_inc(s_inv, 1)
                for c in range(NC):
                    dve.wait_ge(s_rstd, NC * r + c + 1)
                    for i in range(2):
                        if w is not None:
                            ins = dve.scalar_tensor_tensor(xn[:, i, ck(c)], resid[:, i, ck(c)], w[:, i:i + 1],
                                                           rstd[:, ck(c)], ALU.mult, ALU.mult)
                        else:
                            ins = dve.tensor_tensor(xn[:, i, ck(c)], xn[:, i, ck(c)], rstd[:, ck(c)], ALU.mult)
                    ins.then_inc(s_norm, 1)

            for k in range(NB):
                n, R = BLOCK_N[k], BLOCK_R[k]
                norm_dve(k, 1e-5, norm_sb[:, k] if k < 2 else None)
                for j in range(NJ):
                    dve.wait_ge(s_inproj_out, 6 * NC * k + NC * (j + 1))
                    link(dve.tensor_scalar(u[:, j, :], xr[:, j, 0:L], conv_w_sb[:, k, j, 0:1], None, ALU.mult))
                    for t in range(1, TAPS):
                        ins = dve.scalar_tensor_tensor(u[:, j, :], xr[:, j, t:t + L], conv_w_sb[:, k, j, t:t + 1],
                                                       u[:, j, :], ALU.mult, ALU.add)
                        if t < TAPS - 1:
                            link(ins)
                    ins.then_inc(s_conv, 1)
                G = min(P, 2 * n)
                for c in range(NC):
                    dve.wait_ge(s_bc_rows, NC * k + c + 1)
                    link(dve.tensor_copy(parts[0:G, 0, ck(c)], bn(c, G)))
                    link(dve.tensor_tensor(left[0:G, ck(c)], bn(c, G), parts[0:G, 0, ck(c)], ALU.subtract))
                    link(dve.tensor_copy(parts[0:G, 1, ck(c)], left[0:G, ck(c)]))
                    dve.tensor_tensor(parts[0:G, 2, ck(c)], left[0:G, ck(c)], parts[0:G, 1, ck(c)],
                                      ALU.subtract).then_inc(s_split, 1)
                for j in range(NJ):
                    for c in range(NC):
                        item = j * NC + c
                        dve.wait_ge(s_dt_proj, NJ * NC * k + item + 1)
                        ins = dve.tensor_scalar(delta[:, j, ck(c)], bn(item % 8), vec_sb[:, 2, k, j:j + 1], None, ALU.add)
                        ins.then_inc(s_dt_x, 1)
                dve.wait_ge(s_a_mat, k + 1)
                dve.tensor_scalar(a_sb[k][:], a_sb[k][:], -1.0, None, ALU.mult).then_inc(s_a_ready, 1)
                for j in range(NJ):
                    dve.tensor_scalar(diag[:, j, :], ident[:], vec_sb[:, 1, k, j:j + 1], None, ALU.mult).then_inc(s_diag, 1)
                dve.memset(state[:], 0.0)
                for j in range(NJ):
                    dve.wait_ge(s_u_ln, NJ * k + j + 1)
                    dve.tensor_tensor(dtu[:, j, :], dtu[:, j, :], soft[:, j, :], ALU.add)
                    link(dve.tensor_scalar(soft[:, j, :], soft[:, j, :], 1.0, 1.0, ALU.add, ALU.subtract))
                    link(dve.tensor_tensor(dtu[:, j, :], dtu[:, j, :], soft[:, j, :], ALU.subtract))
                    link(dve.scalar_tensor_tensor(delta[:, j, :], delta[:, j, :], 0.0, dtu[:, j, :], ALU.max, ALU.add))
                    dve.tensor_tensor(dtu[:, j, :], delta[:, j, :], u[:, j, :], ALU.mult).then_inc(s_dtu, 1)
                dve.wait_ge(s_dtu, NJ * (k + 1))
                for c in range(NC):
                    base = STEP0[k] + c * n

                    def scan_dve(s, us, first, lo=0):
                        for i in us:
                            dve.wait_ge(s_b_bc, s + (base + i + 1))
                            if not first or i or k + c:
                                dve.wait_ge(s_carry, s + (base + i))
                            b_row = bank[:, 3:4, :].broadcast_to([P, NJ, CK])
                            dve.tensor_tensor(bank[:, 5:8, :], dtu[:, :, ck(c)], b_row, ALU.mult).then_inc(s_b_used, 1)
                            dve.wait_ge(s_b_used, s + (base + i + 1))
                            dve.wait_ge(s_a, s + (base + i + 1))
                            if not first or k + c:
                                dve.wait_ge(s_ysum, s + (base + i + 1 - H_SLOTS))
                            for j in range(NJ):
                                ins = dve.tensor_tensor_scan(h_slot[:, i, j, :], a_slot[:, i % 2, j, :], bank[:, 5 + j, :],
                                                             state[:, bass.ds(s + i, 1), j:j + 1].rearrange("p a b -> p (a b)"),
                                                             ALU.mult, ALU.add)
                            ins.then_inc(s_scan, 1)
                            dve.wait_ge(s_scan, s + (base + i + 1))
                            dve.tensor_scalar(state[:, bass.ds(s + i, 1), :].rearrange("p a b -> p (a b)"),
                                              h_slot[:, i, :, CK - 1], 1.0, None, ALU.mult).then_inc(s_carry, 1)
                    steps(dve, k, scan_dve, c)
                    dve.wait_ge(s_ysum, base + n)
                    dve.tensor_tensor(gate[:, :, ck(c)], bank[:, 0:3, :], gate[:, :, ck(c)], ALU.mult).then_inc(s_y, 1)
                for c in range(NC):
                    dve.wait_ge(s_outproj, NC * k + c + 1)
                    dve.tensor_tensor(resid[:, :, ck(c)], resid[:, :, ck(c)], bank[0:CH, 2 * c:2 * c + 2, :],
                                      ALU.add).then_inc(s_resid, 1)
            norm_dve(3, 1e-5, None)
            for c in range(NC):
                dve.wait_ge(s_norm, NC * 3 + c + 1)
                dve.tensor_tensor(resid[:, :, ck(c)], resid[:, :, ck(c)], xf[:, :, ck(c)], ALU.add).then_inc(f_zz, 1)
            norm_dve(4, 1e-6, None, src=xf, xn=yw[0:CH])
            dve.wait_ge(s_norm, NC * 5)
            for i in range(2):
                ins = dve.tensor_scalar(yw[0:CH, i, :], yw[0:CH, i, :], ffn_vec[:, 0, i:i + 1], ffn_vec[:, 1, i:i + 1],
                                        ALU.mult, ALU.add)
            link(ins)
            dve.tensor_tensor(b2_sum, b2_sum, ffn_vec[:, 3, :], ALU.add).then_inc(f_ffv, 1)
            dve.wait_ge(f_w_raw, 32)
            dve.memset(w2_pad, 0.0).then_inc(f_pv, PV0)
            dve.memset(max_part[:], 0.0).then_inc(f_p, P0)
            dve.memset(max_q[:], 0.0).then_inc(f_attn, O0)
            link(dve.tensor_tensor(w2_raw[:, 0:2, :], w2_raw[:, 0:2, :], w2_raw[:, 2:4, :], ALU.add))
            for i in range(2):
                ins = dve.tensor_copy(w2_pad[:, i, :, :, 0:HD],
                                      w2_raw[:, i, HID:F2].rearrange("p (g j d) -> p g j d", g=NG, j=HG))
            ins.then_inc(f_w2_sum, 1)
            for b in range(14):
                dve.wait_ge(f_w_turn, b + 1)
                dve.tensor_copy(w1t[0:CH, :, b * CH:(b + 1) * CH],
                                bank[0:CH, b % 8, 0:2 * CH].rearrange("p (i f) -> p i f", i=2)).then_inc(f_w_turned, 1)
            for b in range(18):
                f, i = b // 2, b % 2
                dve.wait_ge(f_w_turn, 14 + b + 1)
                dve.tensor_copy(w2t[:, f, i * CH:(i + 1) * CH], bank[:, (14 + b) % 8, 0:CH]).then_inc(f_w_turned, 1)
            dve.wait_ge(f_logit, 1)
            lg = bank[:, 0, 0:KT * E].rearrange("p (b e) -> p b e", e=E)
            link(dve.tensor_reduce(psum_e[:], lg, AX_X, ALU.max))
            dve.tensor_tensor(probs[:], lg, psum_e[:].unsqueeze(2).broadcast_to([P, KT, E]), ALU.subtract).then_inc(f_logit, 1)
            dve.wait_ge(f_probs, 1)
            link(dve.tensor_reduce(psum_e[:], probs[:], AX_X, ALU.add))
            link(dve.reciprocal(psum_e[:], psum_e[:]))
            dve.tensor_tensor(prob_wide, probs[:].unsqueeze(3).broadcast_to([P, KT, E, 32]),
                              psum_e[:].unsqueeze(2).unsqueeze(3).broadcast_to([P, KT, E, 32]), ALU.mult).then_inc(f_probs, 1)
            dve.wait_ge(f_ffn_c, 16 * 7)
            link(dve.memset(search_i[:, 0:1], 0))
            dve.wait_ge(f_prob_bc, NC)
            for r in range(SEARCH_ROUNDS):
                link(dve.tensor_tensor(search_i[:, 1:2], search_i[:, 0:1], search_off[:, r:r + 1], ALU.bitwise_or))
                link(dve.tensor_scalar(flag, prob_bc, search_i[:, 1:2].bitcast(F32), 0.0, ALU.is_ge, ALU.add,
                                       accum_out=search[:, 0:1]))
                dve.tensor_scalar(search[:, 1:2], search[:, 0:1], float(CAP), None, ALU.is_ge).then_inc(f_flag, 1)
                dve.wait_ge(f_votes, r + 1)
                link(dve.tensor_scalar(search_i[:, 2:3], bank[:, 0, r:r + 1], 1.0,
                                       float(2 ** (SEARCH_BITS * (SEARCH_ROUNDS - 1 - r))), ALU.subtract, ALU.mult))
                link(dve.tensor_tensor(search_i[:, 0:1], search_i[:, 0:1], search_i[:, 2:3], ALU.bitwise_or))
            least = search_i[:, 0:1].bitcast(F32)
            link(dve.tensor_scalar(chosen, prob_bc, least, 0.0, ALU.is_gt, ALU.add, accum_out=search[:, 2:3]))
            link(dve.tensor_scalar(search[:, 3:4], search[:, 2:3], -1.0, float(CAP), ALU.mult, ALU.add))
            link(dve.tensor_scalar(flag, prob_bc, least, None, ALU.is_equal))
            link(dve.tensor_tensor_scan(prefix, flag, flag, 0.0, ALU.add, ALU.max))
            link(dve.scalar_tensor_tensor(flag, prefix, search[:, 3:4], flag, ALU.is_le, ALU.mult))
            link(dve.tensor_tensor(chosen, chosen, flag, ALU.add))
            dve.tensor_tensor(selgate, chosen, prob_bc, ALU.mult).then_inc(f_chosen, 1)
            for c in range(NC):
                dve.wait_ge(f_share, c + 1)
                dve.tensor_tensor(yw[0:CH, :, ck(c)], yw[0:CH, :, ck(c)], bank[0:CH, 2 * c:2 * c + 2, :], ALU.mult)
                dve.tensor_copy(yw[CH:CH + 1, 1, ck(c)], bank[CH:CH + 1, 2 * c + 1, :]).then_inc(f_yw, 1)
            for tile in range(4):
                scale = HD ** -0.5 if tile < 2 else 1.0
                for c in range(NC):
                    item = tile * NC + c
                    dve.wait_ge(f_qk_hi, item + 1)
                    if tile:
                        dve.wait_ge(f_qk_lo, item - NC + 1)
                    dve.scalar_tensor_tensor(qk_left[:, ck(c)], bn(item % 8, CH), scale, qk_part[:, tile % 2, 0, ck(c)],
                                             ALU.mult, ALU.subtract).then_inc(f_qk_left, 1)
            def max_dve(step):
                for m in range(HG * 4 * 4):
                    dve.wait_ge(f_mscore, step * (HG * 4 * 4) + (m + 1))
                    dve.tensor_reduce(max_part[:, m // 4, m % 4:m % 4 + 1], bank[:, 5 + m % MAX_RING, :], AX_X, ALU.max).then_inc(f_mred, 1)
                dve.wait_ge(f_mred, (step + 1) * (HG * 4 * 4))
                dve.tensor_reduce(max_q[:], max_part[:], AX_X, ALU.max).then_inc(f_mx, 1)
                dve.wait_ge(f_mxt, step + 1)
                dve.wait_ge(f_qrow, step * 48)
                turned = bank[0:HG * 4, 7, 0:P]
                dve.tensor_scalar(max_row[:, 0, :], turned, -1.0, None, ALU.mult).then_inc(f_ffv, 1)
                dve.wait_ge(f_ffv, step * 3 + 2)
                dve.scalar_tensor_tensor(max_left[:], turned, -1.0, max_row[:, 0, :], ALU.mult, ALU.subtract).then_inc(f_ffv, 1)
                dve.wait_ge(f_ffv, step * 3 + 3)
                dve.tensor_copy(max_row[:, 1, :], max_left[:]).then_inc(f_ffv, 1)
                dve.wait_ge(f_ffv, step * 3 + 4)
                dve.tensor_tensor(max_row[:, 2, :], max_left[:], max_row[:, 1, :], ALU.subtract).then_inc(f_mxrow, 1)

            def take_o(step, g, c):
                dve.wait_ge(f_pv, (step + 1) * KT + PV0)
                dve.tensor_scalar(xa[:, g, bass.ds(c * CK, CK)], bank[:, 4, :], 1.0, None, ALU.mult).then_inc(f_attn, 1)
            max_dve(0)
            for g in range(NG):
                with dve.Fori(0, NC - 1) as c:
                    max_dve(c + (g * NC + 1))
                    take_o(c + g * NC, g, c)
                if g < NG - 1:
                    max_dve((g + 1) * NC)
                take_o(g * NC + NC - 1, g, NC - 1)
            for item in range(NG * NC):
                g, c = item // NC, item % NC
                dve.wait_ge(f_sums, item + 1)
                dve.reciprocal(inv_sb[:, (item % 2) * CK:(item % 2) * CK + CK], bn(item % 8)).then_inc(f_inv, 1)
                dve.wait_ge(f_inv, item + 1)
                dve.tensor_tensor(xa[:, g, ck(c)], xa[:, g, ck(c)], inv_sb[:, (item % 2) * CK:(item % 2) * CK + CK],
                                  ALU.mult).then_inc(f_xa, 1)
            for c in range(NC):
                for i in range(2):
                    item = 2 * c + i
                    dve.wait_ge(f_g, item + 1)
                    dve.wait_ge(f_o, item + 1)
                    link(dve.tensor_tensor(o_sb[:, i, ck(c)], o_sb[:, i, ck(c)], bn(4 + item % 4, CH), ALU.mult))
                    dve.tensor_tensor(resid[:, i, ck(c)], resid[:, i, ck(c)], o_sb[:, i, ck(c)], ALU.add).then_inc(f_zz, 1)
            for b in range(L // P):
                dve.wait_ge(s_fin_t, b + 1)
                dve.tensor_copy(tok_rows[:, b, :], bank[:, b % 8, 0:C]).then_inc(s_fin, 1)

        @block.tensor
        def _(pe):
            pe.wait_ge(s_const, 32)
            pe.wait_ge(s_idx_ok, 1)
            pe.transpose(bank[:, 5, 0:L // P], idx_f[:, 0, :], ident[0:L // P, 0:L // P]).then_inc(s_turned, 1)
            pe.wait_ge(s_vec, 16 * (5 + 3 * NB))
            pe.transpose(bank[0:CH, 6, 0:4], norm_rows[:], ident[0:4, 0:4])
            pe.transpose(bank[0:CH, 6, 8:16], ffn_rows[:], ident[0:8, 0:8])
            pe.transpose(bank[:, 7, 0:3 * NB * NJ], vec_rows[:], ident[0:3 * NB * NJ, 0:3 * NB * NJ]).then_inc(s_turned, 1)
            pe.wait_ge(s_vec_ok, 3)
            for c in range(NC):
                for i in range(2):
                    for t in range(CK // P):
                        b = c * (CK // P) + t
                        if i == 0 and t == 0:
                            pe.wait_ge(s_rows[c], 16 * (CK // P))
                        ins = pe.transpose(bank[0:CH, 2 * c + i, t * P:(t + 1) * P], tok_rows[:, b, i * CH:(i + 1) * CH], ident[:])
                ins.then_inc(s_rows_t, 1)
            pe.wait_ge(s_sel, 2)

            def norm_pe(r, resid=resid):
                if r >= 2:
                    if r < 4:
                        pe.wait_ge(s_resid, NC * (r + 1))
                    else:
                        pe.wait_ge(s_norm, NC * 4)
                    for c in range(NC):
                        for i in range(2):
                            ins = pe.matmul(bn(c, CH), ones[0:CH, 0:CH], resid[:, i, ck(c)], start=i == 0, stop=i == 1)
                        ins.then_inc(s_sum, 1)
                else:
                    pe.wait_ge(s_resid, NC * (r + 1))
                for c in range(NC):
                    pe.wait_ge(s_square, NC * r + c + 1)
                    for i in range(2):
                        ins = pe.matmul(bn(4 + c, CH), ones[0:CH, 0:CH], square[:, i, ck(c)], start=i == 0, stop=i == 1)
                    ins.then_inc(s_var, 1)

            for k in range(NB):
                n, R = BLOCK_N[k], BLOCK_R[k]
                norm_pe(k)
                pe.wait_ge(s_win, 16 * (k + 1))
                for m in range(2 * NJ):
                    for c in range(NC):
                        item = m * NC + c
                        if m == 0:
                            pe.wait_ge(s_norm, NC * k + c + 1)
                        if item >= 8:
                            pe.wait_ge(s_inproj_out, 6 * NC * k + item - 7)
                        for i in range(2):
                            ins = pe.matmul(bn(item % 8), w_in_sb[:, i, m * P:(m + 1) * P], xn[:, i, ck(c)],
                                            start=i == 0, stop=i == 1)
                        ins.then_inc(s_inproj, 1)
                G = min(P, 2 * n)
                cols = (R, 0) if k < 2 else (0, 2 * n)
                pe.wait_ge(s_inproj_out, 6 * NC * (k + 1))
                pe.wait_ge(s_u, NJ * (k + 1))
                for c in range(NC):
                    for j in range(NJ):
                        ins = pe.matmul(bn(c, G), w_x_sb[k][:, j, cols[0]:cols[0] + G], u[:, j, ck(c)],
                                        start=j == 0, stop=j == NJ - 1)
                    ins.then_inc(s_bc_rows, 1)
                    for j in range(NJ):
                        ins = pe.matmul(bn(4 + c, R), w_x_sb[k][:, j, cols[1]:cols[1] + R], u[:, j, ck(c)],
                                        start=j == 0, stop=j == NJ - 1)
                    ins.then_inc(s_dt_in, 1)
                pe.wait_ge(s_split, NC * (k + 1))
                pe.wait_ge(s_dt_sb, NC * (k + 1))
                for j in range(NJ):
                    for c in range(NC):
                        item = j * NC + c
                        if item >= 8:
                            pe.wait_ge(s_dt_x, NJ * NC * k + item - 7)
                        w = w_dt_sb[:, k, j * P:(j + 1) * P] if k < 2 else ones[0:1, :]
                        pe.matmul(bn(item % 8), w, dt_low[0:R, ck(c)], start=True, stop=True).then_inc(s_dt_proj, 1)
                pe.wait_ge(s_stack, STACKED[k + 1])
                pe.wait_ge(s_diag, NJ * (k + 1))
                pe.wait_ge(s_dt_x, NJ * NC * (k + 1))
                for c in range(NC):
                    base = STEP0[k] + c * n
                    if c:
                        pe.wait_ge(s_y, NC * k + c)
                    for j in range(NJ):
                        pe.matmul(bn(j), diag[:, j, :], u[:, j, ck(c)], start=True, stop=False, skip_group_check=True)

                    def add_up(s, v, last=False):
                        pe.wait_ge(s_hc, s + (base + v + 1))
                        for j in range(NJ):
                            ins = pe.matmul(bn(j), ident[:], h_slot[:, v % H_SLOTS, j, :], start=False, stop=last,
                                            skip_group_check=True)
                        ins.then_inc(s_ysum, 1)

                    def scan_pe(s, us, first, lo=0):
                        for i in us:
                            if n < 32:
                                gb, gc, nb, nc_ = 0, 0, s + i, s + (i + n)
                            else:
                                gb = 0 if first else lo // 32
                                gc, nb, nc_ = gb + 2, s + (i - 32 * gb), s + (i - 32 * gb)
                            if not first or i or k + c:
                                pe.wait_ge(s_b_used, s + (base + i))
                            pe.matmul(bn(3), sel[:, bass.ds(nb, 1), :].rearrange("p a m -> p (a m)"), stack[:, gb, ck(c)],
                                      start=True, stop=True).then_inc(s_b_bc, 1)
                            if not first or i or k + c:
                                pe.wait_ge(s_c_row, s + (base + i))
                            pe.matmul(bn(4), sel[:, bass.ds(nc_, 1), :].rearrange("p a m -> p (a m)"), stack[:, gc, ck(c)],
                                      start=True, stop=True).then_inc(s_c_bc, 1)
                            if not first or i >= LAG:
                                add_up(s, i - LAG)
                    steps(pe, k, scan_pe, c)
                    for v in range(n - LAG, n):
                        add_up(0, v, last=v == n - 1)
                pe.wait_ge(s_y, NC * (k + 1))
                for c in range(NC):
                    for i in range(2):
                        for j in range(NJ):
                            ins = pe.matmul(bn(2 * c + i, CH), w_out_sb[:, k, j, i * CH:(i + 1) * CH], gate[:, j, ck(c)],
                                            start=j == 0, stop=j == NJ - 1)
                    ins.then_inc(s_outproj, 1)
            norm_pe(3)
            norm_pe(4, resid=xf)
            pe.wait_ge(f_w2_sum, 1)
            for b in range(14):
                if b < 8:
                    pe.wait_ge(s_norm, NC * 5)
                else:
                    pe.wait_ge(f_w_turned, b - 7)
                for i in range(2):
                    ins = pe.transpose(bank[0:CH, b % 8, i * CH:(i + 1) * CH], w1_raw[:, b, i * CH:(i + 1) * CH], ident[0:CH, 0:CH])
                ins.then_inc(f_w_turn, 1)
            for b in range(18):
                f, i = b // 2, b % 2
                pe.wait_ge(f_w_turned, 14 + b - 7)
                w = w2_raw[:, i, f * P:(f + 1) * P] if f < HID // P else w2_pad[:, i, f - HID // P].rearrange("p j d -> p (j d)")
                pe.transpose(bank[:, (14 + b) % 8, 0:CH], w, ident[0:CH, 0:CH]).then_inc(f_w_turn, 1)
            pe.wait_ge(f_w_turned, 32)
            pe.wait_ge(f_ffn_c, 16 * 7)
            for b in range(KT):
                for i in range(2):
                    ins = pe.matmul(bank[:, 0, b * E:(b + 1) * E], xf[:, i, b * P:(b + 1) * P], w_router_sb[:, i, :],
                                    start=i == 0, stop=i == 1)
            ins.then_inc(f_logit, 1)
            pe.wait_ge(f_probs, 2)
            for b in range(KT):
                ins = pe.transpose(bank[:, 4 + b // 4, (b % 4) * P:(b % 4 + 1) * P],
                                   prob_wide[:, b].rearrange("p e m -> p (e m)"), ident[:])
                if b % 4 == 3:
                    ins.then_inc(f_prob_t, 1)
            for r in range(SEARCH_ROUNDS):
                pe.wait_ge(f_flag, r + 1)
                pe.matmul(bank[:, 0, r:r + 1], group_ones[:], search[:, 1:2], start=True, stop=True).then_inc(f_votes, 1)
            pe.wait_ge(f_chosen, 1)
            for c in range(NC):
                for i in range(2):
                    ins = pe.matmul(bn(2 * c + i, CH + i), width_mask[:, i * CH:(i + 1) * CH + i], chosen[:, ck(c)],
                                    start=True, stop=True)
                ins.then_inc(f_share, 1)
            pe.wait_ge(f_yw, NC)
            for tile in range(4):
                for c in range(NC):
                    item = tile * NC + c
                    if item >= 8:
                        pe.wait_ge(f_qk_left, item - 7)
                    for i in range(2):
                        ins = pe.matmul(bn(item % 8, CH), w1t[0:CH + i, i, HID + tile * CH:HID + (tile + 1) * CH],
                                        yw[0:CH + i, i, ck(c)], start=i == 0, stop=i == 1)
                    ins.then_inc(f_qk, 1)
            pe.wait_ge(f_qk_left, 4 * NC)
            for b in range(KT):
                if b >= 8:
                    pe.wait_ge(f_v_sb, b - 7)
                for i in range(2):
                    ins = pe.matmul(bank[:, b % 8, 0:C], yw[0:CH + i, i, b * P:(b + 1) * P], w1t[0:CH + i, i, HID + 2 * C:F1],
                                    start=i == 0, stop=i == 1)
                ins.then_inc(f_v, 1)
            pe.wait_ge(f_v_sb, KT)

            def max_pe(step, g, c, item):
                head, qt = item // 4, item % 4
                for r in range(4):
                    m = item * 4 + r
                    if m < MAX_RING:
                        pe.wait_ge(f_mred, step * 64)
                        if m == 2:
                            pe.wait_ge(f_mxrow, step)
                    else:
                        pe.wait_ge(f_mred, step * 64 + (m + 1 - MAX_RING))
                    pe.matmul(bank[:, 5 + m % MAX_RING, :], q_stack[0:KR, q_cols(c, head, P, qt * P)],
                              k_stack[g % 2][0:KR, head, r * CK:(r + 1) * CK], start=True, stop=True).then_inc(f_mscore, 1)

            def max_end(step):
                pe.wait_ge(f_mx, step + 1)
                pe.transpose(bank[0:HG * 4, 7, 0:P], max_q[:], ident[:]).then_inc(f_mxt, 1)

            def values(step, g, kt):
                pe.wait_ge(f_p, step * (2 * KT) + (2 * (kt + 1) + P0))
                if kt == 0:
                    pe.wait_ge(f_attn, step + O0)
                for h in range(HG):
                    ins = pe.matmul(bank[32 * h:32 * h + 32, 4, :], v_sb[:, kt, HG * g + h, :], p_slot[:, 2 * (kt % 2) + h // 2, h % 2, :],
                                    start=kt == 0, stop=kt == KT - 1, tile_position=(0, 32 * h), skip_group_check=True)
                ins.then_inc(f_pv, 1)

            def attn_pe(step, g, c, ahead):
                for kt in range(KT):
                    if ahead and kt == 0:
                        max_pe(step + 1, ahead[0], ahead[1], 0)
                        pe.wait_ge(f_qrow, (step + 1) * 48)
                    for half in range(2):
                        pe.wait_ge(f_p, step * (2 * KT) + (2 * kt + half - 1 + P0))
                        for h in range(2 * half, 2 * half + 2):
                            ins = pe.matmul(bank[:, h, :], k_stack[g % 2][0:KR + 3, h, kt * P:(kt + 1) * P],
                                            q_stack[0:KR + 3, q_cols(c, h, CK)], start=True, stop=True)
                        ins.then_inc(f_st, 1)
                    if ahead and kt:
                        max_pe(step + 1, ahead[0], ahead[1], kt)
                    if kt:
                        values(step, g, kt - 1)
                values(step, g, KT - 1)
                if ahead:
                    max_end(step + 1)
            pe.wait_ge(f_k_pad, 2)
            pe.wait_ge(f_kload[0], 16)
            pe.wait_ge(f_qload[0], 16)
            for item in range(HG * 4):
                max_pe(0, 0, 0, item)
            max_end(0)
            for g in range(NG):
                for c in range(1, NC):
                    pe.wait_ge(f_qload[c], 16 * (g + 1))
                with pe.Fori(0, NC - 1) as c:
                    attn_pe(c + g * NC, g, c, (g, c + 1))
                if g < NG - 1:
                    pe.wait_ge(f_kload[(g + 1) % 2], 16 * ((g + 1) // 2 + 1))
                    pe.wait_ge(f_qload[0], 16 * (g + 2))
                    attn_pe(g * NC + NC - 1, g, NC - 1, (g + 1, 0))
                else:
                    pe.wait_ge(f_qrow, NG * NC * 48)
                    attn_pe(g * NC + NC - 1, g, NC - 1, None)
            pe.wait_ge(f_attn, NG * NC + O0)
            for item in range(NG * NC):
                if item >= 8:
                    pe.wait_ge(f_inv, item - 7)
                pe.matmul(bn(item % 8), sum_pick[:], xa[:, item // NC, ck(item % NC)], start=True, stop=True).then_inc(f_sums, 1)
            pe.wait_ge(f_xa, NG * NC)
            for f in range(HID // P):
                for c in range(NC):
                    item = f * NC + c
                    if item >= 8:
                        pe.wait_ge(f_mlp, item - 7)
                    for i in range(2):
                        ins = pe.matmul(bn(item % 8), w1t[0:CH + i, i, f * P:(f + 1) * P], yw[0:CH + i, i, ck(c)],
                                        start=i == 0, stop=i == 1)
                    ins.then_inc(f_fc1, 1)
            pe.wait_ge(f_mlp, HID // P * NC)
            for c in range(NC):
                for i in range(2):
                    item = 2 * c + i
                    if item >= 4:
                        pe.wait_ge(f_o, item - 3)
                        pe.wait_ge(f_zz, NC + item - 3)
                    for f in range(9):
                        src = mlp[:, f, ck(c)] if f < 6 else xa[:, f - 6, ck(c)]
                        ins = pe.matmul(bn(item % 4, CH), w2t[:, f, i * CH:(i + 1) * CH], src, start=f == 0, stop=f == 8)
                    ins.then_inc(f_fc2, 1)
                    pe.matmul(bn(4 + item % 4, CH), width_mask[:, i * CH:(i + 1) * CH], selgate[:, ck(c)],
                              start=True, stop=True).then_inc(f_g, 1)
            pe.wait_ge(f_zz, NC + 2 * NC)
            for b in range(L // P):
                if b >= 8:
                    pe.wait_ge(s_fin, b - 7)
                for i in range(2):
                    ins = pe.transpose(bank[:, b % 8, i * CH:(i + 1) * CH], resid[:, i, b * P:(b + 1) * P], ident[0:CH, 0:CH])
                ins.then_inc(s_fin_t, 1)


_INS = ['x', 'L0_tok_emb', 'L0_tok_norm_w', 'L0_tok_in_proj_w', 'L0_tok_conv_w', 'L0_tok_conv_b', 'L0_tok_x_proj_w',
        'L0_tok_dt_proj_w', 'L0_tok_dt_proj_b', 'L0_tok_A_log', 'L0_tok_D', 'L0_tok_out_proj_w', 'L0_attn_in_w',
        'L0_attn_conv_w', 'L0_attn_conv_b', 'L0_attn_xproj_w', 'L0_attn_A_log', 'L0_attn_dt_bias', 'L0_attn_D',
        'L0_attn_out_w', 'L0_ffn_w_router', 'L0_ffn_gamma1', 'L0_ffn_beta1', 'L0_ffn_w1', 'L0_ffn_b1', 'L0_ffn_w2',
        'L0_ffn_b2']


def shape_constants():
    p = np.arange(P)
    return {
        "ident": np.eye(P, dtype=np.float32),
        "fold": (p[:, None] % 32 == np.arange(32)[None, :]).astype(np.float32),
        "width_mask": ((p[:, None] % 32 == 0) & (np.append(np.arange(C), 0)[None, :] < np.array(WIDTH)[p // 32][:, None])).astype(np.float32),
        "group_ones": (p[:, None] // 32 == p[None, :] // 32).astype(np.float32),
        "sum_pick": (p[:, None] == p[None, :] // 32 * 32 + HD).astype(np.float32),
        "search_off": ((p[:, None] % 32) << (SEARCH_BITS * np.arange(SEARCH_ROUNDS - 1, -1, -1))[None, :]).astype(np.int32),
    }


def kernel(**inputs):
    import concourse.bacc as bacc
    from concourse.bass_utils import run_bass_kernel_spmd

    nc = bacc.Bacc("TRN2", target_bir_lowering=False, num_devices=1)
    arrays, dram = {}, {}

    def give(name, a):
        a = np.ascontiguousarray(a)
        arrays[f"in_{name}"] = a
        return nc.dram_tensor(f"in_{name}", a.shape, mybir.dt.from_np(a.dtype), kind="ExternalInput").ap()

    for name in _INS:
        dram[name] = give(name, inputs[name])
    consts = {name: give("const_" + name, a) for name, a in shape_constants().items()}
    out = nc.dram_tensor("out_0", (1, L, C), F32, kind="ExternalOutput").ap()

    def per_layer(tok, att):
        return [dram["L0_tok_" + tok][0], dram["L0_tok_" + tok][1], dram["L0_attn_" + att]]

    build(nc, dram["x"], dram["L0_tok_emb"], dram["L0_tok_norm_w"], per_layer("in_proj_w", "in_w"),
          per_layer("conv_w", "conv_w"), per_layer("conv_b", "conv_b"), per_layer("x_proj_w", "xproj_w"),
          dram["L0_tok_dt_proj_w"], per_layer("dt_proj_b", "dt_bias"), per_layer("A_log", "A_log"), per_layer("D", "D"),
          per_layer("out_proj_w", "out_w"),
          {"w_router": dram["L0_ffn_w_router"], "gamma": dram["L0_ffn_gamma1"], "beta": dram["L0_ffn_beta1"],
           "w1": dram["L0_ffn_w1"], "b1": dram["L0_ffn_b1"], "w2": dram["L0_ffn_w2"], "b2": dram["L0_ffn_b2"]}, consts, out)
    r = run_bass_kernel_spmd(nc, [arrays], core_ids=[0])
    return r.results[0]["out_0"]
```

```python
from contextlib import ExitStack

import numpy as np
import concourse.bass as bass
from concourse import mybir

F32 = mybir.dt.float32
BF16 = mybir.dt.bfloat16
I32 = mybir.dt.int32
ALU = mybir.AluOpType
ACT = mybir.ActivationFunctionType
AX_X = mybir.AxisListType.X

P = 128
L = 2048
C = 192
V = 8000
CH = C // 2
DI = 2 * C
NJ = DI // P
CK = 512
NC = L // CK
TAPS = 4
TOK_N, TOK_R = 16, 12
ATT_N = 64
BLOCK_N = (TOK_N, TOK_N, ATT_N)
BLOCK_R = (TOK_R, TOK_R, 1)
STEP0 = (0, NC * TOK_N, 2 * NC * TOK_N, 2 * NC * TOK_N + NC * ATT_N)
NB = 3
A_LOG_MAX = 85.0
A_SLOTS, H_SLOTS, C_SLOTS = 2, 4, 4
LAG = 3

E = 4
WIDTH = [C // 2 ** (E - 1 - e) for e in range(E)]
CAP = L // 2
HEADS, HD = 12, 16
HID = 4 * C
F1 = HID + 3 * C
F2 = HID + C
HG = 4
NG = HEADS // HG
KT = L // P
PARTS = 3
PAIRS = ((0, 0), (0, 1), (1, 0), (1, 1), (0, 2), (2, 0))
KR = len(PAIRS) * HD
SEARCH_BITS, SEARCH_ROUNDS = 5, 6
MAX_RING = 3


def part_stack(t, part, group, lo, hi):
    return t[32 * part:32 * part + 32, group, lo:hi]


def build(nc, x, emb, norm_w, w_in, conv_w, conv_b, x_proj, dt_w, dt_b, a_log, d_skip, w_out, ffn, consts, out):
    with ExitStack() as ctx:
        def sb(name, shape, dt=F32):
            return ctx.enter_context(nc.sbuf_tensor(name, shape, dt))

        def sem(name):
            return ctx.enter_context(nc.semaphore(name))

        bank = ctx.enter_context(nc.psum_tensor("bank", [P, 8, CK], F32))
        resid = sb("resid", [CH, 2, L])
        region = sb("region", [P, 3 * (NJ * L) + NJ * (L + TAPS - 1)])
        scratch = sb("scratch", [P, (A_SLOTS + H_SLOTS) * NJ * CK])
        stack_all = sb("stack", [P, 4, L], BF16)
        stack = stack_all[0:3 * 32]
        c_row = sb("c_row", [P, C_SLOTS, CK])
        weights = sb("weights", [P, 32 * P // 2 + 2 * 2 * DI])
        sel = weights[0:3 * 32, 0:32 * P // 2].bitcast(BF16).rearrange("p (m k) -> p m k", k=P)
        w_in_sb = weights[0:CH, 32 * P // 2:].rearrange("p (i n) -> p i n", i=2)
        w_out_sb = sb("w_out_sb", [P, NB, NJ, C])
        w_x_sb = [sb(f"w_x{k}", [P, NJ, BLOCK_R[k] + 2 * BLOCK_N[k]]) for k in range(NB)]
        w_dt_sb = sb("w_dt_sb", [2 * TOK_N + TOK_R, 2, DI])
        norm_sb = sb("norm_sb", [CH, 2, 2])
        conv_w_sb = sb("conv_w_sb", [P, NB, NJ, TAPS])
        vec_sb = sb("vec_sb", [P, 3, NB, NJ])
        a_sb = [sb(f"a{k}", [P, NJ, BLOCK_N[k]]) for k in range(NB)]
        diag = sb("diag", [P, NJ, P])
        state = sb("state", [P, ATT_N, NJ])
        ident = sb("ident", [P, P])
        w1t = weights[0:CH + 1, 0:2 * F1].rearrange("p (i f) -> p i f", i=2)
        w2t = w_out_sb[:].rearrange("p k j c -> p (k j) c")
        w_router_sb = sb("w_router_sb", [CH, 2, E])
        ffn_rows = sb("ffn_rows", [8, CH])
        ffn_vec = sb("ffn_vec", [CH, 4, 2])
        small = c_row[:].rearrange("p s t -> p (s t)")
        width_mask = small[:, 0:C + 1]
        group_ones = small[:, 256:256 + P]
        sum_pick = small[:, 384:384 + 32]
        sum_spread = small[:, 1024:1024 + NC * P].rearrange("p (c m) -> p c m", c=NC)
        search_off = sb("search_off", [P, SEARCH_ROUNDS], I32)
        probs = sb("probs", [P, KT, E])
        psum_e = sb("psum_e", [P, KT])
        search = sb("search", [P, 8])
        search_i = sb("search_i", [P, 4], I32)
        max_part = sb("max_part", [P, HG * 4, 4])
        max_q = sb("max_q", [P, HG * 4])
        max_left = small[0:HG * 4, 512:512 + P]
        max_row = small[0:HG * 4, 640:640 + 3 * P // 2].bitcast(BF16).rearrange("p (a t) -> p a t", a=3)
        fold = sb("fold", [P, 32])
        ones = sb("ones", [P, P])
        idx_rows = sb("idx_rows", [L // P, P], I32)
        idx_f = sb("idx_f", [L // P, 2, P])
        idx = sb("idx", [P, L // P], I32)
        vec_rows = sb("vec_rows", [3 * NB * NJ, P])
        norm_rows = sb("norm_rows", [4, CH])

        RW = NJ * L
        xr = region[:, 0:NJ * (L + TAPS - 1)].rearrange("p (j t) -> p j t", j=NJ)
        dtu = xr[:, :, TAPS - 1:]
        r0 = NJ * (L + TAPS - 1)
        u = region[:, r0:r0 + RW].rearrange("p (j t) -> p j t", j=NJ)
        gate = region[:, r0 + RW:r0 + 2 * RW].rearrange("p (j t) -> p j t", j=NJ)
        delta = region[:, r0 + 2 * RW:r0 + 3 * RW].rearrange("p (j t) -> p j t", j=NJ)
        xn = region[0:CH, r0 + 2 * RW:r0 + 2 * RW + 2 * L].rearrange("p (i t) -> p i t", i=2)
        a_slot = scratch[:, 0:A_SLOTS * NJ * CK].rearrange("p (s j t) -> p s j t", s=A_SLOTS, j=NJ)
        h_slot = scratch[:, A_SLOTS * NJ * CK:].rearrange("p (s j t) -> p s j t", s=H_SLOTS, j=NJ)
        square = scratch[0:CH, 0:2 * L].rearrange("p (i t) -> p i t", i=2)
        inv = scratch[:, 2 * L:2 * L + CK]
        pick = diag[:].rearrange("p j m -> p (j m)").rearrange("p (c m) -> p c m", c=NC)
        soft = scratch[:, 0:NJ * L].rearrange("p (j t) -> p j t", j=NJ)
        parts = scratch[:, NJ * L:NJ * L + 3 * L // 2].bitcast(BF16).rearrange("p (s t) -> p s t", s=3)
        dt_low = c_row[:].rearrange("p s t -> p (s t)")
        left = dtu[:, 0, 0:CK]
        out_rows = region[:, 0:L // P * C].rearrange("p (b c) -> p b c", b=L // P)
        tok_rows = scratch[:, 0:L // P * C].rearrange("p (b c) -> p b c", b=L // P)

        xf = xn
        yw = region[0:CH + 1, 0:2 * L].rearrange("p (i t) -> p i t", i=2)
        selgate = region[:, 2 * L:3 * L]
        v_sb = region[:, 3 * L:6 * L].rearrange("p (b h d) -> p b h d", b=KT, h=HEADS)
        mlp = region[:, 3 * L:9 * L].rearrange("p (f t) -> p f t", f=HID // P)
        w1_raw = region[0:CH, 3 * L:3 * L + 14 * C].rearrange("p (b c) -> p b c", c=C)
        o = 3 * L + 14 * C
        w2_raw = region[0:CH, o:o + 4 * F2].rearrange("p (b f) -> p b f", b=4)
        o += 4 * F2
        w2_pad = region[0:CH, o:o + 2 * NG * P].rearrange("p (i g j d) -> p i g j d", i=2, g=NG, j=HG)
        xa = region[:, r0 + 2 * RW:r0 + 3 * RW].rearrange("p (g t) -> p g t", g=NG)
        k_stack = [region[:, 6 * L:8 * L].bitcast(BF16).rearrange("p (h t) -> p h t", h=HG),
                   scratch[:, 2 * L:4 * L].bitcast(BF16).rearrange("p (h t) -> p h t", h=HG)]
        q_stack = stack_all[:].rearrange("p a t -> p (a t)")

        def q_cols(c, head, n, at=0):
            return bass.ds(c * (HG * CK) + (head * CK + at), n)
        p_slot = scratch[:, 0:2 * L].rearrange("p (s h t) -> p s h t", s=4, h=2)
        prob_bc = scratch[:, 0:L]
        prob_wide = scratch[:, 3 * L:4 * L].rearrange("p (b e m) -> p b e m", b=KT, e=E)
        chosen = scratch[:, L:2 * L]
        flag = scratch[:, 2 * L:3 * L]
        prefix = scratch[:, 3 * L:4 * L]
        qk_part = scratch[0:CH, 0:3 * L].bitcast(BF16).rearrange("p (s a t) -> p s a t", s=2, a=PARTS)
        qk_left = scratch[0:CH, 3 * L:4 * L]
        inv_sb = scratch[:, 0:NG * CK].rearrange("p (g t) -> p g t", g=NG)
        P0 = 2
        O0 = 1
        b2_sum = ffn_vec[:, 2, :]
        PV0 = 2
        o_sb = scratch[0:CH, 0:4 * L].rearrange("p (i t) -> p i t", i=4)[:, 0:2]
        qk_dram = nc.dram_tensor("qk_parts", (2, HEADS, KR, L), BF16, kind="Internal").ap()

        s_const = sem("s_const")
        s_small = sem("s_small")
        s_vec = sem("s_vec")
        s_turned = sem("s_turned")
        s_vec_ok = sem("s_vec_ok")
        s_win = sem("s_win")
        s_idx = sem("s_idx")
        s_idx_ok = sem("s_idx_ok")
        s_rows = [sem(f"s_rows{c}") for c in range(NC)]
        s_rows_t = sem("s_rows_t")
        s_resid = sem("s_resid")
        s_sel = sem("s_sel")
        s_sum = sem("s_sum")
        s_centered = sem("s_centered")
        s_square = sem("s_square")
        s_var = sem("s_var")
        s_pick = sem("s_pick")
        s_spread = sem("s_spread")
        s_inv = sem("s_inv")
        s_rstd = sem("s_rstd")
        s_norm = sem("s_norm")
        s_xr_in = sem("s_xr_in")
        s_xr = sem("s_xr")
        s_gate_in = sem("s_gate_in")
        s_gate = sem("s_gate")
        s_tap = sem("s_tap")
        s_exp = sem("s_exp")
        s_ln = sem("s_ln")
        s_relu_exp = sem("s_relu_exp")
        s_delta = sem("s_delta")
        s_conv = sem("s_conv")
        s_u = sem("s_u")
        s_bc_rows = sem("s_bc_rows")
        s_split = sem("s_split")
        s_stack = sem("s_stack")
        s_dt_in = sem("s_dt_in")
        s_dt_sb = sem("s_dt_sb")
        s_dt_proj = sem("s_dt_proj")
        s_dt_x = sem("s_dt_x")
        s_dtu = sem("s_dtu")
        s_a_log = sem("s_a_log")
        s_a_mat = sem("s_a_mat")
        s_a_ready = sem("s_a_ready")
        s_diag = sem("s_diag")
        s_b_bc = sem("s_b_bc")
        s_c_bc = sem("s_c_bc")
        s_bu = [sem(f"s_bu{j}") for j in range(NJ)]
        s_c_row = sem("s_c_row")
        s_a = sem("s_a")
        s_scan = [sem(f"s_scan{j}") for j in range(NJ)]
        s_carry = sem("s_carry")
        s_hc = sem("s_hc")
        s_ysum = sem("s_ysum")
        s_y = sem("s_y")
        s_outproj = sem("s_outproj")
        s_v = sem("s_v")
        s_fin_t = sem("s_fin_t")
        s_fin = sem("s_fin")
        s_out = sem("s_out")
        s_pool = sem("s_pool")
        f_w_raw = sem("f_w_raw")
        f_ffn_c = sem("f_ffn_c")
        f_ffn_v = sem("f_ffn_v")
        f_w2_sum = sem("f_w2_sum")
        f_w_turn = sem("f_w_turn")
        f_w_turned = sem("f_w_turned")
        f_logit = sem("f_logit")
        f_probs = sem("f_probs")
        f_prob_t = sem("f_prob_t")
        f_prob_bc = sem("f_prob_bc")
        f_cand = sem("f_cand")
        f_flag = sem("f_flag")
        f_votes = sem("f_votes")
        f_chosen = sem("f_chosen")
        f_share = sem("f_share")
        f_yw = sem("f_yw")
        f_qk = sem("f_qk")
        f_qk_hi = sem("f_qk_hi")
        f_qk_left = sem("f_qk_left")
        f_qk_mid = sem("f_qk_mid")
        f_qk_lo = sem("f_qk_lo")
        f_qk_store = [sem(f"f_qk_store{tile}") for tile in range(4)]
        f_v = sem("f_v")
        f_v_sb = sem("f_v_sb")
        f_v_pad = sem("f_v_pad")
        f_k_pad = sem("f_k_pad")
        f_gate2 = sem("f_gate2")
        f_ffv = sem("f_ffv")
        f_ffp = sem("f_ffp")
        f_st = sem("f_st")
        f_p = sem("f_p")
        f_pv = sem("f_pv")
        f_attn = sem("f_attn")
        f_mscore = sem("f_mscore")
        f_mred = sem("f_mred")
        f_mx = sem("f_mx")
        f_mxt = sem("f_mxt")
        f_mxrow = sem("f_mxrow")
        f_qrow = sem("f_qrow")
        f_sums = sem("f_sums")
        f_inv = sem("f_inv")
        f_spread = sem("f_spread")
        f_xa = sem("f_xa")
        f_fc1 = sem("f_fc1")
        f_mlp = sem("f_mlp")
        f_fc2 = sem("f_fc2")
        f_o = sem("f_o")
        f_g = sem("f_g")
        f_zz = sem("f_zz")
        f_kload = [sem(f"f_kload{i}") for i in range(2)]
        f_qload = [sem(f"f_qload{c}") for c in range(NC)]

        def ck(c):
            return slice(c * CK, (c + 1) * CK)

        def bn(b, rows=P):
            return bank[0:rows, b, :]

        block = ctx.enter_context(nc.Block())

        @block.sync
        def _(sp):
            sp.dma_start(idx_rows[:], x.rearrange("a (b p) -> (a b) p", p=P)).then_inc(s_idx, 16)
            sp.dma_start(ident[:], consts["ident"]).then_inc(s_const, 16)
            sp.dma_start(fold[:], consts["fold"]).then_inc(s_const, 16)
            for i, name in enumerate(("gamma", "beta")):
                sp.dma_start(ffn_rows[2 * i:2 * i + 2, :], ffn[name].rearrange("(i p) -> i p", i=2)).then_inc(s_vec, 16)
            sp.dma_start(ffn_rows[4:8, :], ffn["b2"].rearrange("(i p) -> i p", i=4)).then_inc(s_vec, 16)
            for i in range(2):
                with nc.allow_non_contiguous_dma(reason="768 numbers"):
                    sp.dma_start(w_router_sb[:, i, :], ffn["w_router"][:, i * CH:(i + 1) * CH].rearrange("e p -> p e")).then_inc(f_ffn_c, 16)
            for k in range(2):
                sp.dma_start(norm_rows[2 * k:2 * k + 2, :], norm_w[k].rearrange("(i p) -> i p", i=2)).then_inc(s_vec, 16)
                sp.dma_start(w_dt_sb[2 * TOK_N:, k, :], dt_w[k]).then_inc(s_small, 16)
            for k in range(NB):
                sp.dma_start(conv_w_sb[:, k], conv_w[k].rearrange("(j p) a b -> p j (a b)", p=P)).then_inc(s_small, 16)
                for i, v in enumerate((conv_b, d_skip, dt_b)):
                    row = (i * NB + k) * NJ
                    sp.dma_start(vec_rows[row:row + NJ, :], v[k].rearrange("(j p) -> j p", p=P)).then_inc(s_vec, 16)
                sp.dma_start(a_sb[k][:], a_log[k].rearrange("(j p) n -> p j n", p=P)).then_inc(s_small, 16)
                w_x, low = x_proj[k].rearrange("(j p) n -> p j n", p=P), BLOCK_R[k] if k < 2 else 0
                bc = 2 * BLOCK_N[k]
                sp.dma_start(w_x_sb[k][:, :, 0:bc], w_x[:, :, low:low + bc]).then_inc(s_small, 16)
                if k < 2:
                    sp.dma_start(w_x_sb[k][:, :, bc:], w_x[:, :, 0:low]).then_inc(s_small, 16)
                else:
                    with nc.allow_non_contiguous_dma(reason="384 numbers"):
                        sp.dma_start(w_x_sb[k][:, :, bc:], w_x[:, :, bc:]).then_inc(s_small, 16)
                sp.dma_start(w_out_sb[:, k], w_out[k].rearrange("(j p) n -> p j n", p=P)).then_inc(s_small, 16)
            stacked = 0
            for k in range(NB):
                if k:
                    sp.wait_ge(s_gate_in, NJ * NC * k)
                sp.dma_start(w_in_sb[:], w_in[k].rearrange("(i p) n -> p i n", i=2)).then_inc(s_win, 16)
                sp.wait_ge(s_split, NC * (k + 1))
                for g in range(max(1, 2 * BLOCK_N[k] // 32)):
                    for part in range(3):
                        sp.dma_start(part_stack(stack, part, g, 0, L),
                                     parts[32 * g:32 * g + 32, part, :]).then_inc(s_stack, 16)
            sp.wait_ge(s_resid, NC * (NB + 1))
            for t, name in ((width_mask, "width_mask"), (group_ones, "group_ones"), (sum_pick, "sum_pick"), (sum_spread, "sum_spread"),
                            (search_off[:], "search_off")):
                sp.dma_start(t, consts[name]).then_inc(f_ffn_c, 16)
            sp.dma_start(w1t[CH:CH + 1, 1, :], ffn["b1"].rearrange("(a f) -> a f", a=1)).then_inc(f_ffn_c, 16)
            sp.dma_start(w1_raw, ffn["w1"].rearrange("(b p) c -> p b c", p=CH)).then_inc(f_w_raw, 16)
            sp.dma_start(w2_raw, ffn["w2"].rearrange("(b p) f -> p b f", p=CH)).then_inc(f_w_raw, 16)
            for tile in range(4):
                side, half = tile // 2, tile % 2
                sp.wait_ge(f_qk_lo, NC * (tile + 1))
                for j, pair in enumerate(PAIRS):
                    sp.dma_start(qk_dram[side, 6 * half:6 * half + 6, HD * j:HD * j + HD, :],
                                 qk_part[:, tile % 2, pair[side], :]).then_inc(f_qk_store[tile], 16)
            def put_maxima(step, c):
                sp.wait_ge(f_mxrow, step + 1)
                for a in range(3):
                    sp.dma_start(q_stack[KR + a:KR + a + 1, q_cols(c, 0, HG * CK)], max_row[:, a, :]).then_inc(f_qrow, 16)
            for g in range(NG):
                with sp.Fori(0, NC) as c:
                    put_maxima(c + g * NC, c)
            for c in range(NC):
                sp.wait_ge(s_fin, CK // P * (c + 1))
                sp.dma_start(out[0, ck(c), :].rearrange("(b p) c -> p b c", p=P),
                             out_rows[:, c * (CK // P):(c + 1) * (CK // P), :]).then_inc(s_out, 16)
            sp.wait_ge(s_out, 16 * NC)

        SMALL_DMAS = 16 * (2 + NB * 5)
        STACKED = [0]
        for k in range(NB):
            STACKED.append(STACKED[-1] + 16 * 3 * max(1, 2 * BLOCK_N[k] // 32))

        def steps(eng, n, emit):
            emit(0, 0, "first")
            for lo, hi in [(4, min(n - 4, 32))] + ([(32, n - 4)] if n > 32 else []):
                with eng.Fori(lo // 4, hi // 4) as turn:
                    emit(turn * 4, lo // 32, "")
            emit(n - 4, (n - 4) // 32, "last")

        @block.gpsimd
        def _(pool):
            pool.wait_ge(s_idx_ok, 2)
            for b in range(L // P):
                pool.indirect_dma_start(tok_rows[:, b, :], None, emb,
                                        bass.IndirectOffsetOnAxis(idx[:, b:b + 1], 0)).then_inc(s_rows[b * P // CK], 16)
            for k in range(NB):
                n = BLOCK_N[k]
                for c in range(NC):
                    pool.wait_ge(s_exp, NC * k + c + 1)
                    pool.tensor_tensor(delta[:, :, ck(c)], delta[:, :, ck(c)], soft[:, :, ck(c)], ALU.add).then_inc(s_relu_exp, 1)
                for c in range(NC):
                    pool.wait_ge(s_delta, NC * k + c + 1)
                    pool.tensor_tensor(dtu[:, :, ck(c)], delta[:, :, ck(c)], u[:, :, ck(c)], ALU.mult).then_inc(s_dtu, 1)
                for c in range(NC):
                    base = STEP0[k] + c * n
                    with pool.Fori(0, n // 4) as turn:
                        s = turn * 4
                        for i in range(4):
                            pool.wait_ge(s_carry, s + (base + i + 1))
                            pool.wait_ge(s_c_row, s + (base + i + 1))
                            cr = c_row[:, i, :].unsqueeze(1).broadcast_to([P, NJ, CK])
                            pool.tensor_tensor(h_slot[:, i], h_slot[:, i], cr, ALU.mult).then_inc(s_hc, 1)
            pool.wait_ge(f_w_turned, 32)
            pool.memset(v_sb, 0.0).then_inc(f_v_pad, 1)
            pool.wait_ge(f_v_pad, 1)
            pool.memset(v_sb[:, :, :, HD:HD + 1], 1.0).then_inc(f_v_pad, 1)
            for tile in range(4):
                for c in range(NC):
                    pool.wait_ge(f_qk_mid, NC * tile + c + 1)
                    pool.tensor_tensor(qk_part[:, tile % 2, 2, ck(c)], qk_left[:, ck(c)], qk_part[:, tile % 2, 1, ck(c)],
                                       ALU.subtract).then_inc(f_qk_lo, 1)
            for tile in range(4):
                pool.wait_ge(f_qk_store[tile], 16 * len(PAIRS))

            def load_k(g):
                pool.dma_start(k_stack[g % 2][0:KR], qk_dram[1, HG * g:HG * g + HG].rearrange("h r t -> r h t")).then_inc(f_kload[g % 2], 16)

            def load_q(g, c):
                pool.dma_start(q_stack[0:KR, q_cols(c, 0, HG * CK)].rearrange("r (h t) -> r h t", h=HG),
                               qk_dram[0, HG * g:HG * g + HG, :, ck(c)].rearrange("h r t -> r h t")).then_inc(f_qload[c], 16)
            load_k(0)
            for c in range(NC):
                load_q(0, c)
            load_k(1)
            for i in range(2):
                pool.memset(k_stack[i][KR:KR + 3], 1.0).then_inc(f_k_pad, 1)
            for g in range(NG - 1):
                for c in range(NC):
                    pool.wait_ge(f_p, 2 * KT * (NC * g + c + 1) + P0)
                    load_q(g + 1, c)
                if g + 2 < NG:
                    load_k(g + 2)

        @block.scalar
        def _(act):
            def norm_act(r):
                src = xn if r < 4 else yw[0:CH]
                for c in range(NC):
                    if r < 2:
                        act.wait_ge(s_resid, NC * r + (c + 1 if r else NC))
                        src = resid
                    else:
                        act.wait_ge(s_centered, NC * (r - 2) + c + 1)
                    act.activation(square[:, :, ck(c)], src[:, :, ck(c)], ACT.Square).then_inc(s_square, 1)
                act.wait_ge(s_inv, r + 1)
                act.activation(inv, inv, ACT.Sqrt).then_inc(s_rstd, 1)

            for k in range(NB):
                n = BLOCK_N[k]
                norm_act(k)
                def take_xr(c):
                    for m in range(NJ):
                        act.wait_ge(s_xr_in, NJ * (NC * k + c) + m + 1)
                        act.activation(dtu[:, m, ck(c)], bn((NJ * c + m) % 3), ACT.Copy).then_inc(s_xr, 1)

                def silu_u(c):
                    for j in range(NJ):
                        act.wait_ge(s_conv, NJ * (NC * k + c) + j + 1)
                        act.activation(u[:, j, ck(c)], u[:, j, ck(c)], ACT.Silu, bias=vec_sb[:, 0, k, j:j + 1]).then_inc(s_u, 1)

                take_xr(0)
                take_xr(1)
                take_xr(2)
                silu_u(0)
                take_xr(3)
                silu_u(1)
                for c in range(NC):
                    if k < 2:
                        act.wait_ge(s_bc_rows, NC * k + c + 1)
                        act.activation(dt_low[2 * n:2 * n + TOK_R, ck(c)], bank[2 * n:2 * n + TOK_R, 4 + c % 2, :], ACT.Copy).then_inc(s_dt_sb, 1)
                    else:
                        act.wait_ge(s_dt_in, c + 1)
                        act.activation(dt_low[0:1, ck(c)], bn(3, 1), ACT.Copy).then_inc(s_dt_sb, 1)
                    for m in range(NJ):
                        act.wait_ge(s_gate_in, NJ * (NC * k + c) + m + 1)
                        act.activation(gate[:, m, ck(c)], bn((NJ * c + m) % 3), ACT.Silu).then_inc(s_gate, 1)
                    if c < 2:
                        silu_u(c + 2)
                    for j in range(NJ):
                        item = NJ * c + j
                        act.wait_ge(s_dt_proj, NJ * NC * k + item + 1)
                        act.activation(delta[:, j, ck(c)], bn(6 + item % 2), ACT.Relu, bias=vec_sb[:, 2, k, j:j + 1])
                        act.activation(soft[:, j, ck(c)], bn(6 + item % 2), ACT.Abs, bias=vec_sb[:, 2, k, j:j + 1]).then_inc(s_dt_x, 1)
                act.wait_ge(s_a_log, k + 1)
                act.activation(a_sb[k][:], a_sb[k][:], ACT.Exp).then_inc(s_a_mat, 1)
                act.wait_ge(s_dt_x, NJ * NC * (k + 1))
                for c in range(NC):
                    act.activation(soft[:, :, ck(c)], soft[:, :, ck(c)], ACT.Exp, scale=-1.0).then_inc(s_exp, 1)
                act.wait_ge(s_exp, NC * (k + 1))
                act.wait_ge(s_split, NC * (k + 1))
                for c in range(NC):
                    act.activation(dtu[:, :, ck(c)], soft[:, :, ck(c)], ACT.Ln, bias=1.0).then_inc(s_ln, 1)
                act.wait_ge(s_a_ready, k + 1)
                act.wait_ge(s_dtu, NC * (k + 1))
                for c in range(NC):
                    base = STEP0[k] + c * n

                    def carry(s, v):
                        act.activation(state[:, bass.ds(s + v, 1), :].rearrange("p a b -> p (a b)"),
                                       h_slot[:, v % H_SLOTS, :, CK - 1], ACT.Copy).then_inc(s_carry, 1)

                    def scan_act(s, g, end):
                        for i in range(4):
                            if end != "first" or i >= A_SLOTS or c:
                                act.wait_ge(s_scan[NJ - 1], s + (base + i + 1 - A_SLOTS))
                                if end == "first" and i < A_SLOTS:
                                    carry(n - H_SLOTS, H_SLOTS + i - A_SLOTS)
                                else:
                                    carry(s, i - A_SLOTS)
                            for j in range(NJ):
                                ins = act.activation(a_slot[:, i % 2, j, :], delta[:, j, ck(c)], ACT.Exp,
                                                     scale=a_sb[k][:, j, bass.ds(s + i, 1)])
                            ins.then_inc(s_a, 1)
                            act.wait_ge(s_c_bc, s + (base + i + 1))
                            if end != "first" or k + c:
                                act.wait_ge(s_hc, s + (base + i + 1 - C_SLOTS))
                            act.activation(c_row[:, i, :], bn(4), ACT.Copy).then_inc(s_c_row, 1)
                    steps(act, n, scan_act)
                for v in range(A_SLOTS):
                    act.wait_ge(s_scan[NJ - 1], base + n - A_SLOTS + v + 1)
                    carry(n - H_SLOTS, H_SLOTS - A_SLOTS + v)
            norm_act(3)
            norm_act(4)
            act.wait_ge(f_logit, 2)
            act.activation(probs[:], probs[:], ACT.Exp).then_inc(f_probs, 1)
            for c in range(NC):
                act.wait_ge(f_prob_t, c + 1)
                act.activation(prob_bc[:, ck(c)], bn(4 + c), ACT.Copy).then_inc(f_prob_bc, 1)
            for tile in range(4):
                scale = HD ** -0.5 if tile < 2 else 1.0
                for c in range(NC):
                    item = tile * NC + c
                    act.wait_ge(f_qk, item + 1)
                    if tile >= 2 and c == 0:
                        act.wait_ge(f_qk_store[tile - 2], 16 * len(PAIRS))
                    act.activation(qk_part[:, tile % 2, 0, ck(c)], bn(item % 8, CH), ACT.Copy, scale=scale).then_inc(f_qk_hi, 1)
                    act.wait_ge(f_qk_left, item + 1)
                    act.activation(qk_part[:, tile % 2, 1, ck(c)], qk_left[:, ck(c)], ACT.Copy).then_inc(f_qk_mid, 1)
            act.wait_ge(f_v_pad, 2)
            for b in range(KT):
                act.wait_ge(f_v, b + 1)
                act.activation(v_sb[:, b, :, 0:HD], bank[:, b % 8, 0:C].rearrange("p (h d) -> p h d", h=HEADS),
                               ACT.Copy).then_inc(f_v_sb, 1)
            def attn_act(step):
                for kt in range(KT):
                    for half in range(2):
                        act.wait_ge(f_st, (step * (2 * KT)) + (2 * kt + half + 1))
                        act.wait_ge(f_pv, step * KT + (kt - 1 + PV0))
                        act.activation(p_slot[:, 2 * (kt % 2) + half], bank[:, 2 * half:2 * half + 2, :],
                                       ACT.Exp).then_inc(f_p, 1)
            for g in range(NG):
                with act.Fori(0, NC) as c:
                    attn_act(c + g * NC)
            for f in range(HID // P):
                for c in range(NC):
                    item = f * NC + c
                    act.wait_ge(f_fc1, item + 1)
                    act.activation(mlp[:, f, ck(c)], bn(item % 4), ACT.Gelu).then_inc(f_mlp, 1)
            for c in range(NC):
                for i in range(2):
                    item = 2 * c + i
                    act.wait_ge(f_fc2, item + 1)
                    act.activation(o_sb[:, i, ck(c)], bn(item % 4, CH), ACT.Identity, bias=b2_sum[:, i:i + 1]).then_inc(f_o, 1)

        @block.vector
        def _(dve):
            chain = [0]

            def link(ins):
                chain[0] += 1
                ins.then_inc(s_v, 1)
                dve.wait_ge(s_v, chain[0])

            dve.wait_ge(s_idx, 16)
            link(dve.tensor_scalar(idx_f[:, 0, :], idx_rows[:], 0.0, float(V), ALU.is_lt, ALU.mult))
            link(dve.tensor_tensor(idx_f[:, 1, :], idx_rows[:], idx_f[:, 0, :], ALU.add))
            dve.tensor_scalar(idx_f[:, 0, :], idx_f[:, 1, :], 0.0, float(V - 1), ALU.max, ALU.min).then_inc(s_idx_ok, 1)
            dve.wait_ge(s_turned, 1)
            dve.tensor_copy(idx[:], bank[:, 5, 0:L // P]).then_inc(s_idx_ok, 1)
            dve.wait_ge(s_turned, 2)
            dve.tensor_copy(vec_sb[:].rearrange("p a b c -> p (a b c)"), bank[:, 7, 0:3 * NB * NJ]).then_inc(s_vec_ok, 1)
            dve.tensor_copy(norm_sb[:].rearrange("p a b -> p (a b)"), bank[0:CH, 6, 0:4]).then_inc(s_vec_ok, 1)
            dve.tensor_copy(ffn_vec[:].rearrange("p a b -> p (a b)"), bank[0:CH, 6, 8:16]).then_inc(s_vec_ok, 1)
            dve.memset(ones[:], 1.0).then_inc(s_sel, 1)
            dve.memset(xr[:, :, 0:TAPS - 1], 0.0)
            dve.wait_ge(s_const, 32)
            dve.tensor_copy(sel[:], fold[0:96, :].unsqueeze(2).broadcast_to([96, 32, P])).then_inc(s_sel, 1)
            for c in range(NC):
                dve.wait_ge(s_rows_t, c + 1)
                dve.tensor_copy(resid[:, :, ck(c)], bank[0:CH, 2 * c:2 * c + 2, :]).then_inc(s_resid, 1)
            dve.wait_ge(s_small, SMALL_DMAS)
            for k in range(NB):
                dve.tensor_scalar(a_sb[k][:], a_sb[k][:], A_LOG_MAX, None, ALU.min).then_inc(s_a_log, 1)

            def norm_dve(r, eps, w, src=resid, xn=xn):
                if r >= 2:
                    for c in range(NC):
                        dve.wait_ge(s_sum, NC * (r - 2) + c + 1)
                        mean = bank[0:CH, c:c + 1, :].broadcast_to([CH, 2, CK])
                        dve.scalar_tensor_tensor(xn[:, :, ck(c)], mean, -1.0 / C, src[:, :, ck(c)],
                                                 ALU.mult, ALU.add).then_inc(s_centered, 1)
                for c in range(NC):
                    ins = dve.tensor_copy(pick[:, c, :], ident[:, 32 * c:32 * c + 1].broadcast_to([P, CH]))
                ins.then_inc(s_pick, 1)
                dve.wait_ge(s_var, r + 1)
                link(dve.tensor_scalar(inv, bn(4), 1.0 / C, eps, ALU.mult, ALU.add))
                dve.reciprocal(inv, inv).then_inc(s_inv, 1)
                for c in range(NC):
                    dve.wait_ge(s_spread, NC * r + c + 1)
                    for i in range(2):
                        if w is not None:
                            ins = dve.scalar_tensor_tensor(xn[:, i, ck(c)], resid[:, i, ck(c)], w[:, i:i + 1],
                                                           bn(c, CH), ALU.mult, ALU.mult)
                        else:
                            ins = dve.tensor_tensor(xn[:, i, ck(c)], xn[:, i, ck(c)], bn(c, CH), ALU.mult)
                    ins.then_inc(s_norm, 1)

            for k in range(NB):
                n, R = BLOCK_N[k], BLOCK_R[k]
                norm_dve(k, 1e-5, norm_sb[:, k] if k < 2 else None)
                G = min(P, 2 * n)

                def convolve(c):
                    for j in range(NJ):
                        dve.wait_ge(s_xr, NJ * (NC * k + c) + j + 1)
                    for t in range(TAPS):
                        for j in range(NJ):
                            src, w = xr[:, j, c * CK + t:c * CK + t + CK], conv_w_sb[:, k, j, t:t + 1]
                            if t == 0:
                                ins = dve.tensor_scalar(u[:, j, ck(c)], src, w, None, ALU.mult)
                            else:
                                dve.wait_ge(s_tap, NJ * ((TAPS - 1) * (NC * k + c) + t - 1) + j + 1)
                                ins = dve.scalar_tensor_tensor(u[:, j, ck(c)], src, w, u[:, j, ck(c)], ALU.mult, ALU.add)
                            ins.then_inc(s_conv if t == TAPS - 1 else s_tap, 1)

                def split(c):
                    dve.wait_ge(s_bc_rows, NC * k + c + 1)
                    rows = bn(4 + c % 2, G)
                    link(dve.tensor_copy(parts[0:G, 0, ck(c)], rows))
                    link(dve.tensor_tensor(left[0:G, :], rows, parts[0:G, 0, ck(c)], ALU.subtract))
                    link(dve.tensor_copy(parts[0:G, 1, ck(c)], left[0:G, :]))
                    dve.tensor_tensor(parts[0:G, 2, ck(c)], left[0:G, :], parts[0:G, 1, ck(c)], ALU.subtract).then_inc(s_split, 1)

                convolve(0)
                convolve(1)
                convolve(2)
                split(0)
                convolve(3)
                split(1)
                split(2)
                split(3)
                dve.wait_ge(s_spread, NC * (k + 1))
                for j in range(NJ):
                    dve.tensor_scalar(diag[:, j, :], ident[:], vec_sb[:, 1, k, j:j + 1], None, ALU.mult).then_inc(s_diag, 1)
                dve.memset(state[:], 0.0)
                dve.wait_ge(s_a_mat, k + 1)
                dve.tensor_scalar(a_sb[k][:], a_sb[k][:], -1.0, None, ALU.mult).then_inc(s_a_ready, 1)
                for c in range(NC):
                    dve.wait_ge(s_relu_exp, NC * k + c + 1)
                    dve.wait_ge(s_ln, NC * k + c + 1)
                    v, w = soft[:, :, ck(c)], dtu[:, :, ck(c)]
                    link(dve.tensor_scalar(v, v, 1.0, 1.0, ALU.add, ALU.subtract))
                    link(dve.tensor_tensor(w, w, v, ALU.subtract))
                    dve.tensor_tensor(delta[:, :, ck(c)], delta[:, :, ck(c)], w, ALU.add).then_inc(s_delta, 1)
                dve.wait_ge(s_dtu, NC * (k + 1))
                def take_y(c):
                    dve.wait_ge(s_ysum, STEP0[k] + (c + 1) * n)
                    dve.tensor_tensor(gate[:, :, ck(c)], bank[:, 0:3, :], gate[:, :, ck(c)], ALU.mult).then_inc(s_y, 1)

                for c in range(NC):
                    base = STEP0[k] + c * n

                    def b_times(s, v, j, started=True):
                        if j == 0:
                            dve.wait_ge(s_b_bc, s + (base + v + 1))
                        if started:
                            dve.wait_ge(s_scan[j], s + (base + v))
                        dve.tensor_tensor(bank[:, 5 + j, :], dtu[:, j, ck(c)], bn(3), ALU.mult).then_inc(s_bu[j], 1)

                    def scan(s, i, j):
                        dve.wait_ge(s_bu[j], s + (base + i + 1))
                        dve.tensor_tensor_scan(h_slot[:, i, j, :], a_slot[:, i % 2, j, :], bank[:, 5 + j, :],
                                               state[:, bass.ds(s + i, 1), j:j + 1].rearrange("p a b -> p (a b)"),
                                               ALU.mult, ALU.add).then_inc(s_scan[j], 1)

                    def scan_dve(s, g, end):
                        for i in range(4):
                            if c and end == "first" and i == LAG:
                                take_y(c - 1)
                            dve.wait_ge(s_a, s + (base + i + 1))
                            if end != "first" or k + c:
                                dve.wait_ge(s_ysum, s + (base + i + 1 - H_SLOTS))
                            scan(s, i, 0)
                            b_times(s, i, 2, end != "first" or i or k + c)
                            scan(s, i, 1)
                            if end != "last" or i < 3:
                                b_times(s, i + 1, 0)
                            scan(s, i, 2)
                            if end != "last" or i < 3:
                                b_times(s, i + 1, 1)
                    b_times(0, 0, 0, k + c)
                    b_times(0, 0, 1, k + c)
                    steps(dve, n, scan_dve)
                take_y(NC - 1)
                for c in range(NC):
                    dve.wait_ge(s_outproj, NC * k + c + 1)
                    dve.tensor_tensor(resid[:, :, ck(c)], resid[:, :, ck(c)], bank[0:CH, 2 * c:2 * c + 2, :],
                                      ALU.add).then_inc(s_resid, 1)
            norm_dve(3, 1e-5, None)
            for c in range(NC):
                dve.wait_ge(s_norm, NC * 3 + c + 1)
                dve.tensor_tensor(resid[:, :, ck(c)], resid[:, :, ck(c)], xf[:, :, ck(c)], ALU.add).then_inc(f_zz, 1)
            norm_dve(4, 1e-6, None, src=xf, xn=yw[0:CH])
            dve.wait_ge(s_norm, NC * 5)
            for i in range(2):
                ins = dve.tensor_scalar(yw[0:CH, i, :], yw[0:CH, i, :], ffn_vec[:, 0, i:i + 1], ffn_vec[:, 1, i:i + 1],
                                        ALU.mult, ALU.add)
            link(ins)
            dve.tensor_tensor(b2_sum, b2_sum, ffn_vec[:, 3, :], ALU.add).then_inc(f_ffv, 1)
            dve.wait_ge(f_w_raw, 32)
            dve.memset(w2_pad, 0.0).then_inc(f_pv, PV0)
            dve.memset(max_part[:], 0.0).then_inc(f_p, P0)
            dve.memset(max_q[:], 0.0).then_inc(f_attn, O0)
            link(dve.tensor_tensor(w2_raw[:, 0:2, :], w2_raw[:, 0:2, :], w2_raw[:, 2:4, :], ALU.add))
            for i in range(2):
                ins = dve.tensor_copy(w2_pad[:, i, :, :, 0:HD],
                                      w2_raw[:, i, HID:F2].rearrange("p (g j d) -> p g j d", g=NG, j=HG))
            ins.then_inc(f_w2_sum, 1)
            for b in range(14):
                dve.wait_ge(f_w_turn, b + 1)
                dve.tensor_copy(w1t[0:CH, :, b * CH:(b + 1) * CH],
                                bank[0:CH, b % 8, 0:2 * CH].rearrange("p (i f) -> p i f", i=2)).then_inc(f_w_turned, 1)
            for b in range(18):
                f, i = b // 2, b % 2
                dve.wait_ge(f_w_turn, 14 + b + 1)
                dve.tensor_copy(w2t[:, f, i * CH:(i + 1) * CH], bank[:, (14 + b) % 8, 0:CH]).then_inc(f_w_turned, 1)
            dve.wait_ge(f_logit, 1)
            lg = bank[:, 0, 0:KT * E].rearrange("p (b e) -> p b e", e=E)
            link(dve.tensor_reduce(psum_e[:], lg, AX_X, ALU.max))
            dve.tensor_tensor(probs[:], lg, psum_e[:].unsqueeze(2).broadcast_to([P, KT, E]), ALU.subtract).then_inc(f_logit, 1)
            dve.wait_ge(f_probs, 1)
            link(dve.tensor_reduce(psum_e[:], probs[:], AX_X, ALU.add))
            link(dve.reciprocal(psum_e[:], psum_e[:]))
            dve.tensor_tensor(prob_wide, probs[:].unsqueeze(3).broadcast_to([P, KT, E, 32]),
                              psum_e[:].unsqueeze(2).unsqueeze(3).broadcast_to([P, KT, E, 32]), ALU.mult).then_inc(f_probs, 1)
            dve.wait_ge(f_ffn_c, 16 * 8)
            link(dve.memset(search_i[:, 0:1], 0))
            dve.wait_ge(f_prob_bc, NC)
            for r in range(SEARCH_ROUNDS):
                link(dve.tensor_tensor(search_i[:, 1:2], search_i[:, 0:1], search_off[:, r:r + 1], ALU.bitwise_or))
                link(dve.tensor_scalar(flag, prob_bc, search_i[:, 1:2].bitcast(F32), 0.0, ALU.is_ge, ALU.add,
                                       accum_out=search[:, 0:1]))
                dve.tensor_scalar(search[:, 1:2], search[:, 0:1], float(CAP), None, ALU.is_ge).then_inc(f_flag, 1)
                dve.wait_ge(f_votes, r + 1)
                link(dve.tensor_scalar(search_i[:, 2:3], bank[:, 0, r:r + 1], 1.0,
                                       float(2 ** (SEARCH_BITS * (SEARCH_ROUNDS - 1 - r))), ALU.subtract, ALU.mult))
                link(dve.tensor_tensor(search_i[:, 0:1], search_i[:, 0:1], search_i[:, 2:3], ALU.bitwise_or))
            least = search_i[:, 0:1].bitcast(F32)
            link(dve.tensor_scalar(chosen, prob_bc, least, 0.0, ALU.is_gt, ALU.add, accum_out=search[:, 2:3]))
            link(dve.tensor_scalar(search[:, 3:4], search[:, 2:3], -1.0, float(CAP), ALU.mult, ALU.add))
            link(dve.tensor_scalar(flag, prob_bc, least, None, ALU.is_equal))
            link(dve.tensor_tensor_scan(prefix, flag, flag, 0.0, ALU.add, ALU.max))
            link(dve.scalar_tensor_tensor(flag, prefix, search[:, 3:4], flag, ALU.is_le, ALU.mult))
            link(dve.tensor_tensor(chosen, chosen, flag, ALU.add))
            dve.tensor_tensor(selgate, chosen, prob_bc, ALU.mult).then_inc(f_chosen, 1)
            for c in range(NC):
                dve.wait_ge(f_share, c + 1)
                dve.tensor_tensor(yw[0:CH, :, ck(c)], yw[0:CH, :, ck(c)], bank[0:CH, 2 * c:2 * c + 2, :], ALU.mult)
                dve.tensor_copy(yw[CH:CH + 1, 1, ck(c)], bank[CH:CH + 1, 2 * c + 1, :]).then_inc(f_yw, 1)
            for tile in range(4):
                scale = HD ** -0.5 if tile < 2 else 1.0
                for c in range(NC):
                    item = tile * NC + c
                    dve.wait_ge(f_qk_hi, item + 1)
                    if tile:
                        dve.wait_ge(f_qk_lo, item - NC + 1)
                    dve.scalar_tensor_tensor(qk_left[:, ck(c)], bn(item % 8, CH), scale, qk_part[:, tile % 2, 0, ck(c)],
                                             ALU.mult, ALU.subtract).then_inc(f_qk_left, 1)
            def max_dve(step):
                for m in range(HG * 4 * 4):
                    dve.wait_ge(f_mscore, step * (HG * 4 * 4) + (m + 1))
                    dve.tensor_reduce(max_part[:, m // 4, m % 4:m % 4 + 1], bank[:, 5 + m % MAX_RING, :], AX_X, ALU.max).then_inc(f_mred, 1)
                dve.wait_ge(f_mred, (step + 1) * (HG * 4 * 4))
                dve.tensor_reduce(max_q[:], max_part[:], AX_X, ALU.max).then_inc(f_mx, 1)
                dve.wait_ge(f_mxt, step + 1)
                dve.wait_ge(f_qrow, step * 48)
                turned = bank[0:HG * 4, 7, 0:P]
                dve.tensor_scalar(max_row[:, 0, :], turned, -1.0, None, ALU.mult).then_inc(f_ffv, 1)
                dve.wait_ge(f_ffv, step * 3 + 2)
                dve.scalar_tensor_tensor(max_left, turned, -1.0, max_row[:, 0, :], ALU.mult, ALU.subtract).then_inc(f_ffv, 1)
                dve.wait_ge(f_ffv, step * 3 + 3)
                dve.tensor_copy(max_row[:, 1, :], max_left).then_inc(f_ffv, 1)
                dve.wait_ge(f_ffv, step * 3 + 4)
                dve.tensor_tensor(max_row[:, 2, :], max_left, max_row[:, 1, :], ALU.subtract).then_inc(f_mxrow, 1)

            def take_o(step, g, c):
                dve.wait_ge(f_pv, (step + 1) * KT + PV0)
                dve.tensor_scalar(xa[:, g, bass.ds(c * CK, CK)], bank[:, 4, :], 1.0, None, ALU.mult).then_inc(f_attn, 1)
            max_dve(0)
            for g in range(NG):
                with dve.Fori(0, NC - 1) as c:
                    max_dve(c + (g * NC + 1))
                    take_o(c + g * NC, g, c)
                if g < NG - 1:
                    max_dve((g + 1) * NC)
                take_o(g * NC + NC - 1, g, NC - 1)
            for g in range(NG):
                dve.wait_ge(f_sums, g + 1)
                dve.reciprocal(inv_sb[:, g, :], bn(4)).then_inc(f_inv, 1)
                for c in range(NC):
                    item = g * NC + c
                    dve.wait_ge(f_spread, item + 1)
                    dve.tensor_tensor(xa[:, g, ck(c)], xa[:, g, ck(c)], bn(5 + item % 3), ALU.mult).then_inc(f_xa, 1)

            def take_rows(c):
                for b in range(c * (CK // P), (c + 1) * (CK // P)):
                    dve.wait_ge(s_fin_t, b + 1)
                    dve.tensor_copy(out_rows[:, b, :], bank[:, 6 + b % 2, 0:C]).then_inc(s_fin, 1)
            for c in range(NC):
                for i in range(2):
                    item = 2 * c + i
                    dve.wait_ge(f_g, item + 1)
                    dve.wait_ge(f_o, item + 1)
                    link(dve.tensor_tensor(o_sb[:, i, ck(c)], o_sb[:, i, ck(c)], bn(4 + item % 2, CH), ALU.mult))
                    dve.tensor_tensor(resid[:, i, ck(c)], resid[:, i, ck(c)], o_sb[:, i, ck(c)], ALU.add).then_inc(f_zz, 1)
                    if c and i == 0:
                        take_rows(c - 1)
            take_rows(NC - 1)

        @block.tensor
        def _(pe):
            pe.wait_ge(s_const, 32)
            pe.wait_ge(s_idx_ok, 1)
            pe.transpose(bank[:, 5, 0:L // P], idx_f[:, 0, :], ident[0:L // P, 0:L // P]).then_inc(s_turned, 1)
            pe.wait_ge(s_vec, 16 * (5 + 3 * NB))
            pe.transpose(bank[0:CH, 6, 0:4], norm_rows[:], ident[0:4, 0:4])
            pe.transpose(bank[0:CH, 6, 8:16], ffn_rows[:], ident[0:8, 0:8])
            pe.transpose(bank[:, 7, 0:3 * NB * NJ], vec_rows[:], ident[0:3 * NB * NJ, 0:3 * NB * NJ]).then_inc(s_turned, 1)
            pe.wait_ge(s_vec_ok, 3)
            for c in range(NC):
                for i in range(2):
                    for t in range(CK // P):
                        b = c * (CK // P) + t
                        if i == 0 and t == 0:
                            pe.wait_ge(s_rows[c], 16 * (CK // P))
                        ins = pe.transpose(bank[0:CH, 2 * c + i, t * P:(t + 1) * P], tok_rows[:, b, i * CH:(i + 1) * CH], ident[:])
                ins.then_inc(s_rows_t, 1)
            pe.wait_ge(s_sel, 2)

            def norm_pe(r, resid=resid):
                if r >= 2:
                    if r < 4:
                        pe.wait_ge(s_resid, NC * (r + 1))
                    else:
                        pe.wait_ge(s_norm, NC * 4)
                    for c in range(NC):
                        for i in range(2):
                            ins = pe.matmul(bn(c, CH), ones[0:CH, 0:CH], resid[:, i, ck(c)], start=i == 0, stop=i == 1)
                        ins.then_inc(s_sum, 1)
                else:
                    pe.wait_ge(s_resid, NC * (r + 1))
                pe.wait_ge(s_square, NC * (r + 1))
                for i in range(2):
                    for c in range(NC):
                        ins = pe.matmul(bank[32 * c:32 * c + 32, 4, :], ones[0:CH, 0:32], square[:, i, ck(c)],
                                        start=i == 0, stop=i == 1, tile_position=(0, 32 * c), skip_group_check=True)
                ins.then_inc(s_var, 1)
                pe.wait_ge(s_rstd, r + 1)
                pe.wait_ge(s_pick, r + 1)
                for c in range(NC):
                    pe.matmul(bn(c, CH), pick[:, c, :], inv, start=True, stop=True).then_inc(s_spread, 1)

            for k in range(NB):
                n, R = BLOCK_N[k], BLOCK_R[k]
                norm_pe(k)
                pe.wait_ge(s_win, 16 * (k + 1))
                G = min(P, 2 * n)
                M = G + (R if k < 2 else 0)

                def project(c, first, done, taken, count):
                    for m in range(NJ):
                        item = NJ * c + m
                        if count + item >= 3:
                            pe.wait_ge(taken, count + item - 2)
                        for i in range(2):
                            ins = pe.matmul(bn(item % 3), w_in_sb[:, i, (first + m) * P:(first + m + 1) * P], xn[:, i, ck(c)],
                                            start=i == 0, stop=i == 1)
                        ins.then_inc(done, 1)

                pe.wait_ge(s_norm, NC * (k + 1))
                for c in range(NC):
                    project(c, 0, s_xr_in, s_xr, NJ * NC * k)
                pe.wait_ge(s_xr, NJ * NC * (k + 1))
                for c in range(NC):
                    pe.wait_ge(s_u, NJ * (NC * k + c + 1))
                    if c >= 2:
                        pe.wait_ge(s_split, NC * k + c - 1)
                        if k < 2:
                            pe.wait_ge(s_dt_sb, NC * k + c - 1)
                    for j in range(NJ):
                        ins = pe.matmul(bn(4 + c % 2, M), w_x_sb[k][:, j, 0:M], u[:, j, ck(c)], start=j == 0, stop=j == NJ - 1)
                    ins.then_inc(s_bc_rows, 1)
                    if k == 2:
                        if c:
                            pe.wait_ge(s_dt_sb, NC * k + c)
                        for j in range(NJ):
                            ins = pe.matmul(bn(3, 1), w_x_sb[k][:, j, G:G + 1], u[:, j, ck(c)], start=j == 0, stop=j == NJ - 1)
                        ins.then_inc(s_dt_in, 1)
                    project(c, NJ, s_gate_in, s_gate, NJ * NC * k)
                    pe.wait_ge(s_dt_sb, NC * k + c + 1)
                    for j in range(NJ):
                        item = NJ * c + j
                        if NJ * NC * k + item >= 2:
                            pe.wait_ge(s_dt_x, NJ * NC * k + item - 1)
                        if k < 2:
                            w, low = w_dt_sb[2 * n:2 * n + R, k, j * P:(j + 1) * P], dt_low[2 * n:2 * n + R, ck(c)]
                            pe.matmul(bn(6 + item % 2), w, low, start=True, stop=True, tile_position=(2 * n, 0)).then_inc(s_dt_proj, 1)
                        else:
                            pe.matmul(bn(6 + item % 2), ones[0:1, :], dt_low[0:1, ck(c)], start=True, stop=True).then_inc(s_dt_proj, 1)
                pe.wait_ge(s_split, NC * (k + 1))
                pe.wait_ge(s_gate, NJ * NC * (k + 1))
                pe.wait_ge(s_dt_x, NJ * NC * (k + 1))
                pe.wait_ge(s_stack, STACKED[k + 1])
                pe.wait_ge(s_diag, NJ * (k + 1))
                for c in range(NC):
                    base = STEP0[k] + c * n

                    def skip():
                        for j in range(NJ):
                            pe.matmul(bn(j), diag[:, j, :], u[:, j, ck(c)], start=False, stop=False, skip_group_check=True)

                    def add_up(s, v, first=False, last=False, base=base):
                        pe.wait_ge(s_hc, s + (base + v + 1))
                        for j in range(NJ):
                            ins = pe.matmul(bn(j), ident[:], h_slot[:, v % H_SLOTS, j, :], start=first, stop=last,
                                            skip_group_check=True)
                        ins.then_inc(s_ysum, 1)

                    def scan_pe(s, g, end):
                        for i in range(4):
                            if n < 32:
                                gb, gc, nb, nc_ = 0, 0, s + i, s + (i + n)
                            else:
                                gb = g
                                gc, nb, nc_ = gb + 2, s + (i - 32 * gb), s + (i - 32 * gb)
                            if end != "first" or i or k + c:
                                pe.wait_ge(s_bu[NJ - 1], s + (base + i))
                            pe.matmul(bn(3), sel[:, bass.ds(nb, 1), :].rearrange("p a m -> p (a m)"), stack[:, gb, ck(c)],
                                      start=True, stop=True).then_inc(s_b_bc, 1)
                            if end != "first" or i or k + c:
                                pe.wait_ge(s_c_row, s + (base + i))
                            pe.matmul(bn(4), sel[:, bass.ds(nc_, 1), :].rearrange("p a m -> p (a m)"), stack[:, gc, ck(c)],
                                      start=True, stop=True).then_inc(s_c_bc, 1)
                            if end == "last" and i == 0:
                                skip()
                            if end != "first" or i >= LAG:
                                if end == "first" and c:
                                    pe.wait_ge(s_y, NC * k + c)
                                add_up(s, i - LAG, first=end == "first")
                            elif c:
                                add_up(0, n - LAG + i, last=i == LAG - 1, base=base - n)
                    steps(pe, n, scan_pe)
                for v in range(n - LAG, n):
                    add_up(0, v, last=v == n - 1)
                pe.wait_ge(s_y, NC * (k + 1))
                for c in range(NC):
                    for i in range(2):
                        for j in range(NJ):
                            ins = pe.matmul(bn(2 * c + i, CH), w_out_sb[:, k, j, i * CH:(i + 1) * CH], gate[:, j, ck(c)],
                                            start=j == 0, stop=j == NJ - 1)
                    ins.then_inc(s_outproj, 1)
            norm_pe(3)
            norm_pe(4, resid=xf)
            pe.wait_ge(f_w2_sum, 1)
            for b in range(14):
                if b < 8:
                    pe.wait_ge(s_norm, NC * 5)
                else:
                    pe.wait_ge(f_w_turned, b - 7)
                for i in range(2):
                    ins = pe.transpose(bank[0:CH, b % 8, i * CH:(i + 1) * CH], w1_raw[:, b, i * CH:(i + 1) * CH], ident[0:CH, 0:CH])
                ins.then_inc(f_w_turn, 1)
            for b in range(18):
                f, i = b // 2, b % 2
                pe.wait_ge(f_w_turned, 14 + b - 7)
                w = w2_raw[:, i, f * P:(f + 1) * P] if f < HID // P else w2_pad[:, i, f - HID // P].rearrange("p j d -> p (j d)")
                pe.transpose(bank[:, (14 + b) % 8, 0:CH], w, ident[0:CH, 0:CH]).then_inc(f_w_turn, 1)
            pe.wait_ge(f_w_turned, 32)
            pe.wait_ge(f_ffn_c, 16 * 8)
            for b in range(KT):
                for i in range(2):
                    ins = pe.matmul(bank[:, 0, b * E:(b + 1) * E], xf[:, i, b * P:(b + 1) * P], w_router_sb[:, i, :],
                                    start=i == 0, stop=i == 1)
            ins.then_inc(f_logit, 1)
            pe.wait_ge(f_probs, 2)
            for b in range(KT):
                ins = pe.transpose(bank[:, 4 + b // 4, (b % 4) * P:(b % 4 + 1) * P],
                                   prob_wide[:, b].rearrange("p e m -> p (e m)"), ident[:])
                if b % 4 == 3:
                    ins.then_inc(f_prob_t, 1)
            for r in range(SEARCH_ROUNDS):
                pe.wait_ge(f_flag, r + 1)
                pe.matmul(bank[:, 0, r:r + 1], group_ones, search[:, 1:2], start=True, stop=True).then_inc(f_votes, 1)
            pe.wait_ge(f_chosen, 1)
            for c in range(NC):
                for i in range(2):
                    ins = pe.matmul(bn(2 * c + i, CH + i), width_mask[:, i * CH:(i + 1) * CH + i], chosen[:, ck(c)],
                                    start=True, stop=True)
                ins.then_inc(f_share, 1)
            pe.wait_ge(f_yw, NC)
            for tile in range(4):
                for c in range(NC):
                    item = tile * NC + c
                    if item >= 8:
                        pe.wait_ge(f_qk_left, item - 7)
                    for i in range(2):
                        ins = pe.matmul(bn(item % 8, CH), w1t[0:CH + i, i, HID + tile * CH:HID + (tile + 1) * CH],
                                        yw[0:CH + i, i, ck(c)], start=i == 0, stop=i == 1)
                    ins.then_inc(f_qk, 1)
            pe.wait_ge(f_qk_left, 4 * NC)
            for b in range(KT):
                if b >= 8:
                    pe.wait_ge(f_v_sb, b - 7)
                for i in range(2):
                    ins = pe.matmul(bank[:, b % 8, 0:C], yw[0:CH + i, i, b * P:(b + 1) * P], w1t[0:CH + i, i, HID + 2 * C:F1],
                                    start=i == 0, stop=i == 1)
                ins.then_inc(f_v, 1)
            pe.wait_ge(f_v_sb, KT)

            def max_pe(step, g, c, ms):
                for m in ms:
                    head, qt, r = m // 16, m // 4 % 4, m % 4
                    if m < MAX_RING:
                        pe.wait_ge(f_mred, step * 64)
                        if m == 2:
                            pe.wait_ge(f_mxrow, step)
                    else:
                        pe.wait_ge(f_mred, step * 64 + (m + 1 - MAX_RING))
                    pe.matmul(bank[:, 5 + m % MAX_RING, :], q_stack[0:KR, q_cols(c, head, P, qt * P)],
                              k_stack[g % 2][0:KR, head, r * CK:(r + 1) * CK], start=True, stop=True).then_inc(f_mscore, 1)

            def max_end(step):
                pe.wait_ge(f_mx, step + 1)
                pe.transpose(bank[0:HG * 4, 7, 0:P], max_q[:], ident[:]).then_inc(f_mxt, 1)

            def values(step, g, kt):
                pe.wait_ge(f_p, step * (2 * KT) + (2 * (kt + 1) + P0))
                if kt == 0:
                    pe.wait_ge(f_attn, step + O0)
                for h in range(HG):
                    ins = pe.matmul(bank[32 * h:32 * h + 32, 4, :], v_sb[:, kt, HG * g + h, :], p_slot[:, 2 * (kt % 2) + h // 2, h % 2, :],
                                    start=kt == 0, stop=kt == KT - 1, tile_position=(0, 32 * h), skip_group_check=True)
                ins.then_inc(f_pv, 1)

            def attn_pe(step, g, c, ahead):
                for kt in range(KT):
                    ms = list(range(4 * kt + 4, 4 * kt + 8)) if kt < KT - 1 else []
                    if kt == 0:
                        if ahead:
                            max_pe(step + 1, *ahead, range(4))
                        pe.wait_ge(f_qrow, (step + 1) * 48)
                    for half in range(2):
                        pe.wait_ge(f_p, step * (2 * KT) + (2 * kt + half - 1 + P0))
                        for h in range(2 * half, 2 * half + 2):
                            ins = pe.matmul(bank[:, h, :], k_stack[g % 2][0:KR + 3, h, kt * P:(kt + 1) * P],
                                            q_stack[0:KR + 3, q_cols(c, h, CK)], start=True, stop=True)
                        ins.then_inc(f_st, 1)
                        if ahead:
                            max_pe(step + 1, *ahead, ms[half:half + 1])
                    if ahead and kt == KT - 1:
                        max_end(step + 1)
                    if kt:
                        values(step, g, kt - 1)
                    if ahead:
                        max_pe(step + 1, *ahead, ms[2:])
                values(step, g, KT - 1)
            pe.wait_ge(f_k_pad, 2)
            pe.wait_ge(f_kload[0], 16)
            pe.wait_ge(f_qload[0], 16)
            max_pe(0, 0, 0, range(64))
            max_end(0)
            for g in range(NG):
                for c in range(1, NC):
                    pe.wait_ge(f_qload[c], 16 * (g + 1))
                with pe.Fori(0, NC - 1) as c:
                    attn_pe(c + g * NC, g, c, (g, c + 1))
                if g < NG - 1:
                    pe.wait_ge(f_kload[(g + 1) % 2], 16 * ((g + 1) // 2 + 1))
                    pe.wait_ge(f_qload[0], 16 * (g + 2))
                    attn_pe(g * NC + NC - 1, g, NC - 1, (g + 1, 0))
                else:
                    attn_pe(g * NC + NC - 1, g, NC - 1, None)
            def fc1(items):
                for item in items:
                    f, c = item // NC, item % NC
                    if item >= 4:
                        pe.wait_ge(f_mlp, item - 3)
                    for i in range(2):
                        ins = pe.matmul(bn(item % 4), w1t[0:CH + i, i, f * P:(f + 1) * P], yw[0:CH + i, i, ck(c)],
                                        start=i == 0, stop=i == 1)
                    ins.then_inc(f_fc1, 1)

            def pick_sums(g):
                pe.wait_ge(f_attn, NG * NC + O0)
                if g:
                    pe.wait_ge(f_inv, g)
                for c in range(NC):
                    ins = pe.matmul(bank[32 * c:32 * c + 32, 4, :], sum_pick, xa[:, g, ck(c)], start=True, stop=True,
                                    tile_position=(0, 32 * c), skip_group_check=True)
                ins.then_inc(f_sums, 1)

            def spread_sums(g):
                pe.wait_ge(f_inv, g + 1)
                for c in range(NC):
                    item = g * NC + c
                    if item >= 3:
                        pe.wait_ge(f_xa, item - 2)
                    pe.matmul(bn(5 + item % 3), sum_spread[:, c, :], inv_sb[:, g, :], start=True, stop=True).then_inc(f_spread, 1)

            FC1_ITEMS = HID // P * NC
            fc1(range(0, 4))
            for g in range(NG):
                pick_sums(g)
                fc1(range(4 + 5 * g, 9 + 5 * g))
                spread_sums(g)
            fc1(range(4 + 5 * NG, FC1_ITEMS))
            pe.wait_ge(f_xa, NG * NC)
            pe.wait_ge(f_mlp, FC1_ITEMS)

            def turn_rows(c):
                pe.wait_ge(f_zz, NC + 2 * (c + 1))
                for b in range(c * (CK // P), (c + 1) * (CK // P)):
                    if b >= 2:
                        pe.wait_ge(s_fin, b - 1)
                    for i in range(2):
                        ins = pe.transpose(bank[:, 6 + b % 2, i * CH:(i + 1) * CH], resid[:, i, b * P:(b + 1) * P], ident[0:CH, 0:CH])
                    ins.then_inc(s_fin_t, 1)
            for c in range(NC):
                for i in range(2):
                    item = 2 * c + i
                    if item >= 4:
                        pe.wait_ge(f_o, item - 3)
                    for f in range(9):
                        src = mlp[:, f, ck(c)] if f < 6 else xa[:, f - 6, ck(c)]
                        ins = pe.matmul(bn(item % 4, CH), w2t[:, f, i * CH:(i + 1) * CH], src, start=f == 0, stop=f == 8)
                    ins.then_inc(f_fc2, 1)
                    if item >= 2:
                        pe.wait_ge(f_zz, NC + item - 1)
                    pe.matmul(bn(4 + item % 2, CH), width_mask[:, i * CH:(i + 1) * CH], selgate[:, ck(c)],
                              start=True, stop=True).then_inc(f_g, 1)
                    if c and i == 0:
                        turn_rows(c - 1)
            turn_rows(NC - 1)


_INS = ['x', 'L0_tok_emb', 'L0_tok_norm_w', 'L0_tok_in_proj_w', 'L0_tok_conv_w', 'L0_tok_conv_b', 'L0_tok_x_proj_w',
        'L0_tok_dt_proj_w', 'L0_tok_dt_proj_b', 'L0_tok_A_log', 'L0_tok_D', 'L0_tok_out_proj_w', 'L0_attn_in_w',
        'L0_attn_conv_w', 'L0_attn_conv_b', 'L0_attn_xproj_w', 'L0_attn_A_log', 'L0_attn_dt_bias', 'L0_attn_D',
        'L0_attn_out_w', 'L0_ffn_w_router', 'L0_ffn_gamma1', 'L0_ffn_beta1', 'L0_ffn_w1', 'L0_ffn_b1', 'L0_ffn_w2',
        'L0_ffn_b2']


def shape_constants():
    p = np.arange(P)
    return {
        "ident": np.eye(P, dtype=np.float32),
        "fold": (p[:, None] % 32 == np.arange(32)[None, :]).astype(np.float32),
        "width_mask": ((p[:, None] % 32 == 0) & (np.append(np.arange(C), 0)[None, :] < np.array(WIDTH)[p // 32][:, None])).astype(np.float32),
        "group_ones": (p[:, None] // 32 == p[None, :] // 32).astype(np.float32),
        "sum_pick": (p[:, None] == (np.arange(32) % HG * 32 + HD)[None, :]).astype(np.float32),
        "sum_spread": (p[:, None, None] == np.arange(NC)[None, :, None] * 32 + (p // 32)[None, None, :]).astype(np.float32),
        "search_off": ((p[:, None] % 32) << (SEARCH_BITS * np.arange(SEARCH_ROUNDS - 1, -1, -1))[None, :]).astype(np.int32),
    }


def kernel(**inputs):
    import concourse.bacc as bacc
    from concourse.bass_utils import run_bass_kernel_spmd

    nc = bacc.Bacc("TRN2", target_bir_lowering=False, num_devices=1)
    arrays, dram = {}, {}

    def give(name, a):
        a = np.ascontiguousarray(a)
        arrays[f"in_{name}"] = a
        return nc.dram_tensor(f"in_{name}", a.shape, mybir.dt.from_np(a.dtype), kind="ExternalInput").ap()

    for name in _INS:
        dram[name] = give(name, inputs[name])
    consts = {name: give("const_" + name, a) for name, a in shape_constants().items()}
    out = nc.dram_tensor("out_0", (1, L, C), F32, kind="ExternalOutput").ap()

    def per_layer(tok, att):
        return [dram["L0_tok_" + tok][0], dram["L0_tok_" + tok][1], dram["L0_attn_" + att]]

    build(nc, dram["x"], dram["L0_tok_emb"], dram["L0_tok_norm_w"], per_layer("in_proj_w", "in_w"),
          per_layer("conv_w", "conv_w"), per_layer("conv_b", "conv_b"), per_layer("x_proj_w", "xproj_w"),
          dram["L0_tok_dt_proj_w"], per_layer("dt_proj_b", "dt_bias"), per_layer("A_log", "A_log"), per_layer("D", "D"),
          per_layer("out_proj_w", "out_w"),
          {"w_router": dram["L0_ffn_w_router"], "gamma": dram["L0_ffn_gamma1"], "beta": dram["L0_ffn_beta1"],
           "w1": dram["L0_ffn_w1"], "b1": dram["L0_ffn_b1"], "w2": dram["L0_ffn_w2"], "b2": dram["L0_ffn_b2"]}, consts, out)
    r = run_bass_kernel_spmd(nc, [arrays], core_ids=[0])
    return r.results[0]["out_0"]
```

```python
from contextlib import ExitStack

import numpy as np
import concourse.bass as bass
from concourse import mybir

F32 = mybir.dt.float32
BF16 = mybir.dt.bfloat16
I32 = mybir.dt.int32
ALU = mybir.AluOpType
ACT = mybir.ActivationFunctionType
AX_X = mybir.AxisListType.X

P = 128
L = 2048
C = 192
V = 8000
CH = C // 2
DI = 2 * C
NJ = DI // P
CK = 512
NC = L // CK
TAPS = 4
TOK_N, TOK_R = 16, 12
ATT_N = 64
BLOCK_N = (TOK_N, TOK_N, ATT_N)
BLOCK_R = (TOK_R, TOK_R, 1)
STEP0 = (0, NC * TOK_N, 2 * NC * TOK_N, 2 * NC * TOK_N + NC * ATT_N)
NB = 3
A_LOG_MAX = 85.0
H_SLOTS, C_SLOTS = 4, 4
B_BANK, C_BANK, A_BANK = 3, 4, 5
OUT_BANKS = ((3, 4), (5, 6), (0, 1), (2, 7))
LAG = 3

E = 4
WIDTH = [C // 2 ** (E - 1 - e) for e in range(E)]
CAP = L // 2
HEADS, HD = 12, 16
HID = 4 * C
F1 = HID + 3 * C
F2 = HID + C
HG = 4
NG = HEADS // HG
KT = L // P
PARTS = 3
TILES = (2, 0, 3, 1)
PAIRS = ((0, 0), (0, 1), (1, 0), (1, 1), (0, 2), (2, 0))
KR = len(PAIRS) * HD
SEARCH_BITS, SEARCH_ROUNDS = 5, 6
V_RING = 5
MAX_RING = 3


def part_stack(t, part, group, lo, hi):
    return t[32 * part:32 * part + 32, group, lo:hi]


def build(nc, x, emb, norm_w, w_in, conv_w, conv_b, x_proj, dt_w, dt_b, a_log, d_skip, w_out, ffn, consts, out):
    with ExitStack() as ctx:
        def sb(name, shape, dt=F32):
            return ctx.enter_context(nc.sbuf_tensor(name, shape, dt))

        def sem(name):
            return ctx.enter_context(nc.semaphore(name))

        bank = ctx.enter_context(nc.psum_tensor("bank", [P, 8, CK], F32))
        resid = sb("resid", [CH, 2, L])
        region = sb("region", [P, 3 * (NJ * L) + NJ * (L + TAPS - 1)])
        scratch = sb("scratch", [P, NJ * L + 3 * L // 2])
        stack_all = sb("stack", [P, 4, L], BF16)
        stack = stack_all[0:3 * 32]
        c_row = sb("c_row", [P, C_SLOTS, CK])
        weights = sb("weights", [P, 32 * P // 2 + 2 * 2 * DI])
        sel = weights[0:3 * 32, 0:32 * P // 2].bitcast(BF16).rearrange("p (m k) -> p m k", k=P)
        w_in_sb = weights[0:CH, 32 * P // 2:].rearrange("p (i n) -> p i n", i=2)
        w_out_sb = sb("w_out_sb", [P, NB, NJ, C])
        w_x_sb = [sb(f"w_x{k}", [P, NJ, BLOCK_R[k] + 2 * BLOCK_N[k]]) for k in range(NB)]
        w_dt_sb = sb("w_dt_sb", [2 * TOK_N + TOK_R, 2, DI])
        norm_sb = sb("norm_sb", [CH, 2, 2])
        conv_w_sb = sb("conv_w_sb", [P, NB, NJ, TAPS])
        vec_sb = sb("vec_sb", [P, 3, NB, NJ])
        a_sb = [sb(f"a{k}", [P, NJ, BLOCK_N[k]]) for k in range(NB)]
        diag = sb("diag", [P, NJ, P])
        state = sb("state", [P, ATT_N, NJ])
        ident = sb("ident", [P, P])
        w1t = weights[0:CH + 1, 0:2 * F1].rearrange("p (i f) -> p i f", i=2)
        w2t = w_out_sb[:].rearrange("p k j c -> p (k j) c")
        w_router_sb = sb("w_router_sb", [CH, 2, E])
        ffn_rows = sb("ffn_rows", [8, CH])
        ffn_vec = sb("ffn_vec", [CH, 4, 2])
        small = c_row[:].rearrange("p s t -> p (s t)")
        width_mask = small[:, 0:C + 1]
        group_ones = small[:, 256:256 + P]
        sum_pick = small[:, 384:384 + 32]
        sum_spread = small[:, 1024:1024 + NC * P].rearrange("p (c m) -> p c m", c=NC)
        search_off = sb("search_off", [P, SEARCH_ROUNDS], I32)
        probs = sb("probs", [P, KT, E])
        psum_e = sb("psum_e", [P, KT])
        search = sb("search", [P, 8])
        search_i = sb("search_i", [P, 4], I32)
        max_part = sb("max_part", [P, HG * 4, 4])
        max_q = sb("max_q", [P, HG * 4])
        max_left = small[0:HG * 4, 512:512 + P]
        max_row = small[0:HG * 4, 640:640 + 3 * P // 2].bitcast(BF16).rearrange("p (a t) -> p a t", a=3)
        fold = sb("fold", [P, 32])
        ones = sb("ones", [P, P])
        idx_rows = sb("idx_rows", [L // P, P], I32)
        idx_f = sb("idx_f", [L // P, 2, P])
        idx = sb("idx", [P, L // P], I32)
        vec_rows = sb("vec_rows", [3 * NB * NJ, P])
        norm_rows = sb("norm_rows", [4, CH])

        RW = NJ * L
        xr = region[:, 0:NJ * (L + TAPS - 1)].rearrange("p (j t) -> p j t", j=NJ)
        dtu = xr[:, :, TAPS - 1:]
        r0 = NJ * (L + TAPS - 1)
        u = region[:, r0:r0 + RW].rearrange("p (j t) -> p j t", j=NJ)
        gate = region[:, r0 + RW:r0 + 2 * RW].rearrange("p (j t) -> p j t", j=NJ)
        delta = region[:, r0 + 2 * RW:r0 + 3 * RW].rearrange("p (j t) -> p j t", j=NJ)
        xn = region[0:CH, r0 + 2 * RW:r0 + 2 * RW + 2 * L].rearrange("p (i t) -> p i t", i=2)
        h_slot = scratch[:, 3 * L // 2:].rearrange("p (s j t) -> p s j t", s=H_SLOTS, j=NJ)
        square = scratch[0:CH, 0:2 * L].rearrange("p (i t) -> p i t", i=2)
        inv = scratch[:, 2 * L:2 * L + CK]
        pick = diag[:].rearrange("p j m -> p (j m)").rearrange("p (c m) -> p c m", c=NC)
        soft = scratch[:, 0:NJ * L].rearrange("p (j t) -> p j t", j=NJ)
        parts = scratch[:, NJ * L:NJ * L + 3 * L // 2].bitcast(BF16).rearrange("p (s t) -> p s t", s=3)
        dt_low = c_row[:].rearrange("p s t -> p (s t)")
        left = dtu[:, 0, (NC - 1) * CK:]
        out_rows = region[:, 0:L // P * C].rearrange("p (b c) -> p b c", b=L // P)
        tok_rows = scratch[:, 0:L // P * C].rearrange("p (b c) -> p b c", b=L // P)

        xf = xn
        yw = region[0:CH + 1, 0:2 * L].rearrange("p (i t) -> p i t", i=2)
        selgate = region[:, 2 * L:3 * L]
        v_sb = region[:, 3 * L:6 * L].rearrange("p (b h d) -> p b h d", b=KT, h=HEADS)
        mlp = region[:, 3 * L:9 * L].rearrange("p (f t) -> p f t", f=HID // P)
        w1_raw = region[0:CH, 3 * L:3 * L + 14 * C].rearrange("p (b c) -> p b c", c=C)
        o = 3 * L + 14 * C
        w2_raw = region[0:CH, o:o + 4 * F2].rearrange("p (b f) -> p b f", b=4)
        o += 4 * F2
        w2_pad = region[0:CH, o:o + 2 * NG * P].rearrange("p (i g j d) -> p i g j d", i=2, g=NG, j=HG)
        xa = region[:, r0 + 2 * RW:r0 + 3 * RW].rearrange("p (g t) -> p g t", g=NG)
        k_stack = [region[:, 6 * L:8 * L].bitcast(BF16).rearrange("p (h t) -> p h t", h=HG),
                   scratch[:, 2 * L:4 * L].bitcast(BF16).rearrange("p (h t) -> p h t", h=HG)]
        q_stack = stack_all[:].rearrange("p a t -> p (a t)")

        def q_cols(c, head, n, at=0):
            return bass.ds(c * (HG * CK) + (head * CK + at), n)
        p_slot = scratch[:, 0:2 * L].rearrange("p (s h t) -> p s h t", s=4, h=2)
        prob_bc = scratch[:, 0:L]
        prob_wide = scratch[:, 3 * L:4 * L].rearrange("p (b e m) -> p b e m", b=KT, e=E)
        chosen = scratch[:, L:2 * L]
        flag = scratch[:, 2 * L:3 * L]
        prefix = scratch[:, 3 * L:4 * L]
        qk_part = [(scratch[0:CH, 3 * L // 2 * t:3 * L // 2 * (t + 1)] if t < 2 else
                    region[0:CH, r0 + 2 * RW + 3 * L // 2 * (t - 2):r0 + 2 * RW + 3 * L // 2 * (t - 1)]).bitcast(BF16).rearrange(
                        "p (a t) -> p a t", a=PARTS) for t in range(4)]
        qk_left = scratch[0:CH, 3 * L:4 * L]
        inv_sb = scratch[:, 0:NG * CK].rearrange("p (g t) -> p g t", g=NG)
        P0 = 2
        O0 = 1
        b2_sum = ffn_vec[:, 2, :]
        PV0 = 2
        o_sb = scratch[0:CH, 0:4 * L].rearrange("p (i t) -> p i t", i=4)[:, 0:2]
        qk_dram = nc.dram_tensor("qk_parts", (2, HEADS, KR, L), BF16, kind="Internal").ap()

        s_const = sem("s_const")
        s_small = sem("s_small")
        s_vec = sem("s_vec")
        s_turned = sem("s_turned")
        s_vec_ok = sem("s_vec_ok")
        s_win = sem("s_win")
        s_idx = sem("s_idx")
        s_idx_ok = sem("s_idx_ok")
        s_rows = [sem(f"s_rows{c}") for c in range(NC)]
        s_rows_t = sem("s_rows_t")
        s_resid = sem("s_resid")
        s_sel = sem("s_sel")
        s_sum = sem("s_sum")
        s_centered = sem("s_centered")
        s_square = sem("s_square")
        s_var = sem("s_var")
        s_pick = sem("s_pick")
        s_spread = sem("s_spread")
        s_inv = sem("s_inv")
        s_rstd = sem("s_rstd")
        s_norm = sem("s_norm")
        s_xr_in = sem("s_xr_in")
        s_xr = sem("s_xr")
        s_gate_in = sem("s_gate_in")
        s_gate = sem("s_gate")
        s_tap = sem("s_tap")
        s_exp = sem("s_exp")
        s_ln = sem("s_ln")
        s_relu_exp = sem("s_relu_exp")
        s_delta = sem("s_delta")
        s_conv = sem("s_conv")
        s_u = sem("s_u")
        s_bc_rows = sem("s_bc_rows")
        s_split = sem("s_split")
        s_stack = sem("s_stack")
        s_dt_in = sem("s_dt_in")
        s_dt_sb = sem("s_dt_sb")
        s_dt_proj = sem("s_dt_proj")
        s_dt_x = sem("s_dt_x")
        s_dtu = sem("s_dtu")
        s_a_log = sem("s_a_log")
        s_a_mat = sem("s_a_mat")
        s_a_ready = sem("s_a_ready")
        s_diag = sem("s_diag")
        s_b_bc = sem("s_b_bc")
        s_c_bc = sem("s_c_bc")
        s_bu = sem("s_bu")
        s_c_row = sem("s_c_row")
        s_a = [sem(f"s_a{j}") for j in range(NJ)]
        s_scan = [sem(f"s_scan{j}") for j in range(NJ)]
        s_carry = sem("s_carry")
        s_hc = sem("s_hc")
        s_ysum = sem("s_ysum")
        s_y = sem("s_y")
        s_outproj = sem("s_outproj")
        s_v = sem("s_v")
        s_fin_t = sem("s_fin_t")
        s_fin = sem("s_fin")
        s_out = sem("s_out")
        s_pool = sem("s_pool")
        f_w_raw = sem("f_w_raw")
        f_ffn_c = sem("f_ffn_c")
        f_ffn_v = sem("f_ffn_v")
        f_w2_half = sem("f_w2_half")
        f_w_turn = sem("f_w_turn")
        f_w_turned = sem("f_w_turned")
        f_logit = sem("f_logit")
        f_probs = sem("f_probs")
        f_prob_t = sem("f_prob_t")
        f_prob_bc = sem("f_prob_bc")
        f_cand = sem("f_cand")
        f_flag = sem("f_flag")
        f_votes = sem("f_votes")
        f_chosen = sem("f_chosen")
        f_share = sem("f_share")
        f_yw = sem("f_yw")
        f_qk = sem("f_qk")
        f_qk_hi = sem("f_qk_hi")
        f_qk_left = sem("f_qk_left")
        f_qk_mid = sem("f_qk_mid")
        f_qk_lo = sem("f_qk_lo")
        f_qk_store = [sem(f"f_qk_store{tile}") for tile in range(4)]
        f_v = sem("f_v")
        f_v_sb = sem("f_v_sb")
        f_v_pad = sem("f_v_pad")
        f_k_pad = sem("f_k_pad")
        f_gate2 = sem("f_gate2")
        f_ffv = sem("f_ffv")
        f_ffp = sem("f_ffp")
        f_st = sem("f_st")
        f_p = sem("f_p")
        f_pv = sem("f_pv")
        f_attn = sem("f_attn")
        f_mscore = sem("f_mscore")
        f_mred = sem("f_mred")
        f_mx = sem("f_mx")
        f_mxt = sem("f_mxt")
        f_mxrow = sem("f_mxrow")
        f_qrow = sem("f_qrow")
        f_sums = sem("f_sums")
        f_inv = sem("f_inv")
        f_spread = sem("f_spread")
        f_xa = sem("f_xa")
        f_fc1 = sem("f_fc1")
        f_mlp = sem("f_mlp")
        f_fc2 = sem("f_fc2")
        f_o = sem("f_o")
        f_g = sem("f_g")
        f_zz = sem("f_zz")
        f_kload = [sem(f"f_kload{g}") for g in range(NG)]
        f_qfirst = [sem(f"f_qfirst{c}") for c in range(NC)]
        f_qload = [sem(f"f_qload{c}") for c in range(NC)]

        def ck(c):
            return slice(c * CK, (c + 1) * CK)

        def bn(b, rows=P):
            return bank[0:rows, b, :]

        def load_k(eng, g):
            eng.dma_start(k_stack[g % 2][0:KR], qk_dram[1, HG * g:HG * g + HG].rearrange("h r t -> r h t")).then_inc(f_kload[g], 16)

        def load_q(eng, g, c):
            eng.dma_start(q_stack[0:KR, q_cols(c, 0, HG * CK)].rearrange("r (h t) -> r h t", h=HG),
                          qk_dram[0, HG * g:HG * g + HG, :, ck(c)].rearrange("h r t -> r h t")).then_inc(f_qload[c] if g else f_qfirst[c], 16)

        block = ctx.enter_context(nc.Block())

        @block.sync
        def _(sp):
            sp.dma_start(idx_rows[:], x.rearrange("a (b p) -> (a b) p", p=P)).then_inc(s_idx, 16)
            sp.dma_start(ident[:], consts["ident"]).then_inc(s_const, 16)
            sp.dma_start(fold[:], consts["fold"]).then_inc(s_const, 16)
            for i, name in enumerate(("gamma", "beta")):
                sp.dma_start(ffn_rows[2 * i:2 * i + 2, :], ffn[name].rearrange("(i p) -> i p", i=2)).then_inc(s_vec, 16)
            sp.dma_start(ffn_rows[4:8, :], ffn["b2"].rearrange("(i p) -> i p", i=4)).then_inc(s_vec, 16)
            for i in range(2):
                with nc.allow_non_contiguous_dma(reason="768 numbers"):
                    sp.dma_start(w_router_sb[:, i, :], ffn["w_router"][:, i * CH:(i + 1) * CH].rearrange("e p -> p e")).then_inc(f_ffn_c, 16)
            for k in range(2):
                sp.dma_start(norm_rows[2 * k:2 * k + 2, :], norm_w[k].rearrange("(i p) -> i p", i=2)).then_inc(s_vec, 16)
                sp.dma_start(w_dt_sb[2 * TOK_N:, k, :], dt_w[k]).then_inc(s_small, 16)
            for k in range(NB):
                sp.dma_start(conv_w_sb[:, k], conv_w[k].rearrange("(j p) a b -> p j (a b)", p=P)).then_inc(s_small, 16)
                for i, v in enumerate((conv_b, d_skip, dt_b)):
                    row = (i * NB + k) * NJ
                    sp.dma_start(vec_rows[row:row + NJ, :], v[k].rearrange("(j p) -> j p", p=P)).then_inc(s_vec, 16)
                sp.dma_start(a_sb[k][:], a_log[k].rearrange("(j p) n -> p j n", p=P)).then_inc(s_small, 16)
                w_x, low = x_proj[k].rearrange("(j p) n -> p j n", p=P), BLOCK_R[k] if k < 2 else 0
                bc = 2 * BLOCK_N[k]
                sp.dma_start(w_x_sb[k][:, :, 0:bc], w_x[:, :, low:low + bc]).then_inc(s_small, 16)
                if k < 2:
                    sp.dma_start(w_x_sb[k][:, :, bc:], w_x[:, :, 0:low]).then_inc(s_small, 16)
                else:
                    with nc.allow_non_contiguous_dma(reason="384 numbers"):
                        sp.dma_start(w_x_sb[k][:, :, bc:], w_x[:, :, bc:]).then_inc(s_small, 16)
                sp.dma_start(w_out_sb[:, k], w_out[k].rearrange("(j p) n -> p j n", p=P)).then_inc(s_small, 16)
            stacked = 0
            for k in range(NB):
                if k:
                    sp.wait_ge(s_gate_in, NJ * NC * k)
                sp.dma_start(w_in_sb[:], w_in[k].rearrange("(i p) n -> p i n", i=2)).then_inc(s_win, 16)
                sp.wait_ge(s_split, NC * (k + 1))
                for g in range(max(1, 2 * BLOCK_N[k] // 32)):
                    for part in range(3):
                        sp.dma_start(part_stack(stack, part, g, 0, L),
                                     parts[32 * g:32 * g + 32, part, :]).then_inc(s_stack, 16)
            sp.wait_ge(s_resid, NC * (NB + 1))
            for t, name in ((width_mask, "width_mask"), (group_ones, "group_ones"), (sum_pick, "sum_pick"), (sum_spread, "sum_spread"),
                            (search_off[:], "search_off")):
                sp.dma_start(t, consts[name]).then_inc(f_ffn_c, 16)
            sp.dma_start(w1t[CH:CH + 1, 1, :], ffn["b1"].rearrange("(a f) -> a f", a=1)).then_inc(f_ffn_c, 16)
            sp.dma_start(w1_raw, ffn["w1"].rearrange("(b p) c -> p b c", p=CH)).then_inc(f_w_raw, 16)
            sp.dma_start(w2_raw, ffn["w2"].rearrange("(b p) f -> p b f", p=CH)).then_inc(f_w_raw, 16)
            for t, tile in enumerate(TILES):
                side, half = tile // 2, tile % 2
                sp.wait_ge(f_qk_lo, NC * (t + 1))
                for j, pair in enumerate(PAIRS):
                    sp.dma_start(qk_dram[side, 6 * half:6 * half + 6, HD * j:HD * j + HD, :],
                                 qk_part[t][:, pair[side], :]).then_inc(f_qk_store[t], 16)
                if t == 1:
                    sp.wait_ge(f_qk_store[0], 16 * len(PAIRS))
                    sp.wait_ge(f_qk_store[1], 16 * len(PAIRS))
                    load_k(sp, 0)
                    for c in range(NC):
                        load_q(sp, 0, c)
            def put_maxima(step, c):
                sp.wait_ge(f_mxrow, step + 1)
                for a in range(3):
                    sp.dma_start(q_stack[KR + a:KR + a + 1, q_cols(c, 0, HG * CK)], max_row[:, a, :]).then_inc(f_qrow, 16)
            for g in range(NG):
                with sp.Fori(0, NC) as c:
                    put_maxima(c + g * NC, c)
            for c in range(NC):
                sp.wait_ge(s_fin, CK // P * (c + 1))
                sp.dma_start(out[0, ck(c), :].rearrange("(b p) c -> p b c", p=P),
                             out_rows[:, c * (CK // P):(c + 1) * (CK // P), :]).then_inc(s_out, 16)
            sp.wait_ge(s_out, 16 * NC)

        SMALL_DMAS = 16 * (2 + NB * 5)
        STACKED = [0]
        for k in range(NB):
            STACKED.append(STACKED[-1] + 16 * 3 * max(1, 2 * BLOCK_N[k] // 32))

        def steps(eng, n, emit):
            emit(0, 0, "first")
            for lo, hi in [(4, min(n - 4, 32))] + ([(32, n - 4)] if n > 32 else []):
                with eng.Fori(lo // 4, hi // 4) as turn:
                    emit(turn * 4, lo // 32, "")
            emit(n - 4, (n - 4) // 32, "last")

        @block.gpsimd
        def _(pool):
            pool.wait_ge(s_idx_ok, 2)
            for b in range(L // P):
                pool.indirect_dma_start(tok_rows[:, b, :], None, emb,
                                        bass.IndirectOffsetOnAxis(idx[:, b:b + 1], 0)).then_inc(s_rows[b * P // CK], 16)
            for k in range(NB):
                n = BLOCK_N[k]
                for cs in ((0, 1), (2, 3)):
                    for c in cs:
                        pool.wait_ge(s_exp, NC * k + c + 1)
                        pool.tensor_tensor(delta[:, :, ck(c)], delta[:, :, ck(c)], soft[:, :, ck(c)], ALU.add).then_inc(s_relu_exp, 1)
                    for c in cs:
                        pool.wait_ge(s_delta, NC * k + c + 1)
                        pool.tensor_tensor(dtu[:, :, ck(c)], delta[:, :, ck(c)], u[:, :, ck(c)], ALU.mult).then_inc(s_dtu, 1)
                for c in range(NC):
                    base = STEP0[k] + c * n
                    with pool.Fori(0, n // 4) as turn:
                        s = turn * 4
                        for i in range(4):
                            pool.wait_ge(s_carry, s + (base + i + 1))
                            pool.wait_ge(s_c_row, s + (base + i + 1))
                            cr = c_row[:, i, :].unsqueeze(1).broadcast_to([P, NJ, CK])
                            pool.tensor_tensor(h_slot[:, i], h_slot[:, i], cr, ALU.mult).then_inc(s_hc, 1)
            pool.wait_ge(s_resid, NC * (NB + 1))
            pool.wait_ge(f_w_raw, 32)
            pool.memset(w2_pad, 0.0).then_inc(f_pv, PV0)
            pool.tensor_tensor(w2_raw[:, 0:2, :], w2_raw[:, 0:2, :], w2_raw[:, 2:4, :], ALU.add).then_inc(f_w2_half, 1)
            pool.wait_ge(f_pv, PV0)
            pool.wait_ge(f_w2_half, 1)
            for i in range(2):
                pool.tensor_copy(w2_pad[:, i, :, :, 0:HD],
                                 w2_raw[:, i, HID:F2].rearrange("p (g j d) -> p g j d", g=NG, j=HG)).then_inc(f_w2_half, 1)
            pool.memset(k_stack[0][KR:KR + 3], 1.0).then_inc(f_k_pad, 1)
            pool.wait_ge(f_k_pad, 1)
            pool.wait_ge(f_w_turned, 32)
            pool.memset(v_sb, 0.0).then_inc(f_v_pad, 1)
            pool.wait_ge(f_v_pad, 1)
            pool.memset(v_sb[:, :, :, HD:HD + 1], 1.0).then_inc(f_v_pad, 1)
            pool.wait_ge(f_chosen, 1)
            pool.wait_ge(f_v_pad, 2)
            pool.memset(k_stack[1][KR:KR + 3], 1.0).then_inc(f_k_pad, 1)
            pool.wait_ge(f_k_pad, 2)
            for t in range(4):
                for c in range(NC):
                    pool.wait_ge(f_qk_mid, NC * t + c + 1)
                    pool.tensor_tensor(qk_part[t][:, 2, ck(c)], qk_left[:, ck(c)], qk_part[t][:, 1, ck(c)],
                                       ALU.subtract).then_inc(f_qk_lo, 1)
            for t in range(4):
                pool.wait_ge(f_qk_store[t], 16 * len(PAIRS))

            load_k(pool, 1)
            for g in range(NG - 1):
                for c in range(NC):
                    pool.wait_ge(f_p, 2 * KT * (NC * g + c + 1) + P0)
                    load_q(pool, g + 1, c)
                if g + 2 < NG:
                    load_k(pool, g + 2)

        @block.scalar
        def _(act):
            def norm_act(r):
                src = xn if r < 4 else yw[0:CH]
                for c in range(NC):
                    if r < 2:
                        act.wait_ge(s_resid, NC * r + (c + 1 if r else NC))
                        src = resid
                    else:
                        act.wait_ge(s_centered, NC * (r - 2) + c + 1)
                    act.activation(square[:, :, ck(c)], src[:, :, ck(c)], ACT.Square).then_inc(s_square, 1)
                act.wait_ge(s_inv, r + 1)
                act.activation(inv, inv, ACT.Sqrt).then_inc(s_rstd, 1)

            for k in range(NB):
                n = BLOCK_N[k]
                norm_act(k)
                def take_xr(c):
                    for m in range(NJ):
                        act.wait_ge(s_xr_in, NJ * (NC * k + c) + m + 1)
                        act.activation(dtu[:, m, ck(c)], bn((NJ * c + m) % 3), ACT.Copy).then_inc(s_xr, 1)

                def silu_u(c):
                    for j in range(NJ):
                        act.wait_ge(s_conv, NJ * (NC * k + c) + j + 1)
                        act.activation(u[:, j, ck(c)], u[:, j, ck(c)], ACT.Silu, bias=vec_sb[:, 0, k, j:j + 1]).then_inc(s_u, 1)

                def log_exp(cs):
                    act.wait_ge(s_dt_x, NJ * (NC * k + cs[-1] + 1))
                    for c in cs:
                        act.activation(soft[:, :, ck(c)], soft[:, :, ck(c)], ACT.Exp, scale=-1.0).then_inc(s_exp, 1)
                    act.wait_ge(s_exp, NC * k + cs[-1] + 1)
                    if cs[-1] == NC - 1:
                        act.wait_ge(s_split, NC * (k + 1))
                    for c in cs:
                        act.activation(dtu[:, :, ck(c)], soft[:, :, ck(c)], ACT.Ln, bias=1.0).then_inc(s_ln, 1)

                take_xr(0)
                take_xr(1)
                take_xr(2)
                silu_u(0)
                take_xr(3)
                silu_u(1)
                for c in range(NC):
                    if k < 2:
                        act.wait_ge(s_bc_rows, NC * k + c + 1)
                        act.activation(dt_low[2 * n:2 * n + TOK_R, ck(c)], bank[2 * n:2 * n + TOK_R, 4 + c % 2, :], ACT.Copy).then_inc(s_dt_sb, 1)
                    else:
                        act.wait_ge(s_dt_in, c + 1)
                        act.activation(dt_low[0:1, ck(c)], bn(3, 1), ACT.Copy).then_inc(s_dt_sb, 1)
                    for m in range(NJ):
                        act.wait_ge(s_gate_in, NJ * (NC * k + c) + m + 1)
                        act.activation(gate[:, m, ck(c)], bn((NJ * c + m) % 3), ACT.Silu).then_inc(s_gate, 1)
                    if c < 2:
                        silu_u(c + 2)
                    for j in range(NJ):
                        item = NJ * c + j
                        act.wait_ge(s_dt_proj, NJ * NC * k + item + 1)
                        act.activation(delta[:, j, ck(c)], bn(6 + item % 2), ACT.Relu, bias=vec_sb[:, 2, k, j:j + 1])
                        act.activation(soft[:, j, ck(c)], bn(6 + item % 2), ACT.Abs, bias=vec_sb[:, 2, k, j:j + 1]).then_inc(s_dt_x, 1)
                    if c == 1:
                        log_exp((0, 1))
                act.wait_ge(s_a_log, k + 1)
                act.activation(a_sb[k][:], a_sb[k][:], ACT.Exp).then_inc(s_a_mat, 1)
                log_exp((2, 3))
                act.wait_ge(s_a_ready, k + 1)
                act.wait_ge(s_delta, NC * (k + 1))
                for c in range(NC):
                    base = STEP0[k] + c * n

                    def carry(s, v):
                        act.activation(state[:, bass.ds(s + v, 1), :].rearrange("p a b -> p (a b)"),
                                       h_slot[:, v % H_SLOTS, :, CK - 1], ACT.Copy).then_inc(s_carry, 1)

                    def scan_act(s, g, end):
                        for i in range(4):
                            for j in range(NJ):
                                if j == NJ - 1:
                                    act.wait_ge(s_c_bc, s + (base + i + 1))
                                    if end != "first" or k + c:
                                        act.wait_ge(s_hc, s + (base + i + 1 - C_SLOTS))
                                    act.activation(c_row[:, i, :], bn(C_BANK), ACT.Copy).then_inc(s_c_row, 1)
                                if end != "first" or i or k + c:
                                    act.wait_ge(s_scan[j], s + (base + i))
                                if j == NJ - 1 and (end != "first" or i or c):
                                    if end == "first" and i == 0:
                                        carry(n - H_SLOTS, H_SLOTS - 1)
                                    else:
                                        carry(s, i - 1)
                                act.activation(bn(A_BANK + j), delta[:, j, ck(c)], ACT.Exp,
                                               scale=a_sb[k][:, j, bass.ds(s + i, 1)]).then_inc(s_a[j], 1)
                    steps(act, n, scan_act)
                act.wait_ge(s_scan[NJ - 1], base + n)
                carry(n - H_SLOTS, H_SLOTS - 1)
            norm_act(3)
            norm_act(4)
            act.wait_ge(f_logit, 2)
            act.activation(probs[:], probs[:], ACT.Exp).then_inc(f_probs, 1)
            for c in range(NC):
                act.wait_ge(f_prob_t, c + 1)
                act.activation(prob_bc[:, ck(c)], bn(4 + c), ACT.Copy).then_inc(f_prob_bc, 1)
            for b in range(32):
                act.wait_ge(f_w_turn, b + 1)
                if b < 14:
                    act.activation(w1t[0:CH, :, b * CH:(b + 1) * CH],
                                   bank[0:CH, 1 + b % 7, 0:2 * CH].rearrange("p (i f) -> p i f", i=2), ACT.Copy).then_inc(f_w_turned, 1)
                else:
                    f, i = (b - 14) // 2, b % 2
                    act.activation(w2t[:, f, i * CH:(i + 1) * CH], bank[:, 1 + b % 7, 0:CH], ACT.Copy).then_inc(f_w_turned, 1)
            def middle(item):
                t, c = item // NC, item % NC
                act.wait_ge(f_qk_left, item + 1)
                act.activation(qk_part[t][:, 1, ck(c)], qk_left[:, ck(c)], ACT.Copy).then_inc(f_qk_mid, 1)
            for t, tile in enumerate(TILES):
                scale = HD ** -0.5 if tile < 2 else 1.0
                for c in range(NC):
                    item = t * NC + c
                    act.wait_ge(f_qk, item + 1)
                    act.activation(qk_part[t][:, 0, ck(c)], bn(item % 8, CH), ACT.Copy, scale=scale).then_inc(f_qk_hi, 1)
                    if item:
                        middle(item - 1)
            middle(4 * NC - 1)
            act.wait_ge(f_v_pad, 2)
            for b in range(KT):
                act.wait_ge(f_v, b + 1)
                act.activation(v_sb[:, b, :, 0:HD], bank[:, b % V_RING, 0:C].rearrange("p (h d) -> p h d", h=HEADS),
                               ACT.Copy).then_inc(f_v_sb, 1)
            def attn_act(step):
                for kt in range(KT):
                    for half in range(2):
                        act.wait_ge(f_st, (step * (2 * KT)) + (2 * kt + half + 1))
                        act.wait_ge(f_pv, step * KT + (kt - 1 + PV0))
                        act.activation(p_slot[:, 2 * (kt % 2) + half], bank[:, 2 * half:2 * half + 2, :],
                                       ACT.Exp).then_inc(f_p, 1)
            for g in range(NG):
                with act.Fori(0, NC) as c:
                    attn_act(c + g * NC)
            for f in range(HID // P):
                for c in range(NC):
                    item = f * NC + c
                    act.wait_ge(f_fc1, item + 1)
                    act.activation(mlp[:, f, ck(c)], bn(item % 4), ACT.Gelu).then_inc(f_mlp, 1)
            for c in range(NC):
                for i in range(2):
                    item = 2 * c + i
                    act.wait_ge(f_fc2, item + 1)
                    act.activation(o_sb[:, i, ck(c)], bn(item % 4, CH), ACT.Identity, bias=b2_sum[:, i:i + 1]).then_inc(f_o, 1)

        @block.vector
        def _(dve):
            chain = [0]

            def link(ins):
                chain[0] += 1
                ins.then_inc(s_v, 1)
                dve.wait_ge(s_v, chain[0])

            dve.wait_ge(s_idx, 16)
            link(dve.tensor_scalar(idx_f[:, 0, :], idx_rows[:], 0.0, float(V), ALU.is_lt, ALU.mult))
            link(dve.tensor_tensor(idx_f[:, 1, :], idx_rows[:], idx_f[:, 0, :], ALU.add))
            dve.tensor_scalar(idx_f[:, 0, :], idx_f[:, 1, :], 0.0, float(V - 1), ALU.max, ALU.min).then_inc(s_idx_ok, 1)
            dve.wait_ge(s_turned, 1)
            dve.tensor_copy(idx[:], bank[:, 5, 0:L // P]).then_inc(s_idx_ok, 1)
            dve.wait_ge(s_turned, 2)
            dve.tensor_copy(vec_sb[:].rearrange("p a b c -> p (a b c)"), bank[:, 7, 0:3 * NB * NJ]).then_inc(s_vec_ok, 1)
            dve.tensor_copy(norm_sb[:].rearrange("p a b -> p (a b)"), bank[0:CH, 6, 0:4]).then_inc(s_vec_ok, 1)
            dve.tensor_copy(ffn_vec[:].rearrange("p a b -> p (a b)"), bank[0:CH, 6, 8:16]).then_inc(s_vec_ok, 1)
            dve.memset(ones[:], 1.0).then_inc(s_sel, 1)
            dve.memset(xr[:, :, 0:TAPS - 1], 0.0)
            dve.wait_ge(s_const, 32)
            dve.tensor_copy(sel[:], fold[0:96, :].unsqueeze(2).broadcast_to([96, 32, P])).then_inc(s_sel, 1)
            for c in range(NC):
                dve.wait_ge(s_rows_t, c + 1)
                dve.tensor_copy(resid[:, :, ck(c)], bank[0:CH, 2 * c:2 * c + 2, :]).then_inc(s_resid, 1)
            dve.wait_ge(s_small, SMALL_DMAS)
            for k in range(NB):
                dve.tensor_scalar(a_sb[k][:], a_sb[k][:], A_LOG_MAX, None, ALU.min).then_inc(s_a_log, 1)

            def norm_dve(r, eps, w, src=resid, xn=xn):
                if r >= 2:
                    for c in range(NC):
                        dve.wait_ge(s_sum, NC * (r - 2) + c + 1)
                        mean = bank[0:CH, c:c + 1, :].broadcast_to([CH, 2, CK])
                        dve.scalar_tensor_tensor(xn[:, :, ck(c)], mean, -1.0 / C, src[:, :, ck(c)],
                                                 ALU.mult, ALU.add).then_inc(s_centered, 1)
                for c in range(NC):
                    ins = dve.tensor_copy(pick[:, c, :], ident[:, 32 * c:32 * c + 1].broadcast_to([P, CH]))
                ins.then_inc(s_pick, 1)
                dve.wait_ge(s_var, r + 1)
                link(dve.tensor_scalar(inv, bn(4), 1.0 / C, eps, ALU.mult, ALU.add))
                dve.reciprocal(inv, inv).then_inc(s_inv, 1)
                for c in range(NC):
                    dve.wait_ge(s_spread, NC * r + c + 1)
                    for i in range(2):
                        if w is not None:
                            ins = dve.scalar_tensor_tensor(xn[:, i, ck(c)], resid[:, i, ck(c)], w[:, i:i + 1],
                                                           bn(4 + c, CH), ALU.mult, ALU.mult)
                        else:
                            ins = dve.tensor_tensor(xn[:, i, ck(c)], xn[:, i, ck(c)], bn(4 + c, CH), ALU.mult)
                    ins.then_inc(s_norm, 1)

            for k in range(NB):
                n, R = BLOCK_N[k], BLOCK_R[k]
                norm_dve(k, 1e-5, norm_sb[:, k] if k < 2 else None)
                G = min(P, 2 * n)

                def convolve(c):
                    for j in range(NJ):
                        dve.wait_ge(s_xr, NJ * (NC * k + c) + j + 1)
                    for t in range(TAPS):
                        for j in range(NJ):
                            src, w = xr[:, j, c * CK + t:c * CK + t + CK], conv_w_sb[:, k, j, t:t + 1]
                            if t == 0:
                                ins = dve.tensor_scalar(u[:, j, ck(c)], src, w, None, ALU.mult)
                            else:
                                dve.wait_ge(s_tap, NJ * ((TAPS - 1) * (NC * k + c) + t - 1) + j + 1)
                                ins = dve.scalar_tensor_tensor(u[:, j, ck(c)], src, w, u[:, j, ck(c)], ALU.mult, ALU.add)
                            ins.then_inc(s_conv if t == TAPS - 1 else s_tap, 1)

                def split(c):
                    dve.wait_ge(s_bc_rows, NC * k + c + 1)
                    rows = bn(4 + c % 2, G)
                    link(dve.tensor_copy(parts[0:G, 0, ck(c)], rows))
                    link(dve.tensor_tensor(left[0:G, :], rows, parts[0:G, 0, ck(c)], ALU.subtract))
                    link(dve.tensor_copy(parts[0:G, 1, ck(c)], left[0:G, :]))
                    dve.tensor_tensor(parts[0:G, 2, ck(c)], left[0:G, :], parts[0:G, 1, ck(c)], ALU.subtract).then_inc(s_split, 1)

                def log1p(c):
                    dve.wait_ge(s_relu_exp, NC * k + c + 1)
                    dve.wait_ge(s_ln, NC * k + c + 1)
                    v, w = soft[:, :, ck(c)], dtu[:, :, ck(c)]
                    link(dve.tensor_scalar(v, v, 1.0, 1.0, ALU.add, ALU.subtract))
                    link(dve.tensor_tensor(w, w, v, ALU.subtract))
                    dve.tensor_tensor(delta[:, :, ck(c)], delta[:, :, ck(c)], w, ALU.add).then_inc(s_delta, 1)

                for c in range(NC):
                    convolve(c)
                dve.wait_ge(s_spread, NC * (k + 1))
                for j in range(NJ):
                    dve.tensor_scalar(diag[:, j, :], ident[:], vec_sb[:, 1, k, j:j + 1], None, ALU.mult).then_inc(s_diag, 1)
                dve.memset(state[:], 0.0)
                for c in range(3):
                    split(c)
                log1p(0)
                log1p(1)
                split(3)
                dve.wait_ge(s_a_mat, k + 1)
                dve.tensor_scalar(a_sb[k][:], a_sb[k][:], -1.0, None, ALU.mult).then_inc(s_a_ready, 1)
                log1p(2)
                log1p(3)

                def take_y(c):
                    dve.wait_ge(s_ysum, STEP0[k] + (c + 1) * n)
                    dve.tensor_tensor(gate[:, :, ck(c)], bank[:, 0:3, :], gate[:, :, ck(c)], ALU.mult).then_inc(s_y, 1)

                def b_times(s, v, c, fresh=False):
                    if v == 0:
                        dve.wait_ge(s_dtu, NC * k + c + 1)
                    done = STEP0[k] + c * n + v
                    dve.wait_ge(s_b_bc, s + (done + 1))
                    if not fresh:
                        dve.wait_ge(s_ysum, s + (done + 1 - H_SLOTS))
                    dve.tensor_tensor(h_slot[:, v % H_SLOTS], dtu[:, :, ck(c)], bn(B_BANK).unsqueeze(1).broadcast_to([P, NJ, CK]),
                                      ALU.mult).then_inc(s_bu, 1)

                for c in range(NC):
                    base = STEP0[k] + c * n

                    def scan(s, i, j):
                        dve.wait_ge(s_a[j], s + (base + i + 1))
                        dve.tensor_tensor_scan(h_slot[:, i, j, :], bn(A_BANK + j), h_slot[:, i, j, :],
                                               state[:, bass.ds(s + i, 1), j:j + 1].rearrange("p a b -> p (a b)"),
                                               ALU.mult, ALU.add).then_inc(s_scan[j], 1)

                    def scan_dve(s, g, end):
                        for i in range(4):
                            if c and end == "first" and i == LAG:
                                take_y(c - 1)
                            dve.wait_ge(s_bu, s + (base + i + 1))
                            scan(s, i, 0)
                            scan(s, i, 1)
                            if end != "last" or i < 3:
                                b_times(s, i + 1, c, fresh=k + c == 0 and end == "first" and i + 1 < H_SLOTS)
                            elif c + 1 < NC:
                                b_times(0, 0, c + 1)
                            scan(s, i, 2)
                    if c == 0:
                        b_times(0, 0, 0, fresh=k == 0)
                    steps(dve, n, scan_dve)
                take_y(NC - 1)
                for c in range(NC):
                    dve.wait_ge(s_outproj, NC * k + c + 1)
                    first, second = OUT_BANKS[c]
                    dve.tensor_tensor(resid[:, :, ck(c)], resid[:, :, ck(c)], bank[0:CH, first:second + 1:second - first, :],
                                      ALU.add).then_inc(s_resid, 1)
            norm_dve(3, 1e-5, None)
            for c in range(NC):
                dve.wait_ge(s_norm, NC * 3 + c + 1)
                dve.tensor_tensor(resid[:, :, ck(c)], resid[:, :, ck(c)], xf[:, :, ck(c)], ALU.add).then_inc(f_zz, 1)
            norm_dve(4, 1e-6, None, src=xf, xn=yw[0:CH])
            dve.wait_ge(f_logit, 1)
            lg = bank[:, 0, 0:KT * E].rearrange("p (b e) -> p b e", e=E)
            link(dve.tensor_reduce(psum_e[:], lg, AX_X, ALU.max))
            dve.tensor_tensor(probs[:], lg, psum_e[:].unsqueeze(2).broadcast_to([P, KT, E]), ALU.subtract).then_inc(f_logit, 1)
            dve.wait_ge(f_probs, 1)
            link(dve.tensor_reduce(psum_e[:], probs[:], AX_X, ALU.add))
            link(dve.reciprocal(psum_e[:], psum_e[:]))
            dve.tensor_tensor(prob_wide, probs[:].unsqueeze(3).broadcast_to([P, KT, E, 32]),
                              psum_e[:].unsqueeze(2).unsqueeze(3).broadcast_to([P, KT, E, 32]), ALU.mult).then_inc(f_probs, 1)
            dve.wait_ge(s_norm, NC * 5)
            for i in range(2):
                ins = dve.tensor_scalar(yw[0:CH, i, :], yw[0:CH, i, :], ffn_vec[:, 0, i:i + 1], ffn_vec[:, 1, i:i + 1],
                                        ALU.mult, ALU.add)
            link(ins)
            dve.tensor_tensor(b2_sum, b2_sum, ffn_vec[:, 3, :], ALU.add).then_inc(f_ffv, 1)
            dve.memset(max_part[:], 0.0).then_inc(f_p, P0)
            dve.memset(max_q[:], 0.0).then_inc(f_attn, O0)
            dve.wait_ge(f_ffn_c, 16 * 8)
            link(dve.memset(search_i[:, 0:1], 0))
            dve.wait_ge(f_prob_bc, NC)
            for r in range(SEARCH_ROUNDS):
                link(dve.tensor_tensor(search_i[:, 1:2], search_i[:, 0:1], search_off[:, r:r + 1], ALU.bitwise_or))
                link(dve.tensor_scalar(flag, prob_bc, search_i[:, 1:2].bitcast(F32), 0.0, ALU.is_ge, ALU.add,
                                       accum_out=search[:, 0:1]))
                dve.tensor_scalar(search[:, 1:2], search[:, 0:1], float(CAP), None, ALU.is_ge).then_inc(f_flag, 1)
                dve.wait_ge(f_votes, r + 1)
                link(dve.tensor_scalar(search_i[:, 2:3], bank[:, 0, r:r + 1], 1.0,
                                       float(2 ** (SEARCH_BITS * (SEARCH_ROUNDS - 1 - r))), ALU.subtract, ALU.mult))
                link(dve.tensor_tensor(search_i[:, 0:1], search_i[:, 0:1], search_i[:, 2:3], ALU.bitwise_or))
            least = search_i[:, 0:1].bitcast(F32)
            link(dve.tensor_scalar(chosen, prob_bc, least, 0.0, ALU.is_gt, ALU.add, accum_out=search[:, 2:3]))
            link(dve.tensor_scalar(search[:, 3:4], search[:, 2:3], -1.0, float(CAP), ALU.mult, ALU.add))
            link(dve.tensor_scalar(flag, prob_bc, least, None, ALU.is_equal))
            link(dve.tensor_tensor_scan(prefix, flag, flag, 0.0, ALU.add, ALU.max))
            link(dve.scalar_tensor_tensor(flag, prefix, search[:, 3:4], flag, ALU.is_le, ALU.mult))
            link(dve.tensor_tensor(chosen, chosen, flag, ALU.add))
            dve.tensor_tensor(selgate, chosen, prob_bc, ALU.mult).then_inc(f_chosen, 1)
            for c in range(NC):
                dve.wait_ge(f_share, c + 1)
                dve.tensor_tensor(yw[0:CH, :, ck(c)], yw[0:CH, :, ck(c)], bank[0:CH, 2 * c:2 * c + 2, :], ALU.mult)
                dve.tensor_copy(yw[CH:CH + 1, 1, ck(c)], bank[CH:CH + 1, 2 * c + 1, :]).then_inc(f_yw, 1)
            for t, tile in enumerate(TILES):
                scale = HD ** -0.5 if tile < 2 else 1.0
                for c in range(NC):
                    item = t * NC + c
                    dve.wait_ge(f_qk_hi, item + 1)
                    if t:
                        dve.wait_ge(f_qk_lo, item - NC + 1)
                    dve.scalar_tensor_tensor(qk_left[:, ck(c)], bn(item % 8, CH), scale, qk_part[t][:, 0, ck(c)],
                                             ALU.mult, ALU.subtract).then_inc(f_qk_left, 1)
            def max_dve(step):
                for m in range(HG * 4 * 4):
                    dve.wait_ge(f_mscore, step * (HG * 4 * 4) + (m + 1))
                    dve.tensor_reduce(max_part[:, m // 4, m % 4:m % 4 + 1], bank[:, 5 + m % MAX_RING, :], AX_X, ALU.max).then_inc(f_mred, 1)
                dve.wait_ge(f_mred, (step + 1) * (HG * 4 * 4))
                dve.tensor_reduce(max_q[:], max_part[:], AX_X, ALU.max).then_inc(f_mx, 1)
                dve.wait_ge(f_mxt, step + 1)
                dve.wait_ge(f_qrow, step * 48)
                turned = bank[0:HG * 4, 7, 0:P]
                dve.tensor_scalar(max_row[:, 0, :], turned, -1.0, None, ALU.mult).then_inc(f_ffv, 1)
                dve.wait_ge(f_ffv, step * 3 + 2)
                dve.scalar_tensor_tensor(max_left, turned, -1.0, max_row[:, 0, :], ALU.mult, ALU.subtract).then_inc(f_ffv, 1)
                dve.wait_ge(f_ffv, step * 3 + 3)
                dve.tensor_copy(max_row[:, 1, :], max_left).then_inc(f_ffv, 1)
                dve.wait_ge(f_ffv, step * 3 + 4)
                dve.tensor_tensor(max_row[:, 2, :], max_left, max_row[:, 1, :], ALU.subtract).then_inc(f_mxrow, 1)

            def take_o(step, g, c):
                dve.wait_ge(f_pv, (step + 1) * KT + PV0)
                dve.tensor_scalar(xa[:, g, bass.ds(c * CK, CK)], bank[:, 4, :], 1.0, None, ALU.mult).then_inc(f_attn, 1)
            max_dve(0)
            for t in range(4):
                dve.wait_ge(f_qk_store[t], 16 * len(PAIRS))
            for g in range(NG):
                with dve.Fori(0, NC - 1) as c:
                    max_dve(c + (g * NC + 1))
                    take_o(c + g * NC, g, c)
                if g < NG - 1:
                    max_dve((g + 1) * NC)
                take_o(g * NC + NC - 1, g, NC - 1)
            for g in range(NG):
                dve.wait_ge(f_sums, g + 1)
                dve.reciprocal(inv_sb[:, g, :], bn(4)).then_inc(f_inv, 1)
                for c in range(NC):
                    item = g * NC + c
                    dve.wait_ge(f_spread, item + 1)
                    dve.tensor_tensor(xa[:, g, ck(c)], xa[:, g, ck(c)], bn(5 + item % 3), ALU.mult).then_inc(f_xa, 1)

            def take_rows(c):
                for b in range(c * (CK // P), (c + 1) * (CK // P)):
                    dve.wait_ge(s_fin_t, b + 1)
                    dve.tensor_copy(out_rows[:, b, :], bank[:, 6 + b % 2, 0:C]).then_inc(s_fin, 1)
            for c in range(NC):
                for i in range(2):
                    item = 2 * c + i
                    dve.wait_ge(f_g, item + 1)
                    dve.wait_ge(f_o, item + 1)
                    link(dve.tensor_tensor(o_sb[:, i, ck(c)], o_sb[:, i, ck(c)], bn(4 + item % 2, CH), ALU.mult))
                    dve.tensor_tensor(resid[:, i, ck(c)], resid[:, i, ck(c)], o_sb[:, i, ck(c)], ALU.add).then_inc(f_zz, 1)
                    if c and i == 0:
                        take_rows(c - 1)
            take_rows(NC - 1)

        @block.tensor
        def _(pe):
            pe.wait_ge(s_const, 32)
            pe.wait_ge(s_idx_ok, 1)
            pe.transpose(bank[:, 5, 0:L // P], idx_f[:, 0, :], ident[0:L // P, 0:L // P]).then_inc(s_turned, 1)
            pe.wait_ge(s_vec, 16 * (5 + 3 * NB))
            pe.transpose(bank[0:CH, 6, 0:4], norm_rows[:], ident[0:4, 0:4])
            pe.transpose(bank[0:CH, 6, 8:16], ffn_rows[:], ident[0:8, 0:8])
            pe.transpose(bank[:, 7, 0:3 * NB * NJ], vec_rows[:], ident[0:3 * NB * NJ, 0:3 * NB * NJ]).then_inc(s_turned, 1)
            pe.wait_ge(s_vec_ok, 3)
            for c in range(NC):
                for i in range(2):
                    for t in range(CK // P):
                        b = c * (CK // P) + t
                        if i == 0 and t == 0:
                            pe.wait_ge(s_rows[c], 16 * (CK // P))
                        ins = pe.transpose(bank[0:CH, 2 * c + i, t * P:(t + 1) * P], tok_rows[:, b, i * CH:(i + 1) * CH], ident[:])
                ins.then_inc(s_rows_t, 1)
            pe.wait_ge(s_sel, 2)

            def norm_pe(r, resid=resid, between=()):
                if r >= 2:
                    if r < 4:
                        pe.wait_ge(s_resid, NC * (r + 1))
                    else:
                        pe.wait_ge(s_norm, NC * 4)
                    for c in range(NC):
                        for i in range(2):
                            ins = pe.matmul(bn(c, CH), ones[0:CH, 0:CH], resid[:, i, ck(c)], start=i == 0, stop=i == 1)
                        ins.then_inc(s_sum, 1)
                else:
                    pe.wait_ge(s_resid, NC * (r + 1))
                if between:
                    pe.wait_ge(s_centered, NC * (r - 1))
                    between[0]()
                pe.wait_ge(s_square, NC * (r + 1))
                for i in range(2):
                    for c in range(NC):
                        ins = pe.matmul(bank[32 * c:32 * c + 32, 4, :], ones[0:CH, 0:32], square[:, i, ck(c)],
                                        start=i == 0, stop=i == 1, tile_position=(0, 32 * c), skip_group_check=True)
                ins.then_inc(s_var, 1)
                if between:
                    between[1]()
                pe.wait_ge(s_rstd, r + 1)
                pe.wait_ge(s_pick, r + 1)
                for c in range(NC):
                    pe.matmul(bn(4 + c, CH), pick[:, c, :], inv, start=True, stop=True).then_inc(s_spread, 1)

            for k in range(NB):
                n, R = BLOCK_N[k], BLOCK_R[k]
                norm_pe(k)
                pe.wait_ge(s_win, 16 * (k + 1))
                G = min(P, 2 * n)
                M = G + (R if k < 2 else 0)

                def project(c, first, done, taken, count):
                    for m in range(NJ):
                        item = NJ * c + m
                        if count + item >= 3:
                            pe.wait_ge(taken, count + item - 2)
                        for i in range(2):
                            ins = pe.matmul(bn(item % 3), w_in_sb[:, i, (first + m) * P:(first + m + 1) * P], xn[:, i, ck(c)],
                                            start=i == 0, stop=i == 1)
                        ins.then_inc(done, 1)

                for c in range(NC):
                    pe.wait_ge(s_norm, NC * k + c + 1)
                    project(c, 0, s_xr_in, s_xr, NJ * NC * k)
                pe.wait_ge(s_xr, NJ * NC * (k + 1))
                for c in range(NC):
                    pe.wait_ge(s_u, NJ * (NC * k + c + 1))
                    if c >= 2:
                        pe.wait_ge(s_split, NC * k + c - 1)
                        if k < 2:
                            pe.wait_ge(s_dt_sb, NC * k + c - 1)
                    for j in range(NJ):
                        ins = pe.matmul(bn(4 + c % 2, M), w_x_sb[k][:, j, 0:M], u[:, j, ck(c)], start=j == 0, stop=j == NJ - 1)
                    ins.then_inc(s_bc_rows, 1)
                    if k == 2:
                        if c:
                            pe.wait_ge(s_dt_sb, NC * k + c)
                        for j in range(NJ):
                            ins = pe.matmul(bn(3, 1), w_x_sb[k][:, j, G:G + 1], u[:, j, ck(c)], start=j == 0, stop=j == NJ - 1)
                        ins.then_inc(s_dt_in, 1)
                    project(c, NJ, s_gate_in, s_gate, NJ * NC * k)
                    pe.wait_ge(s_dt_sb, NC * k + c + 1)
                    for j in range(NJ):
                        item = NJ * c + j
                        if NJ * NC * k + item >= 2:
                            pe.wait_ge(s_dt_x, NJ * NC * k + item - 1)
                        if k < 2:
                            w, low = w_dt_sb[2 * n:2 * n + R, k, j * P:(j + 1) * P], dt_low[2 * n:2 * n + R, ck(c)]
                            pe.matmul(bn(6 + item % 2), w, low, start=True, stop=True, tile_position=(2 * n, 0)).then_inc(s_dt_proj, 1)
                        else:
                            pe.matmul(bn(6 + item % 2), ones[0:1, :], dt_low[0:1, ck(c)], start=True, stop=True).then_inc(s_dt_proj, 1)
                pe.wait_ge(s_split, NC * (k + 1))
                pe.wait_ge(s_gate, NJ * NC * (k + 1))
                pe.wait_ge(s_dt_x, NJ * NC * (k + 1))
                pe.wait_ge(s_stack, STACKED[k + 1])
                pe.wait_ge(s_diag, NJ * (k + 1))
                for c in range(NC):
                    base = STEP0[k] + c * n

                    def skip():
                        for j in range(NJ):
                            pe.matmul(bn(j), diag[:, j, :], u[:, j, ck(c)], start=False, stop=False, skip_group_check=True)

                    def add_up(s, v, first=False, last=False, base=base):
                        pe.wait_ge(s_hc, s + (base + v + 1))
                        for j in range(NJ):
                            ins = pe.matmul(bn(j), ident[:], h_slot[:, v % H_SLOTS, j, :], start=first, stop=last,
                                            skip_group_check=True)
                        ins.then_inc(s_ysum, 1)

                    def scan_pe(s, g, end):
                        for i in range(4):
                            if n < 32:
                                gb, gc, nb, nc_ = 0, 0, s + i, s + (i + n)
                            else:
                                gb = g
                                gc, nb, nc_ = gb + 2, s + (i - 32 * gb), s + (i - 32 * gb)
                            if end != "first" or i or k + c:
                                pe.wait_ge(s_bu, s + (base + i))
                            pe.matmul(bn(B_BANK), sel[:, bass.ds(nb, 1), :].rearrange("p a m -> p (a m)"), stack[:, gb, ck(c)],
                                      start=True, stop=True).then_inc(s_b_bc, 1)
                            if end != "first" or i or k + c:
                                pe.wait_ge(s_c_row, s + (base + i))
                            pe.matmul(bn(C_BANK), sel[:, bass.ds(nc_, 1), :].rearrange("p a m -> p (a m)"), stack[:, gc, ck(c)],
                                      start=True, stop=True).then_inc(s_c_bc, 1)
                            if end == "last" and i == 0:
                                skip()
                            if end != "first" or i >= LAG:
                                if end == "first" and c:
                                    pe.wait_ge(s_y, NC * k + c)
                                add_up(s, i - LAG, first=end == "first")
                            elif c:
                                add_up(0, n - LAG + i, last=i == LAG - 1, base=base - n)
                    steps(pe, n, scan_pe)
                def project_out(c):
                    for i in range(2):
                        for j in range(NJ):
                            ins = pe.matmul(bank[0:CH, OUT_BANKS[c][i], :], w_out_sb[:, k, j, i * CH:(i + 1) * CH], gate[:, j, ck(c)],
                                            start=j == 0, stop=j == NJ - 1)
                    ins.then_inc(s_outproj, 1)

                add_up(0, n - LAG)
                pe.wait_ge(s_bu, base + n)
                pe.wait_ge(s_c_row, base + n)
                project_out(0)
                add_up(0, n - 2)
                add_up(0, n - 1, last=True)
                for j in range(NJ):
                    pe.wait_ge(s_scan[j], base + n)
                project_out(1)
                pe.wait_ge(s_y, NC * (k + 1))
                project_out(2)
                project_out(3)
            norm_pe(3)
            pe.wait_ge(s_norm, NC * 4)
            pe.wait_ge(f_ffn_c, 16 * 8)

            def logits(blocks):
                for b in blocks:
                    for i in range(2):
                        ins = pe.matmul(bank[:, 0, b * E:(b + 1) * E], xf[:, i, b * P:(b + 1) * P], w_router_sb[:, i, :],
                                        start=i == 0, stop=i == 1)
                if b == KT - 1:
                    ins.then_inc(f_logit, 1)
            norm_pe(4, resid=xf, between=(lambda: logits(range(0, KT // 2)), lambda: logits(range(KT // 2, KT))))
            pe.wait_ge(f_probs, 2)
            for b in range(KT):
                ins = pe.transpose(bank[:, 4 + b // 4, (b % 4) * P:(b % 4 + 1) * P],
                                   prob_wide[:, b].rearrange("p e m -> p (e m)"), ident[:])
                if b % 4 == 3:
                    ins.then_inc(f_prob_t, 1)
            def turn_weights(items):
                for b in items:
                    if b >= 7:
                        pe.wait_ge(f_w_turned, b - 6)
                    if b < 14:
                        for i in range(2):
                            ins = pe.transpose(bank[0:CH, 1 + b % 7, i * CH:(i + 1) * CH], w1_raw[:, b, i * CH:(i + 1) * CH], ident[0:CH, 0:CH])
                    else:
                        f, i = (b - 14) // 2, b % 2
                        w = w2_raw[:, i, f * P:(f + 1) * P] if f < HID // P else w2_pad[:, i, f - HID // P].rearrange("p j d -> p (j d)")
                        ins = pe.transpose(bank[:, 1 + b % 7, 0:CH], w, ident[0:CH, 0:CH])
                    ins.then_inc(f_w_turn, 1)
            pe.wait_ge(f_prob_bc, NC)
            pe.wait_ge(f_w_raw, 32)
            pe.wait_ge(f_w2_half, 3)
            for r in range(SEARCH_ROUNDS):
                pe.wait_ge(f_flag, r + 1)
                pe.matmul(bank[:, 0, r:r + 1], group_ones, search[:, 1:2], start=True, stop=True).then_inc(f_votes, 1)
                turn_weights(range(6 * r, min(32, 6 * r + 6)))
            pe.wait_ge(f_w_turned, 32)
            pe.wait_ge(f_chosen, 1)
            for c in range(NC):
                for i in range(2):
                    ins = pe.matmul(bn(2 * c + i, CH + i), width_mask[:, i * CH:(i + 1) * CH + i], chosen[:, ck(c)],
                                    start=True, stop=True)
                ins.then_inc(f_share, 1)
            pe.wait_ge(f_yw, NC)
            for t, tile in enumerate(TILES):
                for c in range(NC):
                    item = t * NC + c
                    if item >= 8:
                        pe.wait_ge(f_qk_left, item - 7)
                    for i in range(2):
                        ins = pe.matmul(bn(item % 8, CH), w1t[0:CH + i, i, HID + tile * CH:HID + (tile + 1) * CH],
                                        yw[0:CH + i, i, ck(c)], start=i == 0, stop=i == 1)
                    ins.then_inc(f_qk, 1)
            pe.wait_ge(f_qk_left, 4 * NC)
            def value_rows(b):
                if b >= V_RING:
                    pe.wait_ge(f_v_sb, b + 1 - V_RING)
                for i in range(2):
                    ins = pe.matmul(bank[:, b % V_RING, 0:C], yw[0:CH + i, i, b * P:(b + 1) * P], w1t[0:CH + i, i, HID + 2 * C:F1],
                                    start=i == 0, stop=i == 1)
                ins.then_inc(f_v, 1)
            for b in range(KT // 2):
                value_rows(b)

            def max_pe(step, g, c, ms):
                for m in ms:
                    head, qt, r = m // 16, m // 4 % 4, m % 4
                    if m < MAX_RING:
                        pe.wait_ge(f_mred, step * 64)
                        if m == 2:
                            pe.wait_ge(f_mxrow, step)
                    else:
                        pe.wait_ge(f_mred, step * 64 + (m + 1 - MAX_RING))
                    pe.matmul(bank[:, 5 + m % MAX_RING, :], q_stack[0:KR, q_cols(c, head, P, qt * P)],
                              k_stack[g % 2][0:KR, head, r * CK:(r + 1) * CK], start=True, stop=True).then_inc(f_mscore, 1)

            def max_end(step):
                pe.wait_ge(f_mx, step + 1)
                pe.transpose(bank[0:HG * 4, 7, 0:P], max_q[:], ident[:]).then_inc(f_mxt, 1)

            def values(step, g, kt):
                pe.wait_ge(f_p, step * (2 * KT) + (2 * (kt + 1) + P0))
                if kt == 0:
                    pe.wait_ge(f_attn, step + O0)
                for h in range(HG):
                    ins = pe.matmul(bank[32 * h:32 * h + 32, 4, :], v_sb[:, kt, HG * g + h, :], p_slot[:, 2 * (kt % 2) + h // 2, h % 2, :],
                                    start=kt == 0, stop=kt == KT - 1, tile_position=(0, 32 * h), skip_group_check=True)
                ins.then_inc(f_pv, 1)

            def attn_pe(step, g, c, ahead):
                for kt in range(KT):
                    ms = list(range(4 * kt + 4, 4 * kt + 8)) if kt < KT - 1 else []
                    if kt == 0:
                        if ahead:
                            max_pe(step + 1, *ahead, range(4))
                        pe.wait_ge(f_qrow, (step + 1) * 48)
                    for half in range(2):
                        pe.wait_ge(f_p, step * (2 * KT) + (2 * kt + half - 1 + P0))
                        for h in range(2 * half, 2 * half + 2):
                            ins = pe.matmul(bank[:, h, :], k_stack[g % 2][0:KR + 3, h, kt * P:(kt + 1) * P],
                                            q_stack[0:KR + 3, q_cols(c, h, CK)], start=True, stop=True)
                        ins.then_inc(f_st, 1)
                        if ahead:
                            max_pe(step + 1, *ahead, ms[half:half + 1])
                    if ahead and kt == KT - 1:
                        max_end(step + 1)
                    if kt:
                        values(step, g, kt - 1)
                    if ahead:
                        max_pe(step + 1, *ahead, ms[2:])
                values(step, g, KT - 1)
            pe.wait_ge(f_k_pad, 2)
            pe.wait_ge(f_kload[0], 16)
            pe.wait_ge(f_qfirst[0], 16)
            for b in range(KT // 2):
                max_pe(0, 0, 0, range(8 * b, 8 * b + 8))
                value_rows(KT // 2 + b)
            pe.wait_ge(f_v_sb, KT)
            max_end(0)
            for g in range(NG):
                for c in range(1, NC):
                    if g:
                        pe.wait_ge(f_qload[c], 16 * g)
                    else:
                        pe.wait_ge(f_qfirst[c], 16)
                with pe.Fori(0, NC - 1) as c:
                    attn_pe(c + g * NC, g, c, (g, c + 1))
                if g < NG - 1:
                    pe.wait_ge(f_kload[g + 1], 16)
                    pe.wait_ge(f_qload[0], 16 * (g + 1))
                    attn_pe(g * NC + NC - 1, g, NC - 1, (g + 1, 0))
                else:
                    attn_pe(g * NC + NC - 1, g, NC - 1, None)
            def fc1(items):
                for item in items:
                    f, c = item // NC, item % NC
                    if item >= 4:
                        pe.wait_ge(f_mlp, item - 3)
                    for i in range(2):
                        ins = pe.matmul(bn(item % 4), w1t[0:CH + i, i, f * P:(f + 1) * P], yw[0:CH + i, i, ck(c)],
                                        start=i == 0, stop=i == 1)
                    ins.then_inc(f_fc1, 1)

            def pick_sums(g):
                pe.wait_ge(f_attn, NG * NC + O0)
                if g:
                    pe.wait_ge(f_inv, g)
                for c in range(NC):
                    ins = pe.matmul(bank[32 * c:32 * c + 32, 4, :], sum_pick, xa[:, g, ck(c)], start=True, stop=True,
                                    tile_position=(0, 32 * c), skip_group_check=True)
                ins.then_inc(f_sums, 1)

            def spread_sums(g):
                pe.wait_ge(f_inv, g + 1)
                for c in range(NC):
                    item = g * NC + c
                    if item >= 3:
                        pe.wait_ge(f_xa, item - 2)
                    pe.matmul(bn(5 + item % 3), sum_spread[:, c, :], inv_sb[:, g, :], start=True, stop=True).then_inc(f_spread, 1)

            FC1_ITEMS = HID // P * NC
            fc1(range(0, 4))
            for g in range(NG):
                pick_sums(g)
                fc1(range(4 + 5 * g, 9 + 5 * g))
                spread_sums(g)
            fc1(range(4 + 5 * NG, FC1_ITEMS))
            pe.wait_ge(f_xa, NG * NC)
            pe.wait_ge(f_mlp, FC1_ITEMS)

            def turn_rows(c):
                pe.wait_ge(f_zz, NC + 2 * (c + 1))
                for b in range(c * (CK // P), (c + 1) * (CK // P)):
                    if b >= 2:
                        pe.wait_ge(s_fin, b - 1)
                    for i in range(2):
                        ins = pe.transpose(bank[:, 6 + b % 2, i * CH:(i + 1) * CH], resid[:, i, b * P:(b + 1) * P], ident[0:CH, 0:CH])
                    ins.then_inc(s_fin_t, 1)
            for c in range(NC):
                for i in range(2):
                    item = 2 * c + i
                    if item >= 4:
                        pe.wait_ge(f_o, item - 3)
                    for f in range(9):
                        src = mlp[:, f, ck(c)] if f < 6 else xa[:, f - 6, ck(c)]
                        ins = pe.matmul(bn(item % 4, CH), w2t[:, f, i * CH:(i + 1) * CH], src, start=f == 0, stop=f == 8)
                    ins.then_inc(f_fc2, 1)
                    if item >= 2:
                        pe.wait_ge(f_zz, NC + item - 1)
                    pe.matmul(bn(4 + item % 2, CH), width_mask[:, i * CH:(i + 1) * CH], selgate[:, ck(c)],
                              start=True, stop=True).then_inc(f_g, 1)
                    if c and i == 0:
                        turn_rows(c - 1)
            turn_rows(NC - 1)


_INS = ['x', 'L0_tok_emb', 'L0_tok_norm_w', 'L0_tok_in_proj_w', 'L0_tok_conv_w', 'L0_tok_conv_b', 'L0_tok_x_proj_w',
        'L0_tok_dt_proj_w', 'L0_tok_dt_proj_b', 'L0_tok_A_log', 'L0_tok_D', 'L0_tok_out_proj_w', 'L0_attn_in_w',
        'L0_attn_conv_w', 'L0_attn_conv_b', 'L0_attn_xproj_w', 'L0_attn_A_log', 'L0_attn_dt_bias', 'L0_attn_D',
        'L0_attn_out_w', 'L0_ffn_w_router', 'L0_ffn_gamma1', 'L0_ffn_beta1', 'L0_ffn_w1', 'L0_ffn_b1', 'L0_ffn_w2',
        'L0_ffn_b2']


def shape_constants():
    p = np.arange(P)
    return {
        "ident": np.eye(P, dtype=np.float32),
        "fold": (p[:, None] % 32 == np.arange(32)[None, :]).astype(np.float32),
        "width_mask": ((p[:, None] % 32 == 0) & (np.append(np.arange(C), 0)[None, :] < np.array(WIDTH)[p // 32][:, None])).astype(np.float32),
        "group_ones": (p[:, None] // 32 == p[None, :] // 32).astype(np.float32),
        "sum_pick": (p[:, None] == (np.arange(32) % HG * 32 + HD)[None, :]).astype(np.float32),
        "sum_spread": (p[:, None, None] == np.arange(NC)[None, :, None] * 32 + (p // 32)[None, None, :]).astype(np.float32),
        "search_off": ((p[:, None] % 32) << (SEARCH_BITS * np.arange(SEARCH_ROUNDS - 1, -1, -1))[None, :]).astype(np.int32),
    }


def kernel(**inputs):
    import concourse.bacc as bacc
    from concourse.bass_utils import run_bass_kernel_spmd

    nc = bacc.Bacc("TRN2", target_bir_lowering=False, num_devices=1)
    arrays, dram = {}, {}

    def give(name, a):
        a = np.ascontiguousarray(a)
        arrays[f"in_{name}"] = a
        return nc.dram_tensor(f"in_{name}", a.shape, mybir.dt.from_np(a.dtype), kind="ExternalInput").ap()

    for name in _INS:
        dram[name] = give(name, inputs[name])
    consts = {name: give("const_" + name, a) for name, a in shape_constants().items()}
    out = nc.dram_tensor("out_0", (1, L, C), F32, kind="ExternalOutput").ap()

    def per_layer(tok, att):
        return [dram["L0_tok_" + tok][0], dram["L0_tok_" + tok][1], dram["L0_attn_" + att]]

    build(nc, dram["x"], dram["L0_tok_emb"], dram["L0_tok_norm_w"], per_layer("in_proj_w", "in_w"),
          per_layer("conv_w", "conv_w"), per_layer("conv_b", "conv_b"), per_layer("x_proj_w", "xproj_w"),
          dram["L0_tok_dt_proj_w"], per_layer("dt_proj_b", "dt_bias"), per_layer("A_log", "A_log"), per_layer("D", "D"),
          per_layer("out_proj_w", "out_w"),
          {"w_router": dram["L0_ffn_w_router"], "gamma": dram["L0_ffn_gamma1"], "beta": dram["L0_ffn_beta1"],
           "w1": dram["L0_ffn_w1"], "b1": dram["L0_ffn_b1"], "w2": dram["L0_ffn_w2"], "b2": dram["L0_ffn_b2"]}, consts, out)
    r = run_bass_kernel_spmd(nc, [arrays], core_ids=[0])
    return r.results[0]["out_0"]
```
